# Optimizing a Trainium2 kernel written in Bass

```python
import numpy as np
import jax
import jax.numpy as jnp

def _softmax(x, axis=-1):
    return jax.nn.softmax(x, axis=axis)

def _gelu(x):
    return jax.nn.gelu(x, approximate=True)

def _silu(x):
    return jax.nn.silu(x)

def _sigmoid(x):
    return jax.nn.sigmoid(x)

def _layernorm(x, axis=-1, eps=1e-05):
    m = jnp.mean(x, axis=axis, keepdims=True)
    v = jnp.var(x, axis=axis, keepdims=True)
    return (x - m) / jnp.sqrt(v + eps)

def _scatter_add(tgt, idx, src, axis=0):
    return tgt.at[idx].add(src)

def _segment_sum(src, seg, n):
    return jax.ops.segment_sum(src, seg, n)
kernel_name = 'mk_adaln_ffn_d2_seqx_r4_7b47c7'

def setup_inputs(seed: int=0):
    np.random.seed(seed)
    _w = jnp.asarray

    def _rec_inputs():
        import jax
        import jax.numpy as jnp
        _rk = jax.random.key(seed)
        x = -0.0002928 + 1 * jax.random.normal(jax.random.fold_in(_rk, 1), (16, 256, 256), jnp.float32)
        _lenS = 256 - jax.random.randint(jax.random.fold_in(_rk, 7), (16,), 0, max(1, 256 // 4) + 1, jnp.int32)
        _lenS2 = 256 - jax.random.randint(jax.random.fold_in(_rk, 8), (16,), 0, max(1, 256 // 4) + 1, jnp.int32)
        fside_16xSxS_0 = -5.72187e-05 + 0.999849 * jax.random.normal(jax.random.fold_in(_rk, 11), (16, 256, 256), jnp.float32)
        cond_64 = -0.0265395 + 0.99382 * jax.random.normal(jax.random.fold_in(_rk, 13), (16, 64), jnp.float32)
        _validS = jnp.arange(256)[None, :] < _lenS[:, None]
        _validS2 = jnp.arange(256)[None, :] < _lenS2[:, None]
        _causal = jnp.tril(jnp.ones((256, 256), dtype=bool))
        mask_BxS_bk0 = jnp.logical_not(jnp.broadcast_to(_validS[:, :], (16, 256)))
        return (x, fside_16xSxS_0, cond_64, mask_BxS_bk0)
    x, fside_16xSxS_0, cond_64, mask_BxS_bk0 = _rec_inputs()

    def _L0_cond_setup():
        import jax, jax.numpy as jnp
        import numpy as np
        B, N, DIM, H, DH = (2, 512, 256, 16, 64)
        INNER = H * DH
        EPS = 1e-05

        def layernorm(x, g):
            mean = jnp.mean(x, axis=-1, keepdims=True)
            var = jnp.var(x, axis=-1, keepdims=True)
            return (x - mean) * jax.lax.rsqrt(var + EPS) * g
        key = jax.random.key(seed)
        ks = jax.random.split(key, 10)
        x = jax.random.normal(ks[0], (B, N, DIM), dtype=jnp.float32)
        attn_bias = jax.random.normal(ks[1], (H, N, N), dtype=jnp.float32)
        mask = jax.random.randint(ks[2], (B, N), 0, 2).astype(bool)
        g_in = jnp.ones((DIM,), dtype=jnp.float32)
        null_attn_bias = jax.random.normal(ks[3], (H,), dtype=jnp.float32)
        null_kv = jax.random.normal(ks[4], (2, DH), dtype=jnp.float32)
        Wq = jax.random.normal(ks[5], (DIM, INNER), dtype=jnp.float32) * 0.02
        Wkv = jax.random.normal(ks[6], (DIM, 2 * DH), dtype=jnp.float32) * 0.02
        Wo = jax.random.normal(ks[7], (INNER, DIM), dtype=jnp.float32) * 0.02
        g_out = jnp.ones((DIM,), dtype=jnp.float32)
        return {'x': x, 'attn_bias': attn_bias, 'mask': mask, 'g_in': g_in, 'null_attn_bias': null_attn_bias, 'null_kv': null_kv, 'Wq': Wq, 'Wkv': Wkv, 'Wo': Wo, 'g_out': g_out}
    _L0_cond_all = _L0_cond_setup()
    _L0_cond_in = {k: v for k, v in _L0_cond_all.items() if k in ('g_in', 'null_attn_bias', 'Wq', 'Wkv', 'Wo', 'g_out')}
    del _L0_cond_all

    def _L0_ffn_setup():
        import math
        import jax, jax.numpy as jnp
        import numpy as np
        D_MODEL = 256
        D_FF = 1024
        N_EXPERTS = 8
        CAPACITY_FACTOR = 1.25
        L, B = (128, 8)

        def _route(tokens, router_w):
            T = tokens.shape[0]
            E = router_w.shape[0]
            capacity = int(math.ceil(T / E * CAPACITY_FACTOR))
            logits = tokens @ router_w.T
            probs = jax.nn.softmax(logits, axis=-1)
            top1_idx = jnp.argmax(probs, axis=-1)
            top1_prob = jnp.max(probs, axis=-1)
            order = jnp.lexsort((-top1_prob, top1_idx))
            sorted_e = top1_idx[order]
            counts = jnp.bincount(top1_idx, length=E)
            start = jnp.cumsum(counts) - counts
            pos_in_group = jnp.arange(T) - start[sorted_e]
            keep_sorted = pos_in_group < capacity
            keep = jnp.zeros((T,), bool).at[order].set(keep_sorted)
            return jnp.where(keep, top1_idx, 0).astype(jnp.int32)
        key = jax.random.key(seed)
        ks = jax.random.split(key, 6)
        s_in = 1.0 / math.sqrt(D_MODEL)
        s_ff = 1.0 / math.sqrt(D_FF)
        return {'x': jax.random.normal(ks[0], (L, B, D_MODEL), dtype=jnp.float32), 'router_w': jax.random.uniform(ks[1], (N_EXPERTS, D_MODEL), minval=-s_in, maxval=s_in), 'W1': jax.random.uniform(ks[2], (N_EXPERTS, D_MODEL, D_FF), minval=-s_in, maxval=s_in), 'b1': jax.random.uniform(ks[3], (N_EXPERTS, D_FF), minval=-s_in, maxval=s_in), 'W2': jax.random.uniform(ks[4], (N_EXPERTS, D_FF, D_MODEL), minval=-s_ff, maxval=s_ff), 'b2': jax.random.uniform(ks[5], (N_EXPERTS, D_MODEL), minval=-s_ff, maxval=s_ff)}
    _L0_ffn_all = _L0_ffn_setup()
    _L0_ffn_in = {k: v for k, v in _L0_ffn_all.items() if k in ('router_w', 'W1', 'b1', 'W2', 'b2')}
    del _L0_ffn_all

    def _L1_cond_setup():
        import jax, jax.numpy as jnp
        import numpy as np
        B, S, H = (4, 512, 256)
        E = 8
        M = 128
        K = 2
        N_SHARED = 2
        SM = M * N_SHARED
        G = 64
        GE_TEMP = 1.0
        ALPHA = 0.001
        SEQ_AUX = True
        NORM_TOPK = True
        COS_TEMP = 0.78
        CONS_ALPHA = 0.01
        LEAKY_SLOPE = 0.01
        EPS_COS = 1e-08

        def _leaky(x):
            return jnp.where(x >= 0, x, LEAKY_SLOPE * x)

        def _moe_forward(hidden_states, g, wt, wg, w_gate, w_up, w_down, sw_gate, sw_up, sw_down):
            b, s, h = hidden_states.shape
            x = hidden_states.reshape(-1, h)
            T = x.shape[0]
            logits_h = x @ wt.T
            logits_g = g @ wg.T
            logits_g = jnp.repeat(logits_g, s, axis=0)
            logits = (logits_h + logits_g / GE_TEMP) / (1.0 + 1.0 / GE_TEMP)
            scores = jax.nn.softmax(logits, axis=-1)
            topk_w, topk_idx = jax.lax.top_k(scores, K)
            if K > 1 and NORM_TOPK:
                topk_w = topk_w / (topk_w.sum(-1, keepdims=True) + 1e-20)
            onehot = jax.nn.one_hot(topk_idx.reshape(b, s * K), E, dtype=jnp.float32)
            ce = onehot.sum(1) / (s * K / E)
            aux_loss = (ce * scores.reshape(b, s, E).mean(1)).sum(1).mean() * ALPHA
            gp = _leaky(jnp.einsum('th,ehm->etm', x, w_gate))
            up = jnp.einsum('th,ehm->etm', x, w_up)
            y_all = jnp.einsum('etm,emh->eth', gp * up, w_down)
            y_sel = y_all[topk_idx, jnp.arange(T)[:, None], :]
            y = (y_sel * topk_w[..., None]).sum(1).reshape(b, s, h)
            p = _leaky(hidden_states @ sw_gate) * (hidden_states @ sw_up) @ sw_down
            y = y + p
            num = jnp.sum(y * p, -1)
            den = jnp.maximum(jnp.linalg.norm(y, axis=-1), EPS_COS) * jnp.maximum(jnp.linalg.norm(p, axis=-1), EPS_COS)
            closs = CONS_ALPHA * jnp.mean(num / den / (1.0 + COS_TEMP))
            return (y, aux_loss + closs)
        key = jax.random.key(seed)
        ks = jax.random.split(key, 12)
        sh = 1.0 / np.sqrt(H)
        sm = 1.0 / np.sqrt(M)
        ssm = 1.0 / np.sqrt(SM)
        sg = 1.0 / np.sqrt(G)
        return {'hidden_states': jax.random.normal(ks[0], (B, S, H), jnp.float32), 'g': jax.random.normal(ks[1], (B, G), jnp.float32), 'wt': jax.random.uniform(ks[2], (E, H), jnp.float32, -sh, sh), 'wg': jax.random.uniform(ks[3], (E, G), jnp.float32, -sg, sg), 'w_gate': jax.random.uniform(ks[4], (E, H, M), jnp.float32, -sh, sh), 'w_up': jax.random.uniform(ks[5], (E, H, M), jnp.float32, -sh, sh), 'w_down': jax.random.uniform(ks[6], (E, M, H), jnp.float32, -sm, sm), 'sw_gate': jax.random.uniform(ks[7], (H, SM), jnp.float32, -sh, sh), 'sw_up': jax.random.uniform(ks[8], (H, SM), jnp.float32, -sh, sh), 'sw_down': jax.random.uniform(ks[9], (SM, H), jnp.float32, -ssm, ssm)}
    _L1_cond_all = _L1_cond_setup()
    _L1_cond_in = {k: v for k, v in _L1_cond_all.items() if k in ('wt', 'wg', 'w_gate', 'w_up', 'w_down', 'sw_gate', 'sw_up', 'sw_down')}
    del _L1_cond_all

    def _L1_ffn_setup():
        import jax, jax.numpy as jnp
        import numpy as np
        NEG_INF = -1e+30
        K = 2
        key = jax.random.key(seed)
        ks = jax.random.split(key, 5)
        B, S, D, O, E = (8, 512, 256, 256, 8)
        scale = 1.0 / np.sqrt(D)
        return {'x': jax.random.normal(ks[0], (B, S, D), dtype=jnp.float32), 'gate_w': jax.random.normal(ks[1], (E, D), dtype=jnp.float32) * scale, 'gate_b': jnp.zeros((E,), dtype=jnp.float32), 'expert_w': jax.random.normal(ks[2], (E, O, D), dtype=jnp.float32) * scale, 'expert_b': jnp.zeros((E, O), dtype=jnp.float32)}
    _L1_ffn_all = _L1_ffn_setup()
    _L1_ffn_in = {k: v for k, v in _L1_ffn_all.items() if k in ('gate_w', 'gate_b', 'expert_w', 'expert_b')}
    del _L1_ffn_all
    return {'x': x, 'fside_16xSxS_0': fside_16xSxS_0, 'cond_64': cond_64, 'mask_BxS_bk0': mask_BxS_bk0, 'L0_cond_g_in': _L0_cond_in['g_in'], 'L0_cond_null_attn_bias': _L0_cond_in['null_attn_bias'], 'L0_cond_Wq': _L0_cond_in['Wq'], 'L0_cond_Wkv': _L0_cond_in['Wkv'], 'L0_cond_Wo': _L0_cond_in['Wo'], 'L0_cond_g_out': _L0_cond_in['g_out'], 'L0_ffn_router_w': _L0_ffn_in['router_w'], 'L0_ffn_W1': _L0_ffn_in['W1'], 'L0_ffn_b1': _L0_ffn_in['b1'], 'L0_ffn_W2': _L0_ffn_in['W2'], 'L0_ffn_b2': _L0_ffn_in['b2'], 'L1_cond_wt': _L1_cond_in['wt'], 'L1_cond_wg': _L1_cond_in['wg'], 'L1_cond_w_gate': _L1_cond_in['w_gate'], 'L1_cond_w_up': _L1_cond_in['w_up'], 'L1_cond_w_down': _L1_cond_in['w_down'], 'L1_cond_sw_gate': _L1_cond_in['sw_gate'], 'L1_cond_sw_up': _L1_cond_in['sw_up'], 'L1_cond_sw_down': _L1_cond_in['sw_down'], 'L1_ffn_gate_w': _L1_ffn_in['gate_w'], 'L1_ffn_gate_b': _L1_ffn_in['gate_b'], 'L1_ffn_expert_w': _L1_ffn_in['expert_w'], 'L1_ffn_expert_b': _L1_ffn_in['expert_b']}

def reference(x, fside_16xSxS_0, cond_64, mask_BxS_bk0, L0_cond_g_in, L0_cond_null_attn_bias, L0_cond_Wq, L0_cond_Wkv, L0_cond_Wo, L0_cond_g_out, L0_ffn_router_w, L0_ffn_W1, L0_ffn_b1, L0_ffn_W2, L0_ffn_b2, L1_cond_wt, L1_cond_wg, L1_cond_w_gate, L1_cond_w_up, L1_cond_w_down, L1_cond_sw_gate, L1_cond_sw_up, L1_cond_sw_down, L1_ffn_gate_w, L1_ffn_gate_b, L1_ffn_expert_w, L1_ffn_expert_b):
    import jax
    import jax.numpy as jnp

    def _L0_cond_ref(x, attn_bias, mask, g_in, null_attn_bias, null_kv, Wq, Wkv, Wo, g_out):
        import jax, jax.numpy as jnp
        import numpy as np
        B, N, DIM, H, DH = (2, 512, 256, 16, 64)
        INNER = H * DH
        EPS = 1e-05

        def layernorm(x, g):
            mean = jnp.mean(x, axis=-1, keepdims=True)
            var = jnp.var(x, axis=-1, keepdims=True)
            return (x - mean) * jax.lax.rsqrt(var + EPS) * g
        b, n, _ = x.shape
        scale = DH ** (-0.5)
        xn = layernorm(x, g_in)
        q = (xn @ Wq).reshape(b, n, H, DH).transpose(0, 2, 1, 3) * scale
        kv = xn @ Wkv
        k, v = (kv[..., :DH], kv[..., DH:])
        nk = jnp.broadcast_to(null_kv[0], (b, 1, DH))
        nv = jnp.broadcast_to(null_kv[1], (b, 1, DH))
        k = jnp.concatenate([nk, k], axis=1)
        v = jnp.concatenate([nv, v], axis=1)
        sim = jnp.einsum('bhid,bjd->bhij', q, k)
        null_col = jnp.broadcast_to(null_attn_bias[:, None, None], (H, n, 1))
        bias = jnp.concatenate([null_col, attn_bias], axis=-1)
        sim = sim + bias
        neg = -jnp.finfo(sim.dtype).max
        j = n + 1
        causal_mask = jnp.triu(jnp.ones((n, j), dtype=bool), k=j - n + 1)
        sim = jnp.where(causal_mask, neg, sim)
        mask_p = jnp.pad(mask, ((0, 0), (1, 0)), constant_values=True)
        sim = jnp.where(mask_p[:, None, None, :], sim, neg)
        attn = jax.nn.softmax(sim, axis=-1)
        out = jnp.einsum('bhij,bjd->bhid', attn, v)
        out = out.transpose(0, 2, 1, 3).reshape(b, n, INNER)
        out = out @ Wo
        return layernorm(out, g_out)

    def _L0_ffn_ref(x, router_w, W1, b1, W2, b2):
        import math
        import jax, jax.numpy as jnp
        import numpy as np
        D_MODEL = 256
        D_FF = 1024
        N_EXPERTS = 8
        CAPACITY_FACTOR = 1.25
        L, B = (128, 8)

        def _route(tokens, router_w):
            T = tokens.shape[0]
            E = router_w.shape[0]
            capacity = int(math.ceil(T / E * CAPACITY_FACTOR))
            logits = tokens @ router_w.T
            probs = jax.nn.softmax(logits, axis=-1)
            top1_idx = jnp.argmax(probs, axis=-1)
            top1_prob = jnp.max(probs, axis=-1)
            order = jnp.lexsort((-top1_prob, top1_idx))
            sorted_e = top1_idx[order]
            counts = jnp.bincount(top1_idx, length=E)
            start = jnp.cumsum(counts) - counts
            pos_in_group = jnp.arange(T) - start[sorted_e]
            keep_sorted = pos_in_group < capacity
            keep = jnp.zeros((T,), bool).at[order].set(keep_sorted)
            return jnp.where(keep, top1_idx, 0).astype(jnp.int32)
        Lx, Bx, D = x.shape
        T = Lx * Bx
        E = router_w.shape[0]
        tokens = x.reshape(T, D)
        final_e = _route(tokens, router_w)
        out = jnp.zeros_like(tokens)
        for e in range(E):
            h = jax.nn.relu(tokens @ W1[e] + b1[e])
            y = h @ W2[e] + b2[e]
            out = out + jnp.where((final_e == e)[:, None], y, 0.0)
        return out.reshape(Lx, Bx, D)

    def _L1_cond_ref(hidden_states, g, wt, wg, w_gate, w_up, w_down, sw_gate, sw_up, sw_down):
        import jax, jax.numpy as jnp
        import numpy as np
        B, S, H = (4, 512, 256)
        E = 8
        M = 128
        K = 2
        N_SHARED = 2
        SM = M * N_SHARED
        G = 64
        GE_TEMP = 1.0
        ALPHA = 0.001
        SEQ_AUX = True
        NORM_TOPK = True
        COS_TEMP = 0.78
        CONS_ALPHA = 0.01
        LEAKY_SLOPE = 0.01
        EPS_COS = 1e-08

        def _leaky(x):
            return jnp.where(x >= 0, x, LEAKY_SLOPE * x)

        def _moe_forward(hidden_states, g, wt, wg, w_gate, w_up, w_down, sw_gate, sw_up, sw_down):
            b, s, h = hidden_states.shape
            x = hidden_states.reshape(-1, h)
            T = x.shape[0]
            logits_h = x @ wt.T
            logits_g = g @ wg.T
            logits_g = jnp.repeat(logits_g, s, axis=0)
            logits = (logits_h + logits_g / GE_TEMP) / (1.0 + 1.0 / GE_TEMP)
            scores = jax.nn.softmax(logits, axis=-1)
            topk_w, topk_idx = jax.lax.top_k(scores, K)
            if K > 1 and NORM_TOPK:
                topk_w = topk_w / (topk_w.sum(-1, keepdims=True) + 1e-20)
            onehot = jax.nn.one_hot(topk_idx.reshape(b, s * K), E, dtype=jnp.float32)
            ce = onehot.sum(1) / (s * K / E)
            aux_loss = (ce * scores.reshape(b, s, E).mean(1)).sum(1).mean() * ALPHA
            gp = _leaky(jnp.einsum('th,ehm->etm', x, w_gate))
            up = jnp.einsum('th,ehm->etm', x, w_up)
            y_all = jnp.einsum('etm,emh->eth', gp * up, w_down)
            y_sel = y_all[topk_idx, jnp.arange(T)[:, None], :]
            y = (y_sel * topk_w[..., None]).sum(1).reshape(b, s, h)
            p = _leaky(hidden_states @ sw_gate) * (hidden_states @ sw_up) @ sw_down
            y = y + p
            num = jnp.sum(y * p, -1)
            den = jnp.maximum(jnp.linalg.norm(y, axis=-1), EPS_COS) * jnp.maximum(jnp.linalg.norm(p, axis=-1), EPS_COS)
            closs = CONS_ALPHA * jnp.mean(num / den / (1.0 + COS_TEMP))
            return (y, aux_loss + closs)
        y, _ = _moe_forward(hidden_states, g, wt, wg, w_gate, w_up, w_down, sw_gate, sw_up, sw_down)
        return y

    def _L1_ffn_ref(x, gate_w, gate_b, expert_w, expert_b):
        import jax, jax.numpy as jnp
        import numpy as np
        NEG_INF = -1e+30
        K = 2
        pooled = x.mean(axis=1)
        logits = pooled @ gate_w.T + gate_b
        topk_vals, _ = jax.lax.top_k(logits, K)
        min_topk = topk_vals[:, -1:]
        masked = jnp.where(logits < min_topk, -jnp.inf, logits)
        gates = jax.nn.softmax(masked, axis=-1)
        expert_out = jax.nn.gelu(jnp.einsum('bsd,eod->beso', x, expert_w) + expert_b[None, :, None, :], approximate=False)
        return jnp.einsum('be,beso->bso', gates, expert_out)
    x = x + _L0_ffn_ref(_L0_cond_ref(x, fside_16xSxS_0, mask_BxS_bk0, L0_cond_g_in, L0_cond_null_attn_bias, cond_64, L0_cond_Wq, L0_cond_Wkv, L0_cond_Wo, L0_cond_g_out), L0_ffn_router_w, L0_ffn_W1, L0_ffn_b1, L0_ffn_W2, L0_ffn_b2)
    x = x + _L1_ffn_ref(_L1_cond_ref(x, cond_64, L1_cond_wt, L1_cond_wg, L1_cond_w_gate, L1_cond_w_up, L1_cond_w_down, L1_cond_sw_gate, L1_cond_sw_up, L1_cond_sw_down), L1_ffn_gate_w, L1_ffn_gate_b, L1_ffn_expert_w, L1_ffn_expert_b)
    return x

_drawn_inputs = setup_inputs


def setup_inputs(seed=0):
    import zlib

    import numpy as np

    out = dict(_drawn_inputs(seed))
    spreads = {'L0_cond_g_in': (1.0, 0.2),
     'L0_cond_g_out': (1.0, 0.2),
     'L1_ffn_gate_b': (0.0, 0.1),
     'L1_ffn_expert_b': (0.0, 0.1)}
    factors = {'L0_ffn_b1': 3.911, 'L0_ffn_b2': 3.073}
    for name, (base, spread) in spreads.items():
        noise = np.random.default_rng([zlib.crc32(name.encode()), seed]).standard_normal(out[name].shape)
        drawn = base * np.exp(spread * noise) if base else spread * noise
        out[name] = jnp.asarray(drawn.astype(out[name].dtype))
    for name, factor in factors.items():
        out[name] = (out[name] * factor).astype(out[name].dtype)
    return out
```

```python
import numpy as np


def bass_adaln_ffn_kernel(
    nc, x, side, cond_t, null_kv, mask, g_in, null_bias, wq, wkv, wo, router_t,
    w1, b1, w2, b2, wt_t, wg_t, moe_gate, moe_up, moe_down, sw_gate, sw_up, sw_down,
    gate_w_t, gate_b, expert_w_t, expert_b_t, g_out, out,
):
    from contextlib import ExitStack
    import concourse.bass as bass
    from concourse import mybir

    F32 = mybir.dt.float32
    BF16 = mybir.dt.bfloat16
    I32 = mybir.dt.int32
    U8 = mybir.dt.uint8
    ALU = mybir.AluOpType
    ACT = mybir.ActivationFunctionType
    AXX = mybir.AxisListType.X

    P = 128
    B, S, D = 16, 256, 256
    KD = D // P
    NB = S // P
    T = B * S
    NC = T // P
    H, DH = 16, 64
    INNER = H * DH
    NPAIR = H // 2
    W0, W1C = 1 + P, 1 + S
    SW = W0 + W1C
    EPS = 1e-5
    BIG = float(2.0 ** 100)
    E0, FF = 8, 1024
    NF = FF // P
    CAPACITY = int(np.ceil(T / E0 * 1.25))
    TILES = (T + E0 * (P - 1)) // P
    E1, M1 = 8, 128
    NSH = 2
    E2 = 8

    ctx = ExitStack()
    with ctx:
        def sb(name, shape, dt=F32):
            return ctx.enter_context(nc.sbuf_tensor(name, shape, dt))

        def sem(name):
            return ctx.enter_context(nc.semaphore(name))

        psum = ctx.enter_context(nc.psum_tensor("psum", [P, 8, 512], F32))
        bank = [psum[:, k, :] for k in range(8)]
        tokens = sb("tokens", [P, NC, D])
        big_w = sb("big_w", [P, E0 * KD * FF])
        arena = sb("arena", [P, 23200])

        class Arena:
            def __init__(self, base):
                self.base, self.at = base, 0

            def take(self, *shape, rows=P):
                n = int(np.prod(shape))
                ap = self.base[0:rows, self.at:self.at + n]
                self.at += n
                assert self.at <= self.base.shape[1], self.at
                if len(shape) == 2:
                    ap = ap.rearrange("p (a b) -> p a b", b=shape[1])
                if len(shape) == 3:
                    ap = ap.rearrange("p (a b c) -> p a b c", b=shape[1], c=shape[2])
                return ap

        ident = sb("ident", [P, P])
        ones = sb("ones", [P, P])
        before = sb("before", [P, P])
        iota_i = sb("iota_i", [P, P], I32)
        iota_f = sb("iota_f", [P, P])
        token_i = sb("token_i", [P, NC], I32)
        token_f = sb("token_f", [P, NC])
        rev8 = sb("rev8", [P, 8])
        ones_bf = sb("ones_bf", [1, P], BF16)
        penalty = sb("penalty", [1, B, SW], BF16)
        eps_col = sb("eps_col", [P, 1])
        gin = sb("gin", [P, KD])
        gout = sb("gout", [P, KD])
        nb_bc = sb("nb_bc", [P, H])
        xstat = sb("xstat", [P, NC, 6])
        xmv = sb("xmv", [P, NC, 2])
        rstd = sb("rstd", [P, NC])
        shift = sb("shift", [P, NC])
        ostat = sb("ostat", [P, NC, 6])
        router = sb("router", [P, KD, E0])

        A = Arena(arena)
        bias = A.take(H, SW)
        wq_s = A.take(KD, INNER)
        wkv_r = A.take(KD, 2 * DH)
        wk_s = A.take(KD, P)
        wv_s = A.take(KD, DH)
        wo_s = A.take(NPAIR, D)
        xn = A.take(NB, D)
        xn_t = A.take(KD, 1 + S)
        q_t = A.take(NPAIR, S)
        k_t = A.take(1 + S)
        v_s = A.take(NB, DH)
        v_last = A.take(NB, DH)
        null_v = A.take(DH)
        e_first = A.take(P)
        NSIM, NPR, NPN, NPT = 4, 2, 4, 4
        sim = A.take(NSIM, SW)
        pr = A.take(NPR, SW)
        pn = A.take(NPN, SW)
        p_t = A.take(NPT, 3 * P)
        p_last = A.take(NB, 2, NPAIR)
        nmax = A.take(NSIM, 2)
        psum_row = A.take(NPR, 2)
        rinv = A.take(NPR, 2)
        at_t = A.take(NPAIR, S)
        mask_u8 = at_t[0:1, 0:4, :].rearrange("p a b -> p (a b)").bitcast(U8)

        R = Arena(arena[:, E0 * NF * D:])
        omv = R.take(NC, 2)
        r_rstd = R.take(NC)
        h_n = [R.take(D) for _ in range(4)]
        h_t = [R.take(KD, P) for _ in range(2)]
        lg = R.take(NC, E0)
        lmax = R.take(NC)
        ex = R.take(NC, E0)
        esum = R.take(NC)
        prob = R.take(NC)
        hit = R.take(NC, E0)
        top = R.take(NC)
        oh = R.take(E0, NC)
        pe_key = R.take(E0, NC)
        thr = sb("thr", [P, E0], I32)
        cand = sb("cand", [P, E0], I32)
        bit = sb("bit", [P, E0], I32)
        step_bit = sb("step_bit", [P, E0], I32)
        cmp_s = R.take(E0, NC)
        part = R.take(E0)
        above = R.take(E0, NC)
        tie = R.take(E0, NC)
        budget = R.take(E0)
        tot = R.take(E0, NC)
        seg = R.take(E0, NC)
        run = R.take(E0, NC)
        rank = R.take(E0, NC)
        fin = R.take(E0, NC)
        kept = R.take(NC)
        cnt_i = sb("cnt_i", [P, E0], I32)
        ntile = R.take(E0)
        tcum = R.take(E0)
        tstart = R.take(E0)
        pos = R.take(NC)
        pos_i = sb("pos_i", [P, NC], I32)
        hi_i = sb("hi_i", [P, NC], I32)
        hi = R.take(NC)
        lo = R.take(NC)
        oh_lo = [R.take(P) for _ in range(2)]
        oh_hi = [R.take(TILES) for _ in range(2)]
        tcmp = R.take(TILES, E0 - 1)
        tile_f = R.take(TILES)
        tile_e = sb("tile_e", [P, TILES], I32)
        row_tok = sb("row_tok", [P, TILES], I32)

        G = Arena(arena)
        w2_s = G.take(E0, NF, D)
        b1_s = G.take(E0 * NF)
        b2_s = G.take(E0, D)
        gath = [G.take(D) for _ in range(2)]
        g_t = G.take(KD, P)
        act1 = [G.take(FF) for _ in range(2)]
        act_t = G.take(NF, P)
        y_s = [G.take(D) for _ in range(2)]
        w1_s = big_w[:, :].rearrange("p (e k f) -> p e k f", e=E0, k=KD)
        gidx = [sb(f"gidx{k}", [P, 1], I32) for k in range(2)]

        V = Arena(big_w)
        wt_s = V.take(KD, E1)
        wg_s = V.take(E1, rows=64)
        cond_s = V.take(B, rows=64)
        cond_bc = V.take(P, rows=64)
        mg_s = V.take(KD, (E1 + NSH) * M1)
        mu_s = V.take(KD, (E1 + NSH) * M1)
        md_s = V.take(E1 + NSH, D)
        ew_s = V.take(KD, E2, D)
        gw_s = V.take(KD, E2)
        gb_s = V.take(E2, rows=B)
        eb_s = V.take(KD, E2)
        N = Arena(arena)
        yg = [N.take(D) for _ in range(2)]
        x1_s = N.take(NB, D)
        x1_t = N.take(KD, S)
        cgo = N.take(B, E1)
        leak = [N.take(S) for _ in range(2)]
        mid = [N.take(S) for _ in range(2)]
        acc = N.take(NB, D)
        z_t = N.take(KD, T)
        pooled = N.take(KD, B)
        cg = N.take(B, E1)
        glog = N.take(NB, E1)
        gtop = N.take(NB, 8)
        gex = N.take(NB, E1)
        gsum = N.take(NB)
        grec = N.take(NB)
        gsc = N.take(NB, E1)
        gwsum = N.take(NB)
        gidx_f = N.take(NB, 8)
        gw2 = N.take(NB, 2)
        gone = N.take(NB, E1)
        gtwo = N.take(NB, E1)
        gate = N.take(NB, E1)
        gnm = N.take(NB)
        top_i = sb("top_i", [P, NB, 8], mybir.dt.uint32)
        flog = N.take(E2, rows=B)
        ftop = N.take(8, rows=B)
        fex = N.take(E2, rows=B)
        fnm = N.take(1, rows=B)
        fsum = N.take(1, rows=B)
        fkeep = N.take(E2, rows=B)
        fgate = N.take(E2, rows=B)
        fdiag = N.take(B, E2, rows=B)
        fg_bc = N.take(B, E2)
        ge = [N.take(2 * S) for _ in range(2)]
        accf = N.take(KD, 2 * S)
        res = N.take(2 * NB, D)

        h_dram = nc.dram_tensor("h_sorted_from", [T, D], F32, kind="Internal").ap()
        y_dram = nc.dram_tensor("y_sorted", [TILES * P, D], F32, kind="Internal").ap()

        ld_x = [sem(f"ld_x{k}") for k in range(4)]
        ld_w = sem("ld_w")
        ld_bias = sem("ld_bias")
        ld_mask = sem("ld_mask")
        ld_w1 = sem("ld_w1")
        ld_w2 = sem("ld_w2")
        ld_b = sem("ld_b")
        ld_v = sem("ld_v")
        ld_again = sem("ld_again")
        const = sem("const")
        setup = sem("setup")
        ready = sem("ready")
        xvar = sem("xvar")
        xsd = sem("xsd")
        xnorm = sem("xnorm")
        x_ps = sem("x_ps")
        x_ev = sem("x_ev")
        k_ps = sem("k_ps")
        k_ev = sem("k_ev")
        q_ps = sem("q_ps")
        q_ev = sem("q_ev")
        v_ps = sem("v_ps")
        v_ev = sem("v_ev")
        scores = sem("scores")
        simmed = sem("simmed")
        exped = sem("exped")
        recip = sem("recip")
        normed = sem("normed")
        turned = sem("turned")
        pt_ev = sem("pt_ev")
        pv = sem("pv")
        at_ev = sem("at_ev")
        last_ps = sem("last_ps")
        at_done = sem("at_done")
        o_ps = sem("o_ps")
        o_ev = sem("o_ev")
        o_bn = sem("o_bn")
        dch = sem("dch")
        ovar = sem("ovar")
        osd = sem("osd")
        hnorm = sem("hnorm")
        h_ps = sem("h_ps")
        h_ev = sem("h_ev")
        h_st = [sem(f"h_st{k}") for k in range(4)]
        lg_ps = sem("lg_ps")
        lsub = sem("lsub")
        lexp = sem("lexp")
        cpart = sem("cpart")
        csum = sem("csum")
        tie_in = sem("tie_in")
        tie_ps = sem("tie_ps")
        onehot = sem("onehot")
        tab_ps = sem("tab_ps")
        table = sem("table")
        idx_ok = sem("idx_ok")
        got = [sem(f"got{k}") for k in range(2)]
        g_ps = sem("g_ps")
        g_ev = sem("g_ev")
        up_ps = sem("up_ps")
        up_ev = sem("up_ev")
        t_ps = sem("t_ps")
        t_eva = sem("t_eva")
        t_evd = sem("t_evd")
        dn_ps = sem("dn_ps")
        dn_ev = sem("dn_ev")
        y_st = [sem(f"y_st{k}") for k in range(2)]
        ffn_done = sem("ffn_done")
        bch = sem("bch")
        sch = sem("sch")
        tch = sem("tch")
        gch = sem("gch")
        zch = sem("zch")
        fch = sem("fch")
        cb = sem("cb")
        cg_ps = sem("cg_ps")
        cg_ev = sem("cg_ev")
        idx2 = sem("idx2")
        got2 = [sem(f"got2{k}") for k in range(2)]
        x1 = sem("x1")
        x1_ps = sem("x1_ps")
        x1_ev = sem("x1_ev")
        rl_ps = sem("rl_ps")
        rl_sub = sem("rl_sub")
        rl_exp = sem("rl_exp")
        gu_ps = sem("gu_ps")
        lk = sem("lk")
        md = sem("md")
        d_ps = sem("d_ps")
        d_acc = sem("d_acc")
        yfin = sem("yfin")
        z_ps = sem("z_ps")
        z_ev = sem("z_ev")
        pool_r = sem("pool_r")
        fl_ps = sem("fl_ps")
        fl_sub = sem("fl_sub")
        fl_exp = sem("fl_exp")
        fdg = sem("fdg")
        fg_ps = sem("fg_ps")
        fg_ok = sem("fg_ok")
        e_ps = sem("e_ps")
        e_act = sem("e_act")
        e_acc = sem("e_acc")
        r_ps = sem("r_ps")
        r_ev = sem("r_ev")
        stored = sem("stored")
        held = sem("held")
        leaked = sem("leaked")

        def hold(eng, s, value):
            eng.wait_ge(s, value)
            eng.sem_inc(held)

        NSPB = 2
        NSTEP = 26
        THR0 = 0x3C000000

        NSETUP = 14
        NCONST = 15
        S_FREE, T_FREE, PV_FREE = 2, 2, 2

        block = ctx.enter_context(nc.Block())

        @block.sync
        def _(sp):
            for s in h_st + y_st + [stored]:
                sp.sem_inc(s, 16)
            xr = x.rearrange("(c p) d -> p c d", p=P)
            for k in range(4):
                n = NC // 4
                sp.dma_start(tokens[:, k * n:(k + 1) * n, :], xr[:, k * n:(k + 1) * n, :]).then_inc(ld_x[k], 16)
            for dst, src in (
                (gin[:, :], g_in), (wq_s, wq.rearrange("(k p) n -> p k n", p=P)),
                (wkv_r, wkv.rearrange("(k p) n -> p k n", p=P)), (nb_bc[:, :], null_bias.partition_broadcast(P)),
                (k_t[0:DH, 0:1], null_kv[0:1, :].rearrange("a d -> d a")),
                (k_t[DH:P, 0:1], null_kv[0:1, :].rearrange("a d -> d a")),
                (null_v[0:1, :], null_kv[1:2, :]), (gout[:, :], g_out),
                (router[:, :, :], router_t.rearrange("(k p) e -> p k e", p=P)),
            ):
                sp.dma_start(dst, src).then_inc(ld_w, 16)
            sp.dma_start(mask_u8, mask).then_inc(ld_mask, 16)
            sp.dma_start(bias[:, :, 1:W0], side[:, 0:P, 0:P].rearrange("h q k -> q h k")).then_inc(ld_bias, 16)
            sp.dma_start(bias[:, :, W0 + 1:SW], side[:, P:S, :].rearrange("h q k -> q h k")).then_inc(ld_bias, 16)
            sp.dma_start(wo_s, wo.rearrange("(j p) n -> p j n", p=P)).then_inc(ld_bias, 16)
            sp.dma_start(big_w[:, :], w1).then_inc(ld_w1, 16)
            sp.wait_ge(o_ps, B)
            sp.dma_start(w2_s, w2.rearrange("p (e k d) -> p e k d", e=E0, k=NF)).then_inc(ld_w2, 16)

            with sp.Fori(0, NC // 4) as r:
                for u in range(4):
                    sp.wait_ge(hnorm, 4 * r + u + 1)
                    sp.dma_start(h_dram[bass.ds((4 * r + u) * P, P), :], h_n[u]).then_inc(h_st[u], 16)
            sp.dma_start(tokens[:, :, :], xr).then_inc(ld_again, 16)
            sp.wait_ge(table, 1)
            sp.dma_start(b1_s, b1).then_inc(ld_b, 16)
            sp.dma_start(b2_s, b2.rearrange("e d -> (e d)").partition_broadcast(P)
                         .rearrange("p (e d) -> p e d", e=E0)).then_inc(ld_b, 16)

            def store_tile(i, u):
                sp.wait_ge(dn_ev, i + 1 + 2)
                sp.dma_start(y_dram[bass.ds(i * P, P), :], y_s[u]).then_inc(y_st[u], 16)

            store_tile(0, 0)
            with sp.Fori(0, (TILES - 1) // 2) as r:
                for v in range(2):
                    store_tile(1 + 2 * r + v, (1 + v) % 2)
            sp.wait_ge(up_ps, TILES)
            for dst, src in (
                (wt_s, wt_t.rearrange("(k p) e -> p k e", p=P)), (wg_s, wg_t), (cond_s, cond_t),
                (mg_s[:, :, 0:E1 * M1], moe_gate), (mg_s[:, :, E1 * M1:], sw_gate.rearrange("(k p) m -> p k m", p=P)),
                (mu_s[:, :, 0:E1 * M1], moe_up), (mu_s[:, :, E1 * M1:], sw_up.rearrange("(k p) m -> p k m", p=P)),
                (md_s[:, 0:E1, :], moe_down.rearrange("e m d -> m e d")),
                (md_s[:, E1:, :], sw_down.rearrange("(k p) d -> p k d", p=P)),
                (ew_s, expert_w_t), (gw_s, gate_w_t.rearrange("(k p) e -> p k e", p=P)),
                (gb_s, gate_b.partition_broadcast(B)), (eb_s, expert_b_t),
            ):
                sp.dma_start(dst, src).then_inc(ld_v, 16)
            outr = out.rearrange("(c p) d -> p c d", p=P)
            with sp.Fori(0, B // 2) as r:
                sp.wait_ge(r_ev, r + 2)
                sp.dma_start(outr[:, bass.ds(r * 2 * NB, 2 * NB), :], res).then_inc(stored, 16)
            sp.wait_ge(stored, 16 * (B // 2) + 16)

        @block.gpsimd
        def _(pool):
            pool.sem_inc(normed, NPR)
            pool.memset(ident[:, :], 0.0).then_inc(const, 1)
            pool.memset(ones[:, :], 1.0).then_inc(const, 1)
            pool.memset(ones_bf[:, :], 1.0).then_inc(const, 1)
            pool.memset(eps_col[:, :], EPS).then_inc(const, 1)
            pool.memset(e_first[0:1, :], 0.0).then_inc(const, 1)
            pool.memset(xn_t[:, :, 0:1], 0.0).then_inc(const, 1)
            pool.memset(penalty[:, :, :], 0.0).then_inc(const, 1)
            pool.iota(iota_i[:, :], [[1, P]], base=0, channel_multiplier=0).then_inc(const, 1)
            pool.iota(token_i[:, :], [[P, NC]], base=0, channel_multiplier=1).then_inc(const, 1)
            pool.wait_ge(const, 9)
            pool.affine_select(out=ident[:, :], in_=ident[:, :], compare_op=ALU.not_equal, fill=1.0, base=0,
                               pattern=[[-1, P]], channel_multiplier=1).then_inc(const, 1)
            pool.affine_select(out=before[:, :], in_=ones[:, :], compare_op=ALU.is_gt, fill=0.0, base=0,
                               pattern=[[1, P]], channel_multiplier=-1).then_inc(const, 1)
            pool.memset(e_first[0:1, 0:1], 1.0).then_inc(const, 1)
            pool.wait_ge(ld_bias, 48)
            for c0 in (1, W0 + 1 + P):
                pool.affine_select(out=bias[:, :, c0:c0 + P], in_=bias[:, :, c0:c0 + P], compare_op=ALU.is_ge, fill=-BIG,
                                   base=0, pattern=[[0, H], [-1, P]], channel_multiplier=1).then_inc(const, 1)
            pool.memset(v_last, 0.0).then_inc(const, 1)

            def norm_head(b, s):
                g = b * H + s
                pool.wait_ge(recip, g + 1)
                hold(pool, turned, g + 1)
                if s == 0:
                    hold(pool, last_ps, b + 1)
                src, dst, ri = pr[:, s % NPR, :], pn[:, s % NPN, :], rinv[:, s % NPR, :]
                pool.tensor_tensor(p_last[:, :, s % 2, s // 2], src[:, P:SW:S + 1], ri, ALU.mult)
                pool.tensor_scalar(dst[:, 0:W0], src[:, 0:W0], ri[:, 0:1], None, ALU.mult)
                pool.tensor_scalar(dst[:, W0:SW], src[:, W0:SW], ri[:, 1:2], None, ALU.mult).then_inc(normed, 1)

            with pool.Fori(0, B) as b:
                for s in range(H):
                    norm_head(b, s)

            pool.wait_ge(table, 1)
            for u in range(4):
                pool.wait_ge(h_st[u], 16 * (NC // 4) + 16)

            def gather(i, u):
                hold(pool, g_ps, i + 1)
                pool.tensor_copy(gidx[u][:, :], row_tok[:, bass.ds(i, 1)]).then_inc(idx_ok, 1)
                hold(pool, idx_ok, i + 1)
                pool.indirect_dma_start(gath[u], None, h_dram, bass.IndirectOffsetOnAxis(ap=gidx[u][:, 0:1], axis=0)
                                        ).then_inc(got[u], 16)

            gather(0, 0)
            with pool.Fori(0, (TILES - 1) // 2) as r:
                for v in range(2):
                    gather(1 + 2 * r + v, (1 + v) % 2)

            pool.wait_ge(y_st[0], 16 * ((TILES + 1) // 2) + 16)
            pool.wait_ge(y_st[1], 16 * (TILES // 2) + 16)
            with pool.Fori(0, B) as b:
                for k in range(NB):
                    hold(pool, x1, NB * b + k + 1)
                    pool.tensor_copy(gidx[k][:, :], pos_i[:, bass.ds(b * NB + k, 1)]).then_inc(idx2, 1)
                    hold(pool, idx2, NB * b + k + 1)
                    pool.indirect_dma_start(yg[k], None, y_dram,
                                            bass.IndirectOffsetOnAxis(ap=gidx[k][:, 0:1], axis=0)).then_inc(got2[k], 16)

        @block.tensor
        def _(pe):
            pe.sem_inc(turned, NPN)
            pe.sem_inc(pv, NPT)
            pe.sem_inc(last_ps, 1)
            pe.sem_inc(h_ps, 4)
            pe.sem_inc(lg_ps, 2)
            pe.sem_inc(g_ps, 2)
            pe.sem_inc(x1_ps, 1)
            pe.sem_inc(z_ps, 1)
            pe.sem_inc(r_ps, 1)
            b_s, b_t, b_pv, b_a, b_b = bank[0:2], bank[2:4], bank[4:6], bank[6], bank[7]

            def project_x(b, first):
                pe.wait_ge(xnorm, b + 1)
                if not first:
                    pe.wait_ge(o_ev, b)
                for k in range(KD):
                    for n in range(NB):
                        mm = pe.transpose(b_a[:, k * S + n * P:k * S + (n + 1) * P], xn[:, n, k * P:(k + 1) * P], ident[:, :])
                mm.then_inc(x_ps, 1)
                pe.wait_ge(x_ev, b + 1)
                if not first:
                    pe.wait_ge(v_ev, b)
                for k in range(KD):
                    mm = pe.matmul(b_b[:, 0:S], wk_s[:, k, :], xn_t[:, k, 1:1 + S], start=k == 0, stop=k == KD - 1)
                mm.then_inc(k_ps, 1)
                for j in range(4):
                    bk = (b_a, b_b)[j % 2]
                    if j == 1:
                        pe.wait_ge(k_ev, b + 1)
                    if j >= 2:
                        pe.wait_ge(q_ev, 4 * b + j - 1)
                    for i in range(2):
                        for k in range(KD):
                            c = (2 * j + i) * P
                            mm = pe.matmul(bk[:, i * S:(i + 1) * S], wq_s[:, k, c:c + P], xn_t[:, k, 1:1 + S],
                                           start=k == 0, stop=k == KD - 1)
                    mm.then_inc(q_ps, 1)

            def project_v(b):
                pe.wait_ge(q_ev, 4 * b + 4)
                for n in range(NB):
                    o = b_b[:, S + n * DH:S + (n + 1) * DH]
                    for k in range(KD):
                        pe.matmul(o, xn_t[:, k, n * P:(n + 1) * P], wv_s[:, k, :], start=k == 0, stop=n == 1 and k == KD - 1)
                    if n == 0:
                        pe.matmul(o, e_first[0:1, :], null_v[0:1, :], start=False, stop=True)
                for n in range(NB):
                    o = b_b[96:P, S + P + n * DH:S + P + (n + 1) * DH]
                    for k in range(KD):
                        mm = pe.matmul(o, xn_t[:, k, 97 + n * P:129 + n * P], wv_s[:, k, :], start=k == 0, stop=k == KD - 1)
                mm.then_inc(v_ps, 1)

            def qk(b, s):
                g, bk = b * H + s, b_s[s % 2]
                half = slice(DH * (s % 2), DH * (s % 2) + DH)
                if s == 0:
                    pe.wait_ge(q_ev, 4 * b + 4)
                    pe.wait_ge(k_ev, b + 1)
                hold(pe, simmed, g + 1)
                pe.matmul(bk[:, 0:SW], ones_bf[0:1, :], penalty[0:1, bass.ds(b, 1), :].rearrange("p a c -> p (a c)"),
                          start=True, stop=False)
                for c0, w, n in ((0, W0, 0), (W0, W1C, 1)):
                    mm = pe.matmul(bk[:, c0:c0 + w], q_t[half, s // 2, n * P:(n + 1) * P], k_t[half, 0:w],
                                   start=False, stop=n == NB - 1)
                mm.then_inc(scores, 1)

            def turn(b, s):
                g, bk = b * H + s, b_t[s % 2]
                pe.wait_ge(normed, g + 1 + NPR)
                pe.wait_ge(pt_ev, g + 1)
                for n, c0 in enumerate((0, W0, W0 + P)):
                    mm = pe.transpose(bk[:, n * P:(n + 1) * P], pn[:, s % NPN, c0:c0 + P], ident[:, :])
                mm.then_inc(turned, 1)

            def weigh(b, s):
                g, j = b * H + s, s // 2
                pe.wait_ge(pt_ev, g + 1 + T_FREE)
                if s == 0:
                    pe.wait_ge(v_ev, b + 1)
                if s % 4 == 0:
                    pe.wait_ge(at_ev, 4 * b + s // 4 + 1)
                o = b_pv[(s // 4) % 2][DH * (s % 2):DH * (s % 2) + DH, (j % 2) * S:(j % 2) * S + S]
                pe.matmul(o, v_s[:, 0, :], p_t[:, s % NPT, 0:S], start=True, stop=False)
                pe.matmul(o[:, P:S], v_s[:, 1, :], p_t[:, s % NPT, S:S + P], start=False, stop=True).then_inc(pv, 1)

            def last_keys(b):
                pe.wait_ge(normed, (b + 1) * H + NPR)
                pe.wait_ge(pt_ev, (b + 1) * H - 1 + T_FREE)
                for n in range(NB):
                    for hf in range(2):
                        mm = pe.matmul(b_t[0][DH * hf:DH * hf + DH, n * NPAIR:(n + 1) * NPAIR], v_last[96:P, n, :],
                                       p_last[96:P, n, hf, :], start=True, stop=True)
                mm.then_inc(last_ps, 1)

            def project_o(b):
                pe.wait_ge(at_done, b + 1)
                for n in range(NB):
                    for j in range(NPAIR):
                        mm = pe.matmul(b_a[:, n * D:(n + 1) * D], at_t[:, j, n * P:(n + 1) * P], wo_s[:, j, :],
                                       start=j == 0, stop=j == NPAIR - 1)
                mm.then_inc(o_ps, 1)

            def attend(b, more):
                for s in range(H):
                    qk(b, s)
                    if s >= 2:
                        turn(b, s - 2)
                    if s >= 3:
                        weigh(b, s - 3)
                if more:
                    project_x(b + 1, False)
                turn(b, H - 2)
                weigh(b, H - 3)
                turn(b, H - 1)
                weigh(b, H - 2)
                weigh(b, H - 1)
                last_keys(b)
                if more:
                    project_v(b + 1)
                project_o(b)

            pe.wait_ge(const, NCONST)
            pe.wait_ge(setup, NSETUP)
            pe.wait_ge(ld_w, 16 * 9)
            pe.wait_ge(ld_bias, 48)
            project_x(0, True)
            project_v(0)
            with pe.Fori(0, B - 1) as b:
                attend(b, True)
            attend(B - 1, False)

            pe.wait_ge(o_ev, B + 1)
            with pe.Fori(0, NC // 4) as r:
                for half in range(2):
                    for u in (2 * half, 2 * half + 1):
                        c = 4 * r + u
                        pe.wait_ge(hnorm, c + 1)
                        pe.wait_ge(h_ev, c + 1)
                        for k in range(KD):
                            mm = pe.transpose(bank[u % 2][:, k * P:(k + 1) * P], h_n[u][:, k * P:(k + 1) * P], ident[:, :])
                        mm.then_inc(h_ps, 1)
                    for u in (2 * half, 2 * half + 1):
                        c = 4 * r + u
                        pe.wait_ge(h_ev, c + 1 + 2)
                        for k in range(KD):
                            mm = pe.matmul(bank[7][:, bass.ds(c * E0, E0)], h_t[u % 2][:, k, :], router[:, k, :],
                                           start=k == 0, stop=k == KD - 1)
                        mm.then_inc(lg_ps, 1)
            cols = E0 * NC
            with pe.Fori(0, NSTEP + 1) as r:
                pe.wait_ge(cpart, r + 1)
                pe.matmul(bank[6][:, 0:E0], ones[:, :], part, start=True, stop=True).then_inc(csum, 1)
            for n, what in enumerate((tie, fin)):
                flat = what.rearrange("p e c -> p (e c)")
                pe.wait_ge(tie_in, n + 1)
                pe.matmul(bank[4][:, 0:cols], before[:, :], flat, start=True, stop=True)
                pe.matmul(bank[5][:, 0:cols], ones[:, :], flat, start=True, stop=True).then_inc(tie_ps, 1)

            def table_pair(c, first, last):
                for u in range(2):
                    pe.wait_ge(onehot, c + u + 1)
                    pe.matmul(bank[3][:, 0:TILES], oh_lo[u], oh_hi[u], start=first and u == 0, stop=last and u == 1,
                              ).then_inc(tab_ps, 1)

            table_pair(0, True, False)
            with pe.Fori(1, NC // 2 - 1) as r:
                table_pair(2 * r, False, False)
            table_pair(NC - 2, False, True)

            def expert_of(i):
                return pe.value_load(tile_e[0:1, bass.ds(i, 1)], min_val=0, max_val=E0 - 1)

            def rows_in(i, u, turn_no):
                hold(pe, got[u], 16 * turn_no + 16)
                pe.wait_ge(g_ev, i)
                for k in range(KD):
                    mm = pe.transpose(bank[0][:, k * P:(k + 1) * P], gath[u][:, k * P:(k + 1) * P], ident[:, :])
                mm.then_inc(g_ps, 1)

            def expert_up(i, last=False):
                e = expert_of(i)
                pe.wait_ge(g_ev, i + 1)
                pe.wait_ge(up_ev, i)
                for k in range(KD):
                    for f in range(2):
                        mm = pe.matmul(bank[1 + f], g_t[:, k, :],
                                       big_w[:, bass.ds(e * (KD * FF) + (k * FF + f * 512), 512)],
                                       start=k == 0, stop=k == KD - 1)
                mm.then_inc(up_ps, 1)
                return mm

            def turn_up(j, u):
                pe.wait_ge(up_ev, j + 1)
                pe.wait_ge(t_eva, j + 1)
                pe.wait_ge(t_evd, j + 1)
                for f in range(NF):
                    mm = pe.transpose(bank[3 + f // 4][:, (f % 4) * P:(f % 4 + 1) * P], act1[u][:, f * P:(f + 1) * P], ident[:, :])
                mm.then_inc(t_ps, 1)

            def expert_down(j, u):
                e = expert_of(j)
                pe.wait_ge(t_eva, j + 2)
                pe.wait_ge(t_evd, j + 2)
                pe.wait_ge(dn_ev, j + 1)
                for f in range(NF):
                    mm = pe.matmul(bank[5 + u][:, 0:D], act_t[:, f, :], arena[:, bass.ds(e * (NF * D) + f * D, D)],
                                   start=f == 0, stop=f == NF - 1)
                mm.then_inc(dn_ps, 1)

            pe.wait_ge(table, 1)
            pe.wait_ge(ld_w1, 16)
            pe.wait_ge(ld_w2, 16)
            rows_in(0, 0, 0)
            expert_up(0)
            with pe.Fori(0, (TILES - 1) // 2) as r:
                for v in range(2):
                    i = 1 + 2 * r + v
                    rows_in(i, (1 + v) % 2, r + v)
                    turn_up(i - 1, v)
                    expert_up(i)
                    expert_down(i - 1, v)
            turn_up(TILES - 1, 0)
            expert_down(TILES - 1, 0)

            pe.wait_ge(ld_v, 16 * 13)
            pe.wait_ge(cb, 1)
            pe.matmul(bank[7][:, 0:B * E1], ones[0:64, :], cgo[0:64].rearrange("p b e -> p (b e)"),
                      start=True, stop=True).then_inc(cg_ps, 1)

            NQ = NSH + E1

            def up_gate(b, q):
                m = (E1 + q) if q < NSH else q - NSH
                n = NQ * b + q
                pe.wait_ge(md, n + 1)
                bk = bank[2 + q % 2]
                for half, w in enumerate((mg_s, mu_s)):
                    for k in range(KD):
                        mm = pe.matmul(bk[:, half * S:(half + 1) * S], w[:, k, m * M1:(m + 1) * M1], x1_t[:, k, :],
                                       start=k == 0, stop=k == KD - 1)
                mm.then_inc(gu_ps, 1)

            def down_shared(b):
                pe.wait_ge(md, NQ * b + NSH + 2)
                pe.wait_ge(d_acc, (1 + E1) * b + 2)
                for n in range(NB):
                    for q in range(NSH):
                        mm = pe.matmul(bank[4][:, n * D:(n + 1) * D], mid[q][:, n * P:(n + 1) * P], md_s[:, E1 + q, :],
                                       start=q == 0, stop=q == NSH - 1)
                mm.then_inc(d_ps, 1)

            def down(b, q):
                e = q - NSH
                pe.wait_ge(md, NQ * b + q + 1 + 2)
                pe.wait_ge(d_acc, (1 + E1) * b + e + 2)
                for n in range(NB):
                    mm = pe.matmul(bank[4 + (1 + e) % 2][:, n * D:(n + 1) * D], mid[q % 2][:, n * P:(n + 1) * P],
                                   md_s[:, e, :], start=True, stop=True)
                mm.then_inc(d_ps, 1)

            with pe.Fori(0, B) as b:
                pe.wait_ge(x1, NB * (b + 1) + 2)
                pe.wait_ge(x1_ev, b + 1)
                for k in range(KD):
                    for n in range(NB):
                        mm = pe.transpose(bank[0][:, k * S + n * P:k * S + (n + 1) * P], x1_s[:, n, k * P:(k + 1) * P], ident[:, :])
                mm.then_inc(x1_ps, 1)
                pe.wait_ge(x1_ev, b + 2)
                pe.wait_ge(rl_sub, b + 1)
                for n in range(NB):
                    for k in range(KD):
                        mm = pe.matmul(bank[1][:, n * E1:(n + 1) * E1], x1_t[:, k, n * P:(n + 1) * P], wt_s[:, k, :],
                                       start=k == 0, stop=k == KD - 1)
                mm.then_inc(rl_ps, 1)
                up_gate(b, 0)
                up_gate(b, 1)
                down_shared(b)
                up_gate(b, 2)
                for q in range(NSH, NQ):
                    if q + 1 < NQ:
                        up_gate(b, q + 1)
                    down(b, q)
                pe.wait_ge(yfin, b + 1)
                pe.wait_ge(z_ev, b + 1)
                pe.wait_ge(pool_r, b + 1)
                for k in range(KD):
                    for n in range(NB):
                        mm = pe.transpose(bank[6][:, k * S + n * P:k * S + (n + 1) * P], acc[:, n, k * P:(k + 1) * P], ident[:, :])
                mm.then_inc(z_ps, 1)

            pe.wait_ge(pool_r, B + 1)
            for k in range(KD):
                mm = pe.matmul(bank[1][0:B, 0:E2], pooled[:, k, :], gw_s[:, k, :], start=k == 0, stop=k == KD - 1)
            mm.then_inc(fl_ps, 1)
            pe.wait_ge(fdg, 1)
            pe.matmul(bank[7][:, 0:B * E2], ones[0:B, :], fdiag.rearrange("p b e -> p (b e)"), start=True, stop=True).then_inc(fg_ps, 1)
            pe.wait_ge(z_ev, B + 1)
            NE = E2 * KD
            with pe.Fori(0, B // 2) as r:
                for e in range(E2):
                    for oc in range(KD):
                        q = e * KD + oc
                        pe.wait_ge(e_act, NE * r + q + 1)
                        for k in range(KD):
                            mm = pe.matmul(bank[2 + q % 2], ew_s[:, k, e, oc * P:(oc + 1) * P], z_t[:, k, bass.ds(r * 2 * S, 2 * S)],
                                           start=k == 0, stop=k == KD - 1)
                        mm.then_inc(e_ps, 1)
                pe.wait_ge(e_acc, NE * (r + 1) + 2)
                pe.wait_ge(r_ev, r + 1)
                for n in range(2 * NB):
                    for oc in range(KD):
                        mm = pe.transpose(bank[4 + n // 2][:, (n % 2) * D + oc * P:(n % 2) * D + (oc + 1) * P],
                                          accf[:, oc, n * P:(n + 1) * P], ident[:, :])
                mm.then_inc(r_ps, 1)

        @block.scalar
        def _(act):
            act.sem_inc(exped, NSIM)
            act.sem_inc(o_ev, 1)
            act.sem_inc(t_eva, 1)
            act.sem_inc(x1_ev, 1)
            act.sem_inc(z_ev, 1)
            act.sem_inc(h_ev, 2)
            act.sem_inc(e_act, 2)
            b_a, b_b = bank[6], bank[7]
            act.wait_ge(const, NCONST)
            act.wait_ge(xvar, 1)
            act.activation(rstd[:, :], xmv[:, :, 1], ACT.Sqrt, bias=eps_col[:, 0:1]).then_inc(xsd, 1)

            def copies(b):
                act.wait_ge(x_ps, b + 1)
                act.copy(xn_t[:, :, 1:1 + S], b_a.rearrange("p (k t) -> p k t", k=KD)).then_inc(x_ev, 1)
                act.wait_ge(k_ps, b + 1)
                act.copy(k_t[:, 1:1 + S], b_b[:, 0:S]).then_inc(k_ev, 1)
                for j in range(4):
                    act.wait_ge(q_ps, 4 * b + j + 1)
                    act.copy(q_t[:, 2 * j:2 * j + 2, :], (b_a, b_b)[j % 2].rearrange("p (a t) -> p a t", a=2)).then_inc(q_ev, 1)

            def attend(b, more):
                for s in range(H):
                    g = b * H + s
                    act.wait_ge(normed, g + 1)
                    act.wait_ge(simmed, g + 1 + S_FREE)
                    for n, (c0, c1) in enumerate(((0, W0), (W0, SW))):
                        a = act.activation(pr[:, s % NPR, c0:c1], sim[:, s % NSIM, c0:c1], ACT.Exp,
                                           bias=nmax[:, s % NSIM, n:n + 1], scale=-1.0,
                                           accum_out=psum_row[:, s % NPR, n:n + 1])
                    a.then_inc(exped, 1)
                if more:
                    copies(b + 1)
                hold(act, o_ps, b + 1)
                act.copy(tokens[:, bass.ds(b * NB, NB), :], b_a.rearrange("p (n d) -> p n d", n=NB)).then_inc(o_ev, 1)

            act.wait_ge(setup, NSETUP)
            copies(0)
            with act.Fori(0, B - 1) as b:
                attend(b, True)
            attend(B - 1, False)

            act.wait_ge(ovar, 1)
            act.activation(r_rstd, omv[:, :, 1], ACT.Sqrt, bias=eps_col[:, 0:1]).then_inc(osd, 1)
            with act.Fori(0, NC // 4) as r:
                for u in range(4):
                    c = 4 * r + u
                    act.wait_ge(lg_ps, c + 1)
                    act.wait_ge(h_ps, c + 1 + 4)
                    act.copy(h_t[u % 2], bank[u % 2][:, 0:D].rearrange("p (k t) -> p k t", k=KD)).then_inc(h_ev, 1)
            act.wait_ge(lsub, 1)
            act.activation(ex, ex, ACT.Exp).then_inc(lexp, 1)

            act.wait_ge(ld_b, 32)
            act.wait_ge(table, 1)

            def up_copy(i, u):
                act.wait_ge(up_ps, i + 1)
                act.copy(act1[u].rearrange("p (a f) -> p a f", a=2), psum[:, 1:3, :]).then_inc(up_ev, 1)

            def relu_half(j):
                e = act.value_load(tile_e[0:1, bass.ds(j, 1)], min_val=0, max_val=E0 - 1)
                hold(act, t_ps, j + 1)
                for f in range(NF // 2):
                    a = act.activation(act_t[:, f, :], bank[3][:, f * P:(f + 1) * P], ACT.Relu,
                                       bias=b1_s[:, bass.ds(e * NF + f, 1)])
                a.then_inc(t_eva, 1)

            up_copy(0, 0)
            with act.Fori(0, (TILES - 1) // 2) as r:
                for v in range(2):
                    i = 1 + 2 * r + v
                    relu_half(i - 1)
                    up_copy(i, (1 + v) % 2)
            relu_half(TILES - 1)

            NQ = NSH + E1
            with act.Fori(0, B) as b:
                act.wait_ge(x1_ps, b + 2)
                act.copy(x1_t, bank[0].rearrange("p (k t) -> p k t", k=KD)).then_inc(x1_ev, 1)

                def leaky(q):
                    act.wait_ge(gu_ps, NQ * b + q + 1)
                    act.wait_ge(md, NQ * b + q + 1)
                    act.copy(leak[q % 2], bank[2 + q % 2][:, 0:S]).then_inc(lk, 1)

                act.wait_ge(rl_sub, b + 2)
                act.activation(gex, gex, ACT.Exp, scale=0.5).then_inc(rl_exp, 1)
                for q in range(NQ):
                    leaky(q)
                hold(act, z_ps, b + 2)
                act.copy(z_t[:, :, bass.ds(b * S, S)], bank[6].rearrange("p (k t) -> p k t", k=KD)).then_inc(z_ev, 1)
            act.wait_ge(fl_sub, 1)
            act.activation(fex, flog, ACT.Exp, bias=fnm[:, 0:1]).then_inc(fl_exp, 1)
            NE = E2 * KD
            with act.Fori(0, B // 2) as r:
                for e in range(E2):
                    for oc in range(KD):
                        q = e * KD + oc
                        act.wait_ge(e_ps, NE * r + q + 1)
                        act.wait_ge(e_acc, NE * r + q + 1)
                        act.activation(ge[q % 2], bank[2 + q % 2], ACT.Gelu, bias=eb_s[:, oc, e:e + 1]).then_inc(e_act, 1)

        @block.vector
        def _(dve):
            dve.sem_inc(simmed, S_FREE)
            dve.sem_inc(pt_ev, T_FREE)
            dve.sem_inc(at_ev, PV_FREE)
            dve.sem_inc(dn_ev, 2)
            dve.sem_inc(t_evd, 1)
            dve.sem_inc(rl_sub, 1)
            dve.sem_inc(pool_r, 1)
            dve.sem_inc(r_ev, 1)
            dve.sem_inc(x1, 2)
            dve.sem_inc(md, 2)
            dve.sem_inc(d_acc, 2)
            dve.sem_inc(e_acc, 2)
            b_s, b_t, b_pv, b_a, b_b = bank[0:2], bank[2:4], bank[4:6], bank[6], bank[7]

            for k in range(4):
                dve.wait_ge(ld_x[k], 16)
                for c in range(k * NC // 4, (k + 1) * NC // 4):
                    st = dve.bn_stats(xstat[:, c, :], tokens[:, c, :])
            st.then_inc(sch, 1)
            dve.wait_ge(sch, 1)
            for c in range(NC):
                st = dve.bn_aggr(xmv[:, c, :], xstat[:, c, :])
            st.then_inc(xvar, 1)
            dve.wait_ge(ld_w, 16 * 9)
            for k in range(KD):
                dve.tensor_scalar(wq_s[:, k, :], wq_s[:, k, :], gin[:, k:k + 1], DH ** -0.5, ALU.mult, ALU.mult).then_inc(setup, 1)
                for half in range(2):
                    dve.tensor_scalar(wk_s[:, k, half * DH:(half + 1) * DH], wkv_r[:, k, 0:DH], gin[:, k:k + 1], None,
                                      ALU.mult)
                dve.tensor_scalar(wv_s[:, k, :], wkv_r[:, k, DH:], gin[:, k:k + 1], None, ALU.mult).then_inc(setup, 1)
                dve.tensor_scalar(router[:, k, :], router[:, k, :], gout[:, k:k + 1], None, ALU.mult).then_inc(setup, 1)
            dve.wait_ge(ld_bias, 48)
            for c0 in (0, W0):
                dve.tensor_copy(bias[:, :, c0], nb_bc[:, :]).then_inc(setup, 1)
            dve.wait_ge(const, NCONST)
            dve.tensor_copy(iota_f[:, :], iota_i[:, :]).then_inc(setup, 1)
            dve.tensor_copy(token_f[:, :], token_i[:, :]).then_inc(setup, 1)
            dve.tensor_scalar(rev8[:, :], iota_i[:, 0:8], -1.0, 8.0, ALU.mult, ALU.add).then_inc(setup, 1)
            dve.wait_ge(ld_mask, 16)
            mv = mask_u8.rearrange("p (b s) -> p b s", b=B)
            dve.tensor_scalar(penalty[:, :, 1:W0], mv[:, :, 0:P], BIG, -BIG, ALU.mult, ALU.add).then_inc(setup, 1)
            dve.tensor_scalar(penalty[:, :, W0 + 1:SW], mv, BIG, -BIG, ALU.mult, ALU.add).then_inc(setup, 1)
            dve.wait_ge(xsd, 1)
            dve.reciprocal(rstd[:, :], rstd[:, :]).then_inc(setup, 1)
            dve.wait_ge(setup, NSETUP)
            dve.scalar_tensor_tensor(shift[:, :], xmv[:, :, 0], -1.0, rstd[:, :], ALU.mult, ALU.mult).then_inc(sch, 1)
            dve.wait_ge(sch, 2)

            def normalise_x(b, first):
                if not first:
                    dve.wait_ge(x_ps, b)
                for n in range(NB):
                    c = b * NB + n
                    i = dve.tensor_scalar(xn[:, n, :], tokens[:, bass.ds(c, 1), :].rearrange("p a d -> p (a d)"),
                                          rstd[:, bass.ds(c, 1)], shift[:, bass.ds(c, 1)], ALU.mult, ALU.add)
                i.then_inc(xnorm, 1)

            def copy_v(b):
                dve.wait_ge(v_ps, b + 1)
                dve.tensor_copy(v_last[96:P, :, :], b_b[96:P, S + P:2 * S].rearrange("p (n d) -> p n d", n=NB))
                dve.tensor_copy(v_s[:, :, :], b_b[:, S:S + P].rearrange("p (n d) -> p n d", n=NB)).then_inc(v_ev, 1)

            def biased(b, s):
                g = b * H + s
                dve.wait_ge(exped, g + 1)
                hold(dve, scores, g + 1)
                for n, (c0, c1) in enumerate(((0, W0), (W0, SW))):
                    i = dve.tensor_tensor_reduce(sim[:, s % NSIM, c0:c1], b_s[s % 2][:, c0:c1], bias[:, s, c0:c1], -1.0, 3e38,
                                                 ALU.add, ALU.min, nmax[:, s % NSIM, n:n + 1])
                i.then_inc(simmed, 1)

            def invert(b, s):
                g = b * H + s
                dve.wait_ge(normed, g + 1)
                dve.wait_ge(exped, g + 1 + NSIM)
                dve.reciprocal(rinv[:, s % NPR, :], psum_row[:, s % NPR, :]).then_inc(recip, 1)

            def copy_pt(b, s):
                g = b * H + s
                dve.wait_ge(turned, g + 1 + NPN)
                dve.wait_ge(pv, g + 1)
                dve.tensor_copy(p_t[:, s % NPT, :], b_t[s % 2][:, 0:3 * P]).then_inc(pt_ev, 1)

            def copy_at(b, k):
                dve.wait_ge(pv, b * H + 4 * k + 4 + NPT)
                dve.tensor_copy(at_t[:, 2 * k:2 * k + 2, :], b_pv[k % 2].rearrange("p (a t) -> p a t", a=2)).then_inc(at_ev, 1)

            def attend(b, more):
                for s in range(H):
                    biased(b, s)
                    if s >= 1:
                        invert(b, s - 1)
                    if s >= 2:
                        copy_pt(b, s - 2)
                    if s >= 7 and s % 4 == 3:
                        copy_at(b, (s - 7) // 4)
                    if s == 8 and more:
                        normalise_x(b + 1, False)
                invert(b, H - 1)
                copy_pt(b, H - 2)
                copy_pt(b, H - 1)
                copy_at(b, 3)
                dve.wait_ge(last_ps, b + 2)
                dve.wait_ge(at_ev, 4 * b + 4 + PV_FREE)
                dve.tensor_tensor(at_t[:, :, P - 1:S:P], at_t[:, :, P - 1:S:P],
                                  b_t[0][:, 0:NB * NPAIR].rearrange("p (n j) -> p j n", n=NB), ALU.add).then_inc(at_done, 1)
                if more:
                    copy_v(b + 1)
            normalise_x(0, True)
            copy_v(0)
            with dve.Fori(0, B - 1) as b:
                attend(b, True)
            attend(B - 1, False)

            steps = [0]

            def link(ins):
                steps[0] += 1
                ins.then_inc(dch, 1)
                dve.wait_ge(dch, steps[0])

            dve.wait_ge(o_ev, B + 1)
            for c in range(NC):
                i = dve.bn_stats(ostat[:, c, :], tokens[:, c, :])
            link(i)
            for c in range(NC):
                i = dve.bn_aggr(omv[:, c, :], ostat[:, c, :])
            i.then_inc(ovar, 1)
            dve.wait_ge(osd, 1)
            link(dve.reciprocal(r_rstd, r_rstd))
            dve.wait_ge(o_ev, B + 1)
            with dve.Fori(0, NC // 4) as r:
                for u in range(4):
                    c = 4 * r + u
                    dve.wait_ge(h_ps, c + 1)
                    dve.wait_ge(h_st[u], 16 * r + 16)
                    dve.tensor_scalar(h_n[u], tokens[:, bass.ds(c, 1), :].rearrange("p a d -> p (a d)"),
                                      omv[:, bass.ds(c, 1), 0], r_rstd[:, bass.ds(c, 1)], ALU.subtract, ALU.mult).then_inc(hnorm, 1)
            dve.wait_ge(lg_ps, NC + 2)
            link(dve.tensor_copy(lg, bank[7][:, 0:NC * E0].rearrange("p (c e) -> p c e", e=E0)))
            link(dve.tensor_reduce(lmax, lg, AXX, ALU.max))
            bc = [P, NC, E0]
            bt = [P, E0, NC]
            dve.tensor_tensor(ex, lg, lmax.unsqueeze(2).broadcast_to(bc), ALU.subtract).then_inc(lsub, 1)
            link(dve.tensor_tensor(hit, lg, lmax.unsqueeze(2).broadcast_to(bc), ALU.is_equal))
            link(dve.tensor_tensor(hit, hit, rev8[:, :].unsqueeze(1).broadcast_to(bc), ALU.mult))
            link(dve.tensor_reduce(top, hit, AXX, ALU.max))
            link(dve.tensor_tensor(oh, top.unsqueeze(1).broadcast_to(bt), rev8[:, :].unsqueeze(2).broadcast_to(bt), ALU.is_equal))
            dve.wait_ge(lexp, 1)
            link(dve.tensor_reduce(esum, ex, AXX, ALU.add))
            link(dve.reciprocal(prob, esum))
            link(dve.tensor_tensor(pe_key, oh, prob.unsqueeze(1).broadcast_to(bt), ALU.mult))
            link(dve.memset(thr[:, :], THR0))
            link(dve.memset(bit[:, :], 1 << (NSTEP - 1)))
            base, per = steps[0], 6
            with dve.Fori(0, NSTEP) as r:
                at = [0]

                def chain(ins):
                    at[0] += 1
                    ins.then_inc(dch, 1)
                    hold(dve, dch, base + per * r + at[0])

                chain(dve.tensor_tensor(cand[:, :], thr[:, :], bit[:, :], ALU.bitwise_or))
                chain(dve.tensor_tensor(cmp_s, pe_key, cand[:, :].bitcast(F32).unsqueeze(2).broadcast_to(bt), ALU.is_ge))
                dve.tensor_reduce(part, cmp_s, AXX, ALU.add).then_inc(cpart, 1)
                hold(dve, csum, r + 1)
                chain(dve.tensor_scalar(part, bank[6][:, 0:E0], float(CAPACITY), None, ALU.is_ge))
                chain(dve.tensor_tensor(step_bit[:, :], part, bit[:, :], ALU.mult))
                chain(dve.tensor_tensor(thr[:, :], thr[:, :], step_bit[:, :], ALU.bitwise_or))
                chain(dve.tensor_scalar(bit[:, :], bit[:, :], 1, None, ALU.logical_shift_right))
                assert at[0] == per
            steps[0] = base + per * NSTEP
            thr_bc = thr[:, :].bitcast(F32).unsqueeze(2).broadcast_to(bt)
            link(dve.tensor_tensor(above, pe_key, thr_bc, ALU.is_gt))
            dve.tensor_tensor(tie, pe_key, thr_bc, ALU.is_equal).then_inc(tie_in, 1)
            dve.tensor_reduce(part, above, AXX, ALU.add).then_inc(cpart, 1)
            link(dve.memset(seg, 1.0))
            link(dve.memset(seg[:, :, 0:1], 0.0))

            def flat(ap):
                return ap.rearrange("p e c -> p (e c)")

            def ranks(n):
                dve.wait_ge(tie_ps, n)
                w = E0 * NC
                link(dve.tensor_copy(flat(tot), bank[5][:, 0:w]))
                link(dve.tensor_tensor_scan(flat(run), flat(seg), flat(tot), 0.0, ALU.mult, ALU.add))
                link(dve.tensor_tensor(flat(rank), flat(run), flat(tot), ALU.subtract))
                link(dve.tensor_tensor(flat(rank), flat(rank), bank[4][:, 0:w], ALU.add))

            dve.wait_ge(csum, NSTEP + 1)
            link(dve.tensor_scalar(budget, bank[6][:, 0:E0], -1.0, float(CAPACITY), ALU.mult, ALU.add))
            ranks(1)
            link(dve.tensor_tensor(rank, rank, budget.unsqueeze(2).broadcast_to(bt), ALU.is_lt))
            link(dve.tensor_tensor(rank, rank, tie, ALU.mult))
            link(dve.tensor_tensor(fin, above, rank, ALU.add))
            link(dve.tensor_reduce(kept, fin[:, 1:E0, :].rearrange("p e c -> p c e"), AXX, ALU.add))
            link(dve.tensor_scalar(fin[:, 0, :], kept, -1.0, 1.0, ALU.mult, ALU.add))
            dve.sem_inc(tie_in, 1)
            ranks(2)
            link(dve.tensor_scalar(cnt_i[:, :], run[:, :, NC - 1], float(P - 1), None, ALU.add))
            link(dve.tensor_scalar(cnt_i[:, :], cnt_i[:, :], 7, None, ALU.logical_shift_right))
            link(dve.tensor_copy(ntile, cnt_i[:, :]))
            link(dve.tensor_tensor_scan(tcum, ones[:, 0:E0], ntile, 0.0, ALU.mult, ALU.add))
            link(dve.tensor_tensor(tstart, tcum, ntile, ALU.subtract))
            link(dve.tensor_scalar(tcum, tstart, float(P), None, ALU.mult))
            link(dve.tensor_tensor(rank, rank, tcum.unsqueeze(2).broadcast_to(bt), ALU.add))
            link(dve.tensor_tensor(rank, rank, fin, ALU.mult))
            link(dve.tensor_reduce(pos, rank.rearrange("p e c -> p c e"), AXX, ALU.add))
            link(dve.tensor_copy(pos_i[:, :], pos))
            link(dve.tensor_scalar(hi_i[:, :], pos_i[:, :], 7, None, ALU.logical_shift_right))
            link(dve.tensor_copy(hi, hi_i[:, :]))
            link(dve.scalar_tensor_tensor(lo, hi, -float(P), pos, ALU.mult, ALU.add))
            bx = [P, TILES, E0 - 1]
            link(dve.tensor_tensor(tcmp, iota_f[:, 0:TILES].unsqueeze(2).broadcast_to(bx),
                                   tstart[:, 1:E0].unsqueeze(1).broadcast_to(bx), ALU.is_ge))
            link(dve.tensor_reduce(tile_f, tcmp, AXX, ALU.add))
            link(dve.tensor_copy(tile_e[:, :], tile_f))

            def onehots(c, u):
                col = bass.ds(c, 1)
                dve.tensor_scalar(oh_lo[u], iota_f[:, :], lo[:, col], None, ALU.is_equal)
                dve.tensor_scalar(oh_hi[u], iota_f[:, 0:TILES], hi[:, col], token_f[:, col], ALU.is_equal, ALU.mult).then_inc(onehot, 1)

            for c in range(2):
                onehots(c, c)
            with dve.Fori(1, NC // 2) as r:
                for u in range(2):
                    dve.wait_ge(tab_ps, 2 * r + u - 1)
                    onehots(2 * r + u, u)
            dve.wait_ge(tab_ps, NC)
            dve.tensor_copy(row_tok[:, :], bank[3][:, 0:TILES]).then_inc(table, 1)

            dve.wait_ge(ld_b, 32)

            def scale_rows(i):
                dve.wait_ge(g_ps, i + 1 + 2)
                for k in range(KD):
                    m = dve.tensor_scalar(g_t[:, k, :], bank[0][:, k * P:(k + 1) * P], gout[:, k:k + 1], None, ALU.mult)
                m.then_inc(g_ev, 1)

            def relu_half(j):
                e = dve.value_load(tile_e[0:1, bass.ds(j, 1)], min_val=0, max_val=E0 - 1)
                dve.wait_ge(t_ps, j + 1)
                for f in range(NF // 2, NF):
                    m = dve.tensor_scalar(act_t[:, f, :], bank[4][:, (f - 4) * P:(f - 3) * P], b1_s[:, bass.ds(e * NF + f, 1)], 0.0,
                                          ALU.add, ALU.max)
                m.then_inc(t_evd, 1)
                return e

            scale_rows(0)
            with dve.Fori(0, (TILES - 1) // 2) as r:
                for v in range(2):
                    i = 1 + 2 * r + v
                    scale_rows(i)
                    e = relu_half(i - 1)
                    dve.wait_ge(dn_ps, i)
                    dve.wait_ge(y_st[v], 16 * r + 16)
                    dve.tensor_tensor(y_s[v], bank[5 + v][:, 0:D], b2_s[:, bass.ds(e, 1), :].rearrange("p a d -> p (a d)"),
                                      ALU.add).then_inc(dn_ev, 1)
            e = relu_half(TILES - 1)
            dve.wait_ge(dn_ps, TILES)
            dve.wait_ge(y_st[0], 16 * (TILES // 2) + 16)
            dve.tensor_tensor(y_s[0], bank[5][:, 0:D], b2_s[:, bass.ds(e, 1), :].rearrange("p a d -> p (a d)"), ALU.add).then_inc(dn_ev, 1)

            dve.wait_ge(ld_v, 16 * 13)
            dve.wait_ge(y_st[0], 16 * ((TILES + 1) // 2) + 16)
            bo = [64, B, E1]
            dve.tensor_tensor(cgo[0:64], cond_s.unsqueeze(2).broadcast_to(bo), wg_s.unsqueeze(1).broadcast_to(bo), ALU.mult).then_inc(cb, 1)
            dve.wait_ge(cg_ps, 1)
            dve.tensor_copy(cg.rearrange("p b e -> p (b e)"), bank[7][:, 0:B * E1]).then_inc(cg_ev, 1)
            dve.wait_ge(cg_ev, 1)
            dve.wait_ge(ld_again, 16)
            NQ = NSH + E1
            PERB = 18
            with dve.Fori(0, B) as b:
                at2 = [0]

                def clink(ins):
                    at2[0] += 1
                    ins.then_inc(gch, 1)
                    hold(dve, gch, PERB * b + at2[0])

                hold(dve, x1_ps, b + 1)
                for n in range(NB):
                    row = tokens[:, bass.ds(b * NB + n, 1), :].rearrange("p a d -> p (a d)")
                    hold(dve, got2[n], 16 * b + 16)
                    dve.tensor_tensor(x1_s[:, n, :], row, yg[n], ALU.add).then_inc(zch, 1)
                    hold(dve, zch, NB * b + n + 1)
                    dve.tensor_copy(row, x1_s[:, n, :]).then_inc(x1, 1)
                bg = [P, NB, E1]
                dve.wait_ge(rl_ps, b + 1)
                clink(dve.tensor_tensor(glog, bank[1][:, 0:NB * E1].rearrange("p (n e) -> p n e", n=NB),
                                        cg[:, bass.ds(b, 1), :].broadcast_to(bg), ALU.add))
                clink(dve.tensor_reduce(gnm, glog, AXX, ALU.max))
                dve.tensor_tensor(gex, glog, gnm.unsqueeze(2).broadcast_to(bg), ALU.subtract).then_inc(rl_sub, 1)
                hold(dve, rl_exp, b + 1)
                clink(dve.tensor_reduce(gsum, gex, AXX, ALU.add))
                clink(dve.reciprocal(grec, gsum))
                clink(dve.tensor_tensor(gsc, gex, grec.unsqueeze(2).broadcast_to(bg), ALU.mult))
                for n in range(NB):
                    clink(dve.max(gtop[:, n, :], gsc[:, n, :]))
                for n in range(NB):
                    clink(dve.max_index(top_i[:, n, :], gtop[:, n, :], gsc[:, n, :]))
                clink(dve.tensor_copy(gidx_f, top_i[:, :, :]))
                clink(dve.scalar_tensor_tensor(gwsum, gtop[:, :, 0], 1e-20, gtop[:, :, 1], ALU.add, ALU.add))
                clink(dve.reciprocal(grec, gwsum))
                clink(dve.tensor_tensor(gw2, gtop[:, :, 0:2], grec.unsqueeze(2).broadcast_to([P, NB, 2]), ALU.mult))
                io = iota_f[:, 0:E1].unsqueeze(1).broadcast_to(bg)
                for k, dst in enumerate((gone, gtwo)):
                    clink(dve.tensor_tensor(dst, io, gidx_f[:, :, k:k + 1].broadcast_to(bg), ALU.is_equal))
                    clink(dve.tensor_tensor(dst, dst, gw2[:, :, k:k + 1].broadcast_to(bg), ALU.mult))
                clink(dve.tensor_tensor(gate, gone, gtwo, ALU.add))

                def product(q):
                    dve.wait_ge(lk, NQ * b + q + 1)
                    if q >= NSH:
                        hold(dve, d_ps, (1 + E1) * b + (1 if q < 2 * NSH else q - NSH))
                    dve.scalar_tensor_tensor(mid[q % 2], leak[q % 2], 0.01, leak[q % 2], ALU.mult, ALU.max).then_inc(leaked, 1)
                    dve.wait_ge(leaked, NQ * b + q + 1)
                    dve.tensor_tensor(mid[q % 2], mid[q % 2], bank[2 + q % 2][:, S:2 * S], ALU.mult).then_inc(md, 1)

                def add_expert(q):
                    e = q - NSH
                    dve.wait_ge(d_ps, (1 + E1) * b + 2 + e)
                    dve.wait_ge(d_acc, (1 + E1) * b + 1 + e + 2)
                    for n in range(NB):
                        m = dve.scalar_tensor_tensor(acc[:, n, :], bank[4 + (1 + e) % 2][:, n * D:(n + 1) * D], gate[:, n, e:e + 1],
                                                     acc[:, n, :], ALU.mult, ALU.add)
                    m.then_inc(d_acc, 1)

                product(0)
                product(1)
                dve.wait_ge(d_ps, (1 + E1) * b + 1)
                dve.wait_ge(z_ps, b + 1)
                dve.tensor_copy(acc.rearrange("p n d -> p (n d)"), bank[4]).then_inc(d_acc, 1)
                product(2)
                for q in range(NSH, NQ):
                    if q + 1 < NQ:
                        product(q + 1)
                    add_expert(q)
                dve.wait_ge(d_acc, (1 + E1) * (b + 1) + 2)
                dve.sem_inc(yfin, 1)
                hold(dve, z_ev, b + 2)
                dve.tensor_reduce(pooled[:, :, bass.ds(b, 1)].rearrange("p k a -> p (k a)"),
                                  bank[6].rearrange("p (k t) -> p k t", k=KD), AXX, ALU.add).then_inc(pool_r, 1)
                PERB_seen = at2[0]
            assert PERB_seen == PERB, PERB_seen

            fs = [0]

            def flink(ins):
                fs[0] += 1
                ins.then_inc(fch, 1)
                dve.wait_ge(fch, fs[0])

            dve.wait_ge(fl_ps, 1)
            flink(dve.scalar_tensor_tensor(flog, bank[1][0:B, 0:E2], 1.0 / S, gb_s, ALU.mult, ALU.add))
            flink(dve.max(ftop, flog))
            dve.tensor_scalar(fnm, ftop[:, 0:1], -1.0, None, ALU.mult).then_inc(fl_sub, 1)
            flink(dve.tensor_scalar(fkeep, flog, ftop[:, 1:2], None, ALU.is_ge))
            dve.wait_ge(fl_exp, 1)
            flink(dve.tensor_tensor(fex, fex, fkeep, ALU.mult))
            flink(dve.tensor_reduce(fsum, fex, AXX, ALU.add))
            flink(dve.reciprocal(fsum, fsum))
            flink(dve.tensor_scalar(fgate, fex, fsum[:, 0:1], None, ALU.mult))
            bd = [B, B, E2]
            dve.tensor_tensor(fdiag, fgate.unsqueeze(1).broadcast_to(bd), ident[0:B, 0:B].unsqueeze(2).broadcast_to(bd),
                              ALU.mult).then_inc(fdg, 1)
            dve.wait_ge(fg_ps, 1)
            flink(dve.tensor_copy(fg_bc.rearrange("p b e -> p (b e)"), bank[7][:, 0:B * E2]))
            NE = E2 * KD
            with dve.Fori(0, B // 2) as r:
                hold(dve, r_ps, r + 1)
                for e in range(E2):
                    for oc in range(KD):
                        q = e * KD + oc
                        hold(dve, e_act, NE * r + q + 1 + 2)
                        if e:
                            hold(dve, e_acc, NE * r + q - KD + 1 + 2)
                        for half in range(2):
                            o = accf[:, oc, half * S:(half + 1) * S]
                            src = ge[q % 2][:, half * S:(half + 1) * S]
                            w = fg_bc[:, bass.ds(2 * r + half, 1), e]
                            m = (dve.scalar_tensor_tensor(o, src, w, o, ALU.mult, ALU.add) if e else
                                 dve.tensor_scalar(o, src, w, None, ALU.mult))
                        m.then_inc(e_acc, 1)
                dve.wait_ge(r_ps, r + 2)
                dve.wait_ge(stored, 16 * r + 16)
                for n in range(2):
                    m = dve.tensor_tensor(res[:, 2 * n:2 * n + 2, :], bank[4 + n].rearrange("p (a d) -> p a d", a=2),
                                          tokens[:, bass.ds(r * 2 * NB + 2 * n, 2), :], ALU.add)
                m.then_inc(r_ev, 1)


def kernel(**inputs):
    import concourse.bacc as bacc
    from concourse import mybir
    from concourse.bass_utils import run_bass_kernel_spmd

    def chunks(a, p=128):
        return a.reshape(a.shape[0] // p, p, -1).transpose(1, 0, 2)

    i = {k: np.asarray(v) for k, v in inputs.items()}
    laid = {
        "x": i["x"].reshape(4096, 256),
        "side": i["fside_16xSxS_0"],
        "cond_t": i["cond_64"].T,
        "null_kv": i["cond_64"][0:2],
        "mask": i["mask_BxS_bk0"].reshape(1, 4096),
        "g_in": i["L0_cond_g_in"].reshape(2, 128).T,
        "null_bias": i["L0_cond_null_attn_bias"],
        "wq": i["L0_cond_Wq"], "wkv": i["L0_cond_Wkv"], "wo": i["L0_cond_Wo"],
        "router_t": i["L0_ffn_router_w"].T,
        "w1": i["L0_ffn_W1"].reshape(8, 2, 128, 1024).transpose(2, 0, 1, 3).reshape(128, -1),
        "b1": i["L0_ffn_b1"].reshape(64, 128).T,
        "w2": i["L0_ffn_W2"].reshape(8, 8, 128, 256).transpose(2, 0, 1, 3).reshape(128, -1),
        "b2": i["L0_ffn_b2"],
        "wt_t": i["L1_cond_wt"].T, "wg_t": i["L1_cond_wg"].T,
        "moe_gate": chunks(i["L1_cond_w_gate"].transpose(1, 0, 2).reshape(256, 1024)),
        "moe_up": chunks(i["L1_cond_w_up"].transpose(1, 0, 2).reshape(256, 1024)),
        "moe_down": i["L1_cond_w_down"],
        "sw_gate": i["L1_cond_sw_gate"], "sw_up": i["L1_cond_sw_up"], "sw_down": i["L1_cond_sw_down"],
        "gate_w_t": i["L1_ffn_gate_w"].T, "gate_b": i["L1_ffn_gate_b"],
        "expert_w_t": i["L1_ffn_expert_w"].transpose(2, 0, 1).reshape(2, 128, 8, 256).transpose(1, 0, 2, 3),
        "expert_b_t": i["L1_ffn_expert_b"].reshape(8, 2, 128).transpose(2, 1, 0),
        "g_out": i["L0_cond_g_out"].reshape(2, 128).T,
    }
    nc = bacc.Bacc("TRN2", target_bir_lowering=False, num_devices=1)
    arrays, aps = {}, {}
    for name, a in laid.items():
        arrays[name] = np.ascontiguousarray(a)
        aps[name] = nc.dram_tensor(name, arrays[name].shape, mybir.dt.from_np(arrays[name].dtype), kind="ExternalInput").ap()
    aps["out"] = nc.dram_tensor("out", (4096, 256), mybir.dt.float32, kind="ExternalOutput").ap()
    bass_adaln_ffn_kernel(nc, **aps)
    r = run_bass_kernel_spmd(nc, [arrays], core_ids=[0])
    return r.results[0]["out"].reshape(16, 256, 256)
```

```python
import numpy as np


def bass_adaln_ffn_kernel(
    nc, x, side, cond_t, null_kv, mask, g_in, null_bias, wq, wkv, wo, router_t,
    w1, b1, w2, b2, wt_t, wg_t, moe_gate, moe_up, moe_down, sw_gate, sw_up, sw_down,
    gate_w_t, gate_b, expert_w_t, expert_b_t, g_out, out,
):
    from contextlib import ExitStack
    import concourse.bass as bass
    from concourse import mybir

    F32 = mybir.dt.float32
    BF16 = mybir.dt.bfloat16
    I32 = mybir.dt.int32
    U8 = mybir.dt.uint8
    ALU = mybir.AluOpType
    ACT = mybir.ActivationFunctionType
    AXX = mybir.AxisListType.X

    P = 128
    B, S, D = 16, 256, 256
    KD = D // P
    NB = S // P
    T = B * S
    NC = T // P
    H, DH = 16, 64
    INNER = H * DH
    NPAIR = H // 2
    W0, W1C = 1 + P, 1 + S
    SW = W0 + W1C
    EPS = 1e-5
    BIG = float(2.0 ** 100)
    QL = S // 4
    KEY0 = S - QL
    LW = QL + 1
    NTW = B // 2
    E0, FF = 8, 1024
    NF = FF // P
    CAPACITY = int(np.ceil(T / E0 * 1.25))
    TILES = (T + E0 * (P - 1)) // P
    TILES_L = (B * QL + E0 + E0 * (P - 1)) // P
    E1, M1 = 8, 128
    NSH = 2
    E2 = 8

    ctx = ExitStack()
    with ctx:
        def sb(name, shape, dt=F32):
            return ctx.enter_context(nc.sbuf_tensor(name, shape, dt))

        def sem(name):
            return ctx.enter_context(nc.semaphore(name))

        psum = ctx.enter_context(nc.psum_tensor("psum", [P, 8, 512], F32))
        bank = [psum[:, k, :] for k in range(8)]
        tokens = sb("tokens", [P, NC, D])
        big_w = sb("big_w", [P, E0 * KD * FF])
        arena = sb("arena", [P, 23216])

        class Arena:
            def __init__(self, base):
                self.base, self.at = base, 0

            def take(self, *shape, rows=P):
                n = int(np.prod(shape))
                ap = self.base[0:rows, self.at:self.at + n]
                self.at += n
                assert self.at <= self.base.shape[1], self.at
                if len(shape) == 2:
                    ap = ap.rearrange("p (a b) -> p a b", b=shape[1])
                if len(shape) == 3:
                    ap = ap.rearrange("p (a b c) -> p a b c", b=shape[1], c=shape[2])
                return ap

        ident = sb("ident", [P, P])
        ones = sb("ones", [P, P])
        before = sb("before", [P, P])
        iota_i = sb("iota_i", [P, P], I32)
        iota_f = sb("iota_f", [P, P])
        token_i = sb("token_i", [P, NC], I32)
        rev8 = sb("rev8", [P, 8])
        ones_bf = sb("ones_bf", [1, P], BF16)
        penalty = sb("penalty", [1, B, SW], BF16)
        eps_col = sb("eps_col", [P, 1])
        gin = sb("gin", [P, KD])
        gout = sb("gout", [P, KD])
        nb_bc = sb("nb_bc", [P, H])
        xstat = sb("xstat", [P, NC, 6])
        xmv = sb("xmv", [P, NC, 2])
        rstd = sb("rstd", [P, NC])
        shift = sb("shift", [P, NC])
        ostat = sb("ostat", [P, NC, 6])
        router = sb("router", [P, KD, E0])

        A = Arena(arena)
        wq_s = A.take(KD, INNER)
        wkv_r = A.take(KD, 2 * DH)
        wk_s = A.take(KD, P)
        wv_s = A.take(KD, DH)
        wo_s = A.take(NPAIR, D)
        nk_col = sb("nk_col", [P, 1])
        nv_col = sb("nv_col", [P, 1])
        early_f = sb("early_f", [1, 1])
        early_i = sb("early_i", [1, 1], I32)
        L = Arena(arena)
        L.at = A.at
        bias = A.take(H, SW)
        xn = A.take(NB, D)
        xn_t = A.take(KD, 1 + S)
        q_t = A.take(NPAIR, S)
        k_t = A.take(1 + S)
        v_s = A.take(NB, DH)
        v_last = A.take(NB, DH)
        null_v = A.take(DH)
        e_first = A.take(P)
        NSIM, NPR, NPN, NPT = 4, 2, 4, 4
        sim = A.take(NSIM, SW)
        pr = A.take(NPR, SW)
        pn = A.take(NPN, SW)
        p_t = A.take(NPT, 3 * P)
        p_last = A.take(NB, 2, NPAIR)
        nmax = A.take(NSIM, 2)
        psum_row = A.take(NPR, 2)
        rinv = A.take(NPR, 2)
        at_t = A.take(NPAIR, S)
        mask_u8 = A.take(B * S // 4, rows=1).bitcast(U8)

        bias_l = L.take(NPAIR, LW)
        x_l = L.take(NTW, D)
        o_l = L.take(NTW + 1, D)
        h_l = L.take(NTW + 1, D)
        xn_l = L.take(D)
        xt_l = L.take(KD, P)
        q_l = L.take(NPAIR, P)
        k_l = L.take(2, LW)
        v_l = L.take(2, DH)
        sim_l = [L.take(NPAIR, LW) for _ in range(2)]
        ex_l = [L.take(NPAIR, LW) for _ in range(2)]
        pt_l = [L.take(NPAIR * P) for _ in range(2)]
        at_l = L.take(NPAIR, P)
        at_null = L.take(P)
        nm_l = [L.take(NPAIR) for _ in range(2)]
        rs_l = [L.take(NPAIR) for _ in range(2)]
        st_l = L.take(NTW + 1, 6)
        mv_l = L.take(NTW + 1, 2)
        rstd_l = L.take(NTW + 1)
        ht_l = tokens[:, 0:NTW + 1, :]
        pen_l = penalty[:, :, :].rearrange("p b c -> p (b c)")[:, 0:B * LW].rearrange("p (b c) -> p b c", c=LW)

        R = Arena(arena[:, E0 * NF * D:])
        omv = R.take(NC, 2)
        r_rstd = R.take(NC)
        h_n = [R.take(D) for _ in range(4)]
        h_t = [R.take(KD, P) for _ in range(2)]
        lg = R.take(NC, E0)
        lmax = R.take(NC)
        ex = R.take(NC, E0)
        esum = R.take(NC)
        prob = R.take(NC)
        hit = R.take(NC, E0)
        top = R.take(NC)
        oh = R.take(E0, NC)
        pe_key = R.take(E0, NC)
        thr = sb("thr", [P, E0], I32)
        cand = sb("cand", [P, E0], I32)
        bit = sb("bit", [P, E0], I32)
        step_bit = sb("step_bit", [P, E0], I32)
        cmp_s = hit.rearrange("p c e -> p (c e)").rearrange("p (e c) -> p e c", e=E0)
        part = R.take(E0)
        above = R.take(E0, NC)
        tie = R.take(E0, NC)
        budget = R.take(E0)
        tot = R.take(E0, NC)
        seg = R.take(E0, NC)
        run = R.take(E0, NC)
        rank = R.take(E0, NC)
        fin = R.take(E0, NC)
        kept = R.take(NC)
        cnt_i = sb("cnt_i", [P, E0], I32)
        ntile = R.take(E0)
        tcum = R.take(E0)
        tstart = R.take(E0)
        pos = R.take(NC)
        slot = sb("slot", [P, NC])
        reserved = sb("reserved", [P, 1])
        token_s = sb("token_s", [P, NC])
        pos_i = sb("pos_i", [P, NC], I32)
        hi_i = sb("hi_i", [P, NC], I32)
        hi = R.take(NC)
        lo = R.take(NC)
        NTC = 8
        oh_lo = R.take(NTC, P)
        oh_hi = R.take(NTC, TILES)
        tcmp = R.take(TILES, E0 - 1)
        tile_f = R.take(TILES)
        tile_e = sb("tile_e", [P, TILES], I32)
        row_tok = sb("row_tok", [P, TILES], I32)

        G = Arena(arena)
        w2_s = G.take(E0, NF, D)
        b1_s = G.take(E0 * NF)
        b2_s = G.take(E0, D)
        gath = [G.take(D) for _ in range(2)]
        g_t = G.take(KD, P)
        act1 = [G.take(FF) for _ in range(2)]
        act_t = G.take(NF, P)
        y_s = [G.take(D) for _ in range(2)]
        w1_s = big_w[:, :].rearrange("p (e k f) -> p e k f", e=E0, k=KD)
        gidx = [sb(f"gidx{k}", [P, 1], I32) for k in range(2)]

        V = Arena(big_w)
        wt_s = V.take(KD, E1)
        wg_s = V.take(E1, rows=64)
        cond_s = V.take(B, rows=64)
        cond_bc = V.take(P, rows=64)
        mg_s = V.take(KD, (E1 + NSH) * M1)
        mu_s = V.take(KD, (E1 + NSH) * M1)
        md_s = V.take(E1 + NSH, D)
        ew_s = V.take(KD, E2, D)
        gw_s = V.take(KD, E2)
        gb_s = V.take(E2, rows=B)
        eb_s = V.take(KD, E2)
        N = Arena(arena)
        yg = [N.take(D) for _ in range(2)]
        x1_s = N.take(NB, D)
        x1_t = N.take(KD, S)
        cgo = N.take(B, E1)
        leak = [N.take(S) for _ in range(2)]
        mid = [N.take(S) for _ in range(2)]
        acc = N.take(NB, D)
        z_t = N.take(KD, T)
        pooled = N.take(KD, B)
        cg = N.take(B, E1)
        glog = N.take(NB, E1)
        gtop = N.take(NB, 8)
        gex = N.take(NB, E1)
        gsum = N.take(NB)
        grec = N.take(NB)
        gsc = N.take(NB, E1)
        gwsum = N.take(NB)
        gidx_f = N.take(NB, 8)
        gw2 = N.take(NB, 2)
        gone = N.take(NB, E1)
        gtwo = N.take(NB, E1)
        gate = N.take(NB, E1)
        gnm = N.take(NB)
        top_i = sb("top_i", [P, NB, 8], mybir.dt.uint32)
        flog = N.take(E2, rows=B)
        ftop = N.take(8, rows=B)
        fex = N.take(E2, rows=B)
        fnm = N.take(1, rows=B)
        fsum = N.take(1, rows=B)
        fkeep = N.take(E2, rows=B)
        fgate = N.take(E2, rows=B)
        fdiag = N.take(B, E2, rows=B)
        fg_bc = N.take(B, E2)
        ge = [N.take(2 * S) for _ in range(2)]
        accf = N.take(KD, 2 * S)
        res = N.take(2 * NB, D)

        h_dram = nc.dram_tensor("h_sorted_from", [T, D], F32, kind="Internal").ap()
        h_late = nc.dram_tensor("h_late", [1 + B * QL, D], F32, kind="Internal").ap()
        y_late = nc.dram_tensor("y_late", [TILES_L * P, D], F32, kind="Internal").ap()
        y_dram = nc.dram_tensor("y_sorted", [TILES * P, D], F32, kind="Internal").ap()

        ld_x = [sem(f"ld_x{k}") for k in range(4)]
        ld_w = sem("ld_w")
        ld_bias = sem("ld_bias")
        ld_mask = sem("ld_mask")
        ld_w1 = sem("ld_w1")
        ld_w2 = sem("ld_w2")
        ld_b = sem("ld_b")
        ld_v = sem("ld_v")
        ld_again = sem("ld_again")
        const = sem("const")
        gconst = sem("gconst")
        early = sem("early")
        lflag = sem("lflag")
        gsetup = sem("gsetup")
        gch0 = sem("gch0")
        ld_l = sem("ld_l")
        lconst = sem("lconst")
        slots = sem("slots")
        lsetup = sem("lsetup")
        lvar = sem("lvar")
        lsd = sem("lsd")
        l_dv = sem("l_dv")
        l_xn = sem("l_xn")
        l_x = sem("l_x")
        l_xc = sem("l_xc")
        l_kv = sem("l_kv")
        l_kc = sem("l_kc")
        l_vc = sem("l_vc")
        l_q = sem("l_q")
        l_qc = sem("l_qc")
        l_s = sem("l_s")
        l_sub = sem("l_sub")
        l_e = sem("l_e")
        l_p = sem("l_p")
        l_t = sem("l_t")
        l_tc = sem("l_tc")
        l_pv = sem("l_pv")
        l_ac = sem("l_ac")
        l_o = sem("l_o")
        l_oc = sem("l_oc")
        lovar = sem("lovar")
        losd = sem("losd")
        l_h = sem("l_h")
        l_ht = sem("l_ht")
        l_htc = sem("l_htc")
        l_lg = sem("l_lg")
        l_hs = sem("l_hs")
        setup = sem("setup")
        ready = sem("ready")
        xvar = sem("xvar")
        xsd = sem("xsd")
        xnorm = sem("xnorm")
        x_ps = sem("x_ps")
        x_ev = sem("x_ev")
        k_ps = sem("k_ps")
        k_ev = sem("k_ev")
        q_ps = sem("q_ps")
        q_ev = sem("q_ev")
        v_ps = sem("v_ps")
        v_ev = sem("v_ev")
        scores = sem("scores")
        simmed = sem("simmed")
        exped = sem("exped")
        recip = sem("recip")
        normed = sem("normed")
        turned = sem("turned")
        pt_ev = sem("pt_ev")
        pv = sem("pv")
        at_ev = sem("at_ev")
        last_ps = sem("last_ps")
        at_done = sem("at_done")
        o_ps = sem("o_ps")
        o_ev = sem("o_ev")
        o_bn = sem("o_bn")
        dch = sem("dch")
        ovar = sem("ovar")
        osd = sem("osd")
        hnorm = sem("hnorm")
        h_ps = sem("h_ps")
        h_ev = sem("h_ev")
        h_st = [sem(f"h_st{k}") for k in range(4)]
        lg_ps = sem("lg_ps")
        lsub = sem("lsub")
        lexp = sem("lexp")
        cpart = sem("cpart")
        csum = sem("csum")
        tie_in = sem("tie_in")
        tie_ps = sem("tie_ps")
        onehot = sem("onehot")
        tab_ps = sem("tab_ps")
        table = sem("table")
        idx_ok = sem("idx_ok")
        got = [sem(f"got{k}") for k in range(2)]
        g_ps = sem("g_ps")
        g_ev = sem("g_ev")
        up_ps = sem("up_ps")
        up_ev = sem("up_ev")
        t_ps = sem("t_ps")
        t_eva = sem("t_eva")
        t_evd = sem("t_evd")
        dn_ps = sem("dn_ps")
        dn_ev = sem("dn_ev")
        y_st = [sem(f"y_st{k}") for k in range(2)]
        ffn_done = sem("ffn_done")
        bch = sem("bch")
        sch = sem("sch")
        tch = sem("tch")
        gch = sem("gch")
        zch = sem("zch")
        fch = sem("fch")
        cb = sem("cb")
        cg_ps = sem("cg_ps")
        cg_ev = sem("cg_ev")
        idx2 = sem("idx2")
        got2 = [sem(f"got2{k}") for k in range(2)]
        x1 = sem("x1")
        x1_ps = sem("x1_ps")
        x1_ev = sem("x1_ev")
        rl_ps = sem("rl_ps")
        rl_sub = sem("rl_sub")
        rl_exp = sem("rl_exp")
        gu_ps = sem("gu_ps")
        lk = sem("lk")
        md = sem("md")
        d_ps = sem("d_ps")
        d_acc = sem("d_acc")
        yfin = sem("yfin")
        z_ps = sem("z_ps")
        z_ev = sem("z_ev")
        pool_r = sem("pool_r")
        fl_ps = sem("fl_ps")
        fl_sub = sem("fl_sub")
        fl_exp = sem("fl_exp")
        fdg = sem("fdg")
        fg_ps = sem("fg_ps")
        fg_ok = sem("fg_ok")
        e_ps = sem("e_ps")
        e_act = sem("e_act")
        e_acc = sem("e_acc")
        r_ps = sem("r_ps")
        r_ev = sem("r_ev")
        stored = sem("stored")
        held = sem("held")
        leaked = sem("leaked")

        def hold(eng, s, value):
            eng.wait_ge(s, value)
            eng.sem_inc(held)

        NSPB = 2
        NSTEP = 26
        THR0 = 0x3C000000

        NSETUP = 8
        NGSETUP = 6
        NCONST = 8
        NGCONST = 7
        NLD = 11

        def branch(eng):
            eng.wait_ge(early, 1)
            return eng.value_load(early_i[0:1, 0:1], min_val=0, max_val=1) == 1
        S_FREE, T_FREE, PV_FREE = 2, 2, 2

        block = ctx.enter_context(nc.Block())

        @block.sync
        def _(sp):
            for s in h_st + y_st + [stored]:
                sp.sem_inc(s, 16)
            xr = x.rearrange("(c p) d -> p c d", p=P)
            late_x = x.rearrange("(c t s) d -> t s c d", t=2, s=S)
            late_side = side.rearrange("(j t) q k -> t q j k", t=2)
            sp.dma_start(mask_u8, mask).then_inc(ld_mask, 16)
            for t in range(2):
                sp.dma_start(x_l[t * QL:(t + 1) * QL, :, :], late_x[t, KEY0:S, :, :]).then_inc(ld_x[0], 16)
            for dst, src in (
                (gin[:, :], g_in), (wkv_r, wkv.rearrange("(k p) n -> p k n", p=P)),
                (wq_s, wq.rearrange("(k p) n -> p k n", p=P)), (nb_bc[:, :], null_bias.partition_broadcast(P)),
                (nk_col[0:DH, :], null_kv[0:1, :].rearrange("a d -> d a")),
                (nk_col[DH:P, :], null_kv[0:1, :].rearrange("a d -> d a")),
                (nv_col[0:DH, :], null_kv[1:2, :].rearrange("a d -> d a")),
                (nv_col[DH:P, :], null_kv[1:2, :].rearrange("a d -> d a")),
                (gout[:, :], g_out), (router[:, :, :], router_t.rearrange("(k p) e -> p k e", p=P)),
                (wo_s, wo.rearrange("(j p) n -> p j n", p=P)),
            ):
                sp.dma_start(dst, src).then_inc(ld_w, 16)
            general = branch(sp)

            with sp.If(general):
                sp.wait_ge(ld_x[0], 32)
                for k in range(4):
                    n = NC // 4
                    sp.dma_start(tokens[:, k * n:(k + 1) * n, :], xr[:, k * n:(k + 1) * n, :]).then_inc(ld_x[k], 16)
                sp.dma_start(null_v[0:1, :], null_kv[1:2, :]).then_inc(ld_bias, 16)
                sp.dma_start(bias[:, :, 1:W0], side[:, 0:P, 0:P].rearrange("h q k -> q h k")).then_inc(ld_bias, 16)
                sp.dma_start(bias[:, :, W0 + 1:SW], side[:, P:S, :].rearrange("h q k -> q h k")).then_inc(ld_bias, 16)
                sp.dma_start(big_w[:, :], w1).then_inc(ld_w1, 16)
                sp.wait_ge(o_ps, B)
                sp.dma_start(w2_s, w2.rearrange("p (e k d) -> p e k d", e=E0, k=NF)).then_inc(ld_w2, 16)
                with sp.Fori(0, NC // 4) as r:
                    for u in range(4):
                        sp.wait_ge(hnorm, 4 * r + u + 1)
                        sp.dma_start(h_dram[bass.ds((4 * r + u) * P, P), :], h_n[u]).then_inc(h_st[u], 16)
                sp.dma_start(tokens[:, :, :], xr).then_inc(ld_again, 16)
            with sp.Else():
                for t in range(2):
                    rows = slice(t * QL, (t + 1) * QL)
                    sp.dma_start(bias_l[rows, :, 0:QL], late_side[t, KEY0:S, :, KEY0:S]).then_inc(ld_l, 16)
                    sp.dma_start(v_l[QL:LW, t, :], null_kv[1:2, :]).then_inc(ld_l, 16)
                sp.dma_start(big_w[:, :], w1).then_inc(ld_w1, 16)
                sp.wait_ge(l_h, NTW + 1)
                sp.dma_start(h_late[0:1, :], h_l[0:1, NTW, :]).then_inc(l_hs, 16)
                sp.dma_start(h_late[1:, :].rearrange("(c p) d -> p c d", p=P), h_l[:, 0:NTW, :]).then_inc(l_hs, 16)
                sp.wait_ge(l_lg, 1)
                sp.wait_ge(l_hs, 32)
                sp.dma_start(w2_s, w2.rearrange("p (e k d) -> p e k d", e=E0, k=NF)).then_inc(ld_w2, 16)
                sp.dma_start(tokens[:, :, :], xr).then_inc(ld_again, 16)
            sp.wait_ge(table, 1)
            sp.dma_start(b1_s, b1).then_inc(ld_b, 16)
            sp.dma_start(b2_s, b2.rearrange("e d -> (e d)").partition_broadcast(P)
                         .rearrange("p (e d) -> p e d", e=E0)).then_inc(ld_b, 16)

            def store_tiles(tiles, rows):
                def store_tile(i, u):
                    sp.wait_ge(dn_ev, i + 1 + 2)
                    sp.dma_start(rows[bass.ds(i * P, P), :], y_s[u]).then_inc(y_st[u], 16)

                store_tile(0, 0)
                with sp.Fori(0, (tiles - 1) // 2) as r:
                    for v in range(2):
                        store_tile(1 + 2 * r + v, (1 + v) % 2)
                if tiles % 2 == 0:
                    store_tile(tiles - 1, 1)
                sp.wait_ge(up_ps, tiles)

            with sp.If(general):
                store_tiles(TILES, y_dram)
            with sp.Else():
                store_tiles(TILES_L, y_late)
            for dst, src in (
                (wt_s, wt_t.rearrange("(k p) e -> p k e", p=P)), (wg_s, wg_t), (cond_s, cond_t),
                (mg_s[:, :, 0:E1 * M1], moe_gate), (mg_s[:, :, E1 * M1:], sw_gate.rearrange("(k p) m -> p k m", p=P)),
                (mu_s[:, :, 0:E1 * M1], moe_up), (mu_s[:, :, E1 * M1:], sw_up.rearrange("(k p) m -> p k m", p=P)),
                (md_s[:, 0:E1, :], moe_down.rearrange("e m d -> m e d")),
                (md_s[:, E1:, :], sw_down.rearrange("(k p) d -> p k d", p=P)),
                (ew_s, expert_w_t), (gw_s, gate_w_t.rearrange("(k p) e -> p k e", p=P)),
                (gb_s, gate_b.partition_broadcast(B)), (eb_s, expert_b_t),
            ):
                sp.dma_start(dst, src).then_inc(ld_v, 16)
            outr = out.rearrange("(c p) d -> p c d", p=P)
            with sp.Fori(0, B // 2) as r:
                sp.wait_ge(r_ev, r + 2)
                sp.dma_start(outr[:, bass.ds(r * 2 * NB, 2 * NB), :], res).then_inc(stored, 16)
            sp.wait_ge(stored, 16 * (B // 2) + 16)

        @block.gpsimd
        def _(pool):
            pool.sem_inc(normed, NPR)
            pool.memset(ident[:, :], 0.0).then_inc(const, 1)
            pool.memset(ones[:, :], 1.0).then_inc(const, 1)
            pool.memset(ones_bf[:, :], 1.0).then_inc(const, 1)
            pool.memset(eps_col[:, :], EPS).then_inc(const, 1)
            pool.memset(penalty[:, :, :], 0.0).then_inc(const, 1)
            pool.iota(iota_i[:, :], [[1, P]], base=0, channel_multiplier=0).then_inc(const, 1)
            pool.wait_ge(const, 6)
            pool.affine_select(out=ident[:, :], in_=ident[:, :], compare_op=ALU.not_equal, fill=1.0, base=0,
                               pattern=[[-1, P]], channel_multiplier=1).then_inc(const, 1)
            pool.affine_select(out=before[:, :], in_=ones[:, :], compare_op=ALU.is_gt, fill=0.0, base=0,
                               pattern=[[1, P]], channel_multiplier=-1).then_inc(const, 1)
            general = branch(pool)

            def norm_head(b, s):
                g = b * H + s
                pool.wait_ge(recip, g + 1)
                hold(pool, turned, g + 1)
                if s == 0:
                    hold(pool, last_ps, b + 1)
                src, dst, ri = pr[:, s % NPR, :], pn[:, s % NPN, :], rinv[:, s % NPR, :]
                pool.tensor_tensor(p_last[:, :, s % 2, s // 2], src[:, P:SW:S + 1], ri, ALU.mult)
                pool.tensor_scalar(dst[:, 0:W0], src[:, 0:W0], ri[:, 0:1], None, ALU.mult)
                pool.tensor_scalar(dst[:, W0:SW], src[:, W0:SW], ri[:, 1:2], None, ALU.mult).then_inc(normed, 1)

            with pool.If(general):
                pool.memset(e_first[0:1, :], 0.0).then_inc(gconst, 1)
                pool.memset(xn_t[:, :, 0:1], 0.0).then_inc(gconst, 1)
                pool.memset(v_last, 0.0).then_inc(gconst, 1)
                pool.wait_ge(gconst, 3)
                pool.memset(e_first[0:1, 0:1], 1.0).then_inc(gconst, 1)
                pool.memset(slot[:, :], 1.0).then_inc(slots, 1)
                pool.iota(token_i[:, :], [[P, NC]], base=0, channel_multiplier=1).then_inc(slots, 1)
                pool.memset(reserved[:, :], 0.0).then_inc(slots, 2)
                pool.wait_ge(ld_bias, 48)
                for c0 in (1, W0 + 1 + P):
                    pool.affine_select(out=bias[:, :, c0:c0 + P], in_=bias[:, :, c0:c0 + P], compare_op=ALU.is_ge, fill=-BIG,
                                       base=0, pattern=[[0, H], [-1, P]], channel_multiplier=1).then_inc(gconst, 1)
                pool.wait_ge(gsetup, NGSETUP)
                pool.sem_inc(gconst, 1)
                with pool.Fori(0, B) as b:
                    for s in range(H):
                        norm_head(b, s)
            with pool.Else():
                pool.wait_ge(ld_l, 64)
                pool.wait_ge(const, NCONST)
                for t in range(2):
                    if t:
                        pool.wait_ge(lconst, 1)
                    rows = bias_l[t * QL:(t + 1) * QL, :, 0:QL]
                    pool.affine_select(out=rows, in_=rows, compare_op=ALU.is_ge, fill=-BIG, base=0,
                                       pattern=[[0, NPAIR], [-1, QL]], channel_multiplier=1).then_inc(lconst, 1)
                pool.wait_ge(lconst, 2)
                pool.memset(slot[:, :], 0.0).then_inc(slots, 1)
                pool.memset(reserved[:, :], 1.0).then_inc(slots, 1)
                pool.iota(token_i[:, :], [[QL // NB, NC]], base=1 - QL // NB - (P - QL), channel_multiplier=1).then_inc(slots, 1)
                pool.wait_ge(slots, 3)
                pool.memset(slot[P - QL:P, 1:NC:NB], 1.0).then_inc(slots, 1)

            def gathers(tiles, rows):
                def gather(i, u):
                    hold(pool, g_ps, i + 1)
                    pool.tensor_copy(gidx[u][:, :], row_tok[:, bass.ds(i, 1)]).then_inc(idx_ok, 1)
                    hold(pool, idx_ok, i + 1)
                    pool.indirect_dma_start(gath[u], None, rows, bass.IndirectOffsetOnAxis(ap=gidx[u][:, 0:1], axis=0)
                                            ).then_inc(got[u], 16)

                gather(0, 0)
                with pool.Fori(0, (tiles - 1) // 2) as r:
                    for v in range(2):
                        gather(1 + 2 * r + v, (1 + v) % 2)
                if tiles % 2 == 0:
                    gather(tiles - 1, 1)
                pool.wait_ge(y_st[0], 16 * ((tiles + 1) // 2) + 16)
                pool.wait_ge(y_st[1], 16 * (tiles // 2) + 16)

            pool.wait_ge(table, 1)
            with pool.If(general):
                for u in range(4):
                    pool.wait_ge(h_st[u], 16 * (NC // 4) + 16)
                gathers(TILES, h_dram)
            with pool.Else():
                pool.wait_ge(l_hs, 32)
                gathers(TILES_L, h_late)

            def expert_rows(rows):
                with pool.Fori(0, B) as b:
                    for k in range(NB):
                        hold(pool, x1, NB * b + k + 1)
                        pool.tensor_copy(gidx[k][:, :], pos_i[:, bass.ds(b * NB + k, 1)]).then_inc(idx2, 1)
                        hold(pool, idx2, NB * b + k + 1)
                        pool.indirect_dma_start(yg[k], None, rows,
                                                bass.IndirectOffsetOnAxis(ap=gidx[k][:, 0:1], axis=0)).then_inc(got2[k], 16)

            with pool.If(general):
                expert_rows(y_dram)
            with pool.Else():
                expert_rows(y_late)

        @block.tensor
        def _(pe):
            pe.sem_inc(turned, NPN)
            pe.sem_inc(pv, NPT)
            pe.sem_inc(last_ps, 1)
            pe.sem_inc(h_ps, 4)
            pe.sem_inc(lg_ps, 2)
            pe.sem_inc(g_ps, 2)
            pe.sem_inc(x1_ps, 1)
            pe.sem_inc(z_ps, 1)
            pe.sem_inc(r_ps, 1)
            b_s, b_t, b_pv, b_a, b_b = bank[0:2], bank[2:4], bank[4:6], bank[6], bank[7]

            def project_x(b, first):
                pe.wait_ge(xnorm, b + 1)
                if not first:
                    pe.wait_ge(o_ev, b)
                for k in range(KD):
                    for n in range(NB):
                        mm = pe.transpose(b_a[:, k * S + n * P:k * S + (n + 1) * P], xn[:, n, k * P:(k + 1) * P], ident[:, :])
                mm.then_inc(x_ps, 1)
                pe.wait_ge(x_ev, b + 1)
                if not first:
                    pe.wait_ge(v_ev, b)
                for k in range(KD):
                    mm = pe.matmul(b_b[:, 0:S], wk_s[:, k, :], xn_t[:, k, 1:1 + S], start=k == 0, stop=k == KD - 1)
                mm.then_inc(k_ps, 1)
                for j in range(4):
                    bk = (b_a, b_b)[j % 2]
                    if j == 1:
                        pe.wait_ge(k_ev, b + 1)
                    if j >= 2:
                        pe.wait_ge(q_ev, 4 * b + j - 1)
                    for i in range(2):
                        for k in range(KD):
                            c = (2 * j + i) * P
                            mm = pe.matmul(bk[:, i * S:(i + 1) * S], wq_s[:, k, c:c + P], xn_t[:, k, 1:1 + S],
                                           start=k == 0, stop=k == KD - 1)
                    mm.then_inc(q_ps, 1)

            def project_v(b):
                pe.wait_ge(q_ev, 4 * b + 4)
                for n in range(NB):
                    o = b_b[:, S + n * DH:S + (n + 1) * DH]
                    for k in range(KD):
                        pe.matmul(o, xn_t[:, k, n * P:(n + 1) * P], wv_s[:, k, :], start=k == 0, stop=n == 1 and k == KD - 1)
                    if n == 0:
                        pe.matmul(o, e_first[0:1, :], null_v[0:1, :], start=False, stop=True)
                for n in range(NB):
                    o = b_b[96:P, S + P + n * DH:S + P + (n + 1) * DH]
                    for k in range(KD):
                        mm = pe.matmul(o, xn_t[:, k, 97 + n * P:129 + n * P], wv_s[:, k, :], start=k == 0, stop=k == KD - 1)
                mm.then_inc(v_ps, 1)

            def qk(b, s):
                g, bk = b * H + s, b_s[s % 2]
                half = slice(DH * (s % 2), DH * (s % 2) + DH)
                if s == 0:
                    pe.wait_ge(q_ev, 4 * b + 4)
                    pe.wait_ge(k_ev, b + 1)
                hold(pe, simmed, g + 1)
                pe.matmul(bk[:, 0:SW], ones_bf[0:1, :], penalty[0:1, bass.ds(b, 1), :].rearrange("p a c -> p (a c)"),
                          start=True, stop=False)
                for c0, w, n in ((0, W0, 0), (W0, W1C, 1)):
                    mm = pe.matmul(bk[:, c0:c0 + w], q_t[half, s // 2, n * P:(n + 1) * P], k_t[half, 0:w],
                                   start=False, stop=n == NB - 1)
                mm.then_inc(scores, 1)

            def turn(b, s):
                g, bk = b * H + s, b_t[s % 2]
                pe.wait_ge(normed, g + 1 + NPR)
                pe.wait_ge(pt_ev, g + 1)
                for n, c0 in enumerate((0, W0, W0 + P)):
                    mm = pe.transpose(bk[:, n * P:(n + 1) * P], pn[:, s % NPN, c0:c0 + P], ident[:, :])
                mm.then_inc(turned, 1)

            def weigh(b, s):
                g, j = b * H + s, s // 2
                pe.wait_ge(pt_ev, g + 1 + T_FREE)
                if s == 0:
                    pe.wait_ge(v_ev, b + 1)
                if s % 4 == 0:
                    pe.wait_ge(at_ev, 4 * b + s // 4 + 1)
                o = b_pv[(s // 4) % 2][DH * (s % 2):DH * (s % 2) + DH, (j % 2) * S:(j % 2) * S + S]
                pe.matmul(o, v_s[:, 0, :], p_t[:, s % NPT, 0:S], start=True, stop=False)
                pe.matmul(o[:, P:S], v_s[:, 1, :], p_t[:, s % NPT, S:S + P], start=False, stop=True).then_inc(pv, 1)

            def last_keys(b):
                pe.wait_ge(normed, (b + 1) * H + NPR)
                pe.wait_ge(pt_ev, (b + 1) * H - 1 + T_FREE)
                for n in range(NB):
                    for hf in range(2):
                        mm = pe.matmul(b_t[0][DH * hf:DH * hf + DH, n * NPAIR:(n + 1) * NPAIR], v_last[96:P, n, :],
                                       p_last[96:P, n, hf, :], start=True, stop=True)
                mm.then_inc(last_ps, 1)

            def project_o(b):
                pe.wait_ge(at_done, b + 1)
                for n in range(NB):
                    for j in range(NPAIR):
                        mm = pe.matmul(b_a[:, n * D:(n + 1) * D], at_t[:, j, n * P:(n + 1) * P], wo_s[:, j, :],
                                       start=j == 0, stop=j == NPAIR - 1)
                mm.then_inc(o_ps, 1)

            def attend(b, more):
                for s in range(H):
                    qk(b, s)
                    if s >= 2:
                        turn(b, s - 2)
                    if s >= 3:
                        weigh(b, s - 3)
                if more:
                    project_x(b + 1, False)
                turn(b, H - 2)
                weigh(b, H - 3)
                turn(b, H - 1)
                weigh(b, H - 2)
                weigh(b, H - 1)
                last_keys(b)
                if more:
                    project_v(b + 1)
                project_o(b)

            def turn_late_x(c):
                pe.wait_ge(l_xn, c + 1)
                for k in range(KD):
                    mm = pe.transpose(bank[7][:, k * P:(k + 1) * P], xn_l[:, k * P:(k + 1) * P], ident[:, :])
                mm.then_inc(l_x, 1)

            def project_late_kv(c):
                pe.wait_ge(l_xc, c + 1)
                for k in range(KD):
                    pe.matmul(bank[7][:, 2 * P:3 * P], wk_s[:, k, :], xt_l[:, k, :], start=k == 0, stop=k == KD - 1)
                for t in range(2):
                    for k in range(KD):
                        mm = pe.matmul(bank[7][0:QL, 3 * P + t * DH:3 * P + (t + 1) * DH], xt_l[:, k, t * QL:(t + 1) * QL],
                                       wv_s[:, k, :], start=k == 0, stop=k == KD - 1)
                mm.then_inc(l_kv, 1)

            def project_late_q(c):
                for j in range(NPAIR):
                    for k in range(KD):
                        mm = pe.matmul(bank[j // 4][:, (j % 4) * P:(j % 4 + 1) * P], wq_s[:, k, j * P:(j + 1) * P], xt_l[:, k, :],
                                       start=k == 0, stop=k == KD - 1)
                    if j % 4 == 3:
                        mm.then_inc(l_q, 1)

            def late_scores(c, t):
                for a in range(2):
                    bk = bank[2 * t + a]
                    pe.matmul(bk[:, 0:4 * LW].rearrange("p (j w) -> p j w", w=LW), ones_bf[0:1, :],
                              pen_l[0:1, bass.ds(2 * c + t, 1), :].broadcast_to([1, 4, LW]), start=True, stop=False)
                    for j in range(4):
                        for u in range(2):
                            half = slice(u * DH, (u + 1) * DH)
                            mm = pe.matmul(bk[half, j * LW:(j + 1) * LW], q_l[half, 4 * a + j, t * QL:(t + 1) * QL],
                                           k_l[half, t, :], start=False, stop=j == 3)
                mm.then_inc(l_s, 1)

            def turn_late(t):
                for j in range(NPAIR):
                    mm = pe.transpose(bank[4 + j // 4][0:LW, (j % 4) * P:(j % 4 + 1) * P], ex_l[t][:, j, :], ident[:, :])
                mm.then_inc(l_t, 1)

            def weigh_late(t):
                for u in range(2):
                    mm = pe.matmul(bank[6][u * DH:(u + 1) * DH, :].rearrange("p (j q) -> p j q", q=QL), v_l[0:LW, t, :],
                                   pt_l[t][0:LW, :].rearrange("p (j u q) -> p j u q", u=2, q=QL)[:, :, u, :], start=True, stop=True)
                mm.then_inc(l_pv, 1)

            def project_late_o(bk, lhs):
                for j in range(NPAIR):
                    mm = pe.matmul(bk[:, 0:D], lhs(j), wo_s[:, j, :], start=j == 0, stop=j == NPAIR - 1)
                mm.then_inc(l_o, 1)

            def attend_late(c, first, last):
                pe.wait_ge(l_qc, 2 * c + 2)
                pe.wait_ge(l_kc, c + 1)
                late_scores(c, 0)
                if not first:
                    pe.wait_ge(l_tc, 2 * c)
                    pe.wait_ge(l_ac, 2 * c - 1)
                    weigh_late(1)
                late_scores(c, 1)
                if not last:
                    pe.wait_ge(l_vc, c + 1)
                    turn_late_x(c + 1)
                pe.wait_ge(l_sub, 2 * c + 1)
                if not first:
                    pe.wait_ge(l_ac, 2 * c)
                    project_late_o(bank[0], lambda j: at_l[:, j, :])
                pe.wait_ge(l_p, 2 * c + 1)
                turn_late(0)
                if not last:
                    project_late_kv(c + 1)
                pe.wait_ge(l_tc, 2 * c + 1)
                pe.wait_ge(l_vc, c + 1)
                weigh_late(0)
                if not last:
                    if not first:
                        pe.wait_ge(l_oc, c)
                    project_late_q(c + 1)
                pe.wait_ge(l_p, 2 * c + 2)
                turn_late(1)

            pe.wait_ge(const, NCONST)
            pe.wait_ge(ld_w, 16 * NLD)
            general = branch(pe)
            with pe.If(general):
                pe.wait_ge(gconst, NGCONST)
                pe.wait_ge(setup, NSETUP)
                project_x(0, True)
                project_v(0)
                with pe.Fori(0, B - 1) as b:
                    attend(b, True)
                attend(B - 1, False)

                pe.wait_ge(o_ev, B + 1)
                with pe.Fori(0, NC // 4) as r:
                    for half in range(2):
                        for u in (2 * half, 2 * half + 1):
                            c = 4 * r + u
                            pe.wait_ge(hnorm, c + 1)
                            pe.wait_ge(h_ev, c + 1)
                            for k in range(KD):
                                mm = pe.transpose(bank[u % 2][:, k * P:(k + 1) * P], h_n[u][:, k * P:(k + 1) * P], ident[:, :])
                            mm.then_inc(h_ps, 1)
                        for u in (2 * half, 2 * half + 1):
                            c = 4 * r + u
                            pe.wait_ge(h_ev, c + 1 + 2)
                            for k in range(KD):
                                mm = pe.matmul(bank[7][:, bass.ds(c * E0, E0)], h_t[u % 2][:, k, :], router[:, k, :],
                                               start=k == 0, stop=k == KD - 1)
                            mm.then_inc(lg_ps, 1)
            with pe.Else():
                pe.wait_ge(setup, NSETUP)
                pe.wait_ge(lsetup, 5)
                turn_late_x(0)
                project_late_kv(0)
                project_late_q(0)
                attend_late(0, True, False)
                with pe.Fori(1, NTW - 1) as c:
                    attend_late(c, False, False)
                attend_late(NTW - 1, False, True)
                pe.wait_ge(l_tc, 2 * NTW)
                pe.wait_ge(l_ac, 2 * NTW - 1)
                weigh_late(1)
                project_late_o(bank[1], lambda j: at_null)
                pe.wait_ge(l_ac, 2 * NTW)
                project_late_o(bank[0], lambda j: at_l[:, j, :])
                for c in range(NTW + 1):
                    pe.wait_ge(l_h, c + 1)
                    if c == 0:
                        pe.wait_ge(l_oc, NTW + 1)
                    for k in range(KD):
                        mm = pe.transpose(bank[c // 2][:, (c % 2 * KD + k) * P:(c % 2 * KD + k + 1) * P], h_l[:, c, k * P:(k + 1) * P],
                                          ident[:, :])
                    if c % 2 or c == NTW:
                        mm.then_inc(l_ht, 1)
                for c in range(NTW + 1):
                    pe.wait_ge(l_htc, c // 2 + 1)
                    for t in range(2):
                        o = (bank[6][P - QL:P, (2 * c + t) * E0:(2 * c + t + 1) * E0] if c < NTW else
                             bank[7][t * QL:(t + 1) * QL, 0:E0])
                        for k in range(KD):
                            mm = pe.matmul(o, ht_l[:, c, k * P + t * QL:k * P + (t + 1) * QL], router[:, k, :],
                                           start=k == 0, stop=k == KD - 1)
                mm.then_inc(l_lg, 1)
            cols = E0 * NC
            with pe.Fori(0, NSTEP + 1) as r:
                pe.wait_ge(cpart, r + 1)
                pe.matmul(bank[6][:, 0:E0], ones[:, :], part, start=True, stop=True).then_inc(csum, 1)
            for n, what in enumerate((tie, above)):
                flat = what.rearrange("p e c -> p (e c)")
                pe.wait_ge(tie_in, n + 1)
                pe.matmul(bank[4][:, 0:cols], before[:, :], flat, start=True, stop=True)
                pe.matmul(bank[5][:, 0:cols], ones[:, :], flat, start=True, stop=True).then_inc(tie_ps, 1)

            for m in range(NC // NTC):
                pe.wait_ge(onehot, m + 1)
                for c in range(NTC):
                    mm = pe.matmul(bank[3][:, 0:TILES], oh_lo[:, c, :], oh_hi[:, c, :], start=m + c == 0,
                                   stop=(m + 1) * NTC + c == NC + NTC - 1)
                mm.then_inc(tab_ps, 1)

            def expert_of(i):
                return pe.value_load(tile_e[0:1, bass.ds(i, 1)], min_val=0, max_val=E0 - 1)

            def rows_in(i, u, turn_no):
                hold(pe, got[u], 16 * turn_no + 16)
                pe.wait_ge(g_ev, i)
                for k in range(KD):
                    mm = pe.transpose(bank[0][:, k * P:(k + 1) * P], gath[u][:, k * P:(k + 1) * P], ident[:, :])
                mm.then_inc(g_ps, 1)

            def expert_up(i, last=False):
                e = expert_of(i)
                pe.wait_ge(g_ev, i + 1)
                pe.wait_ge(up_ev, i)
                for k in range(KD):
                    for f in range(2):
                        mm = pe.matmul(bank[1 + f], g_t[:, k, :],
                                       big_w[:, bass.ds(e * (KD * FF) + (k * FF + f * 512), 512)],
                                       start=k == 0, stop=k == KD - 1)
                mm.then_inc(up_ps, 1)
                return mm

            def turn_up(j, u):
                pe.wait_ge(up_ev, j + 1)
                pe.wait_ge(t_eva, j + 1)
                pe.wait_ge(t_evd, j + 1)
                for f in range(NF):
                    mm = pe.transpose(bank[3 + f // 4][:, (f % 4) * P:(f % 4 + 1) * P], act1[u][:, f * P:(f + 1) * P], ident[:, :])
                mm.then_inc(t_ps, 1)

            def expert_down(j, u):
                e = expert_of(j)
                pe.wait_ge(t_eva, j + 2)
                pe.wait_ge(t_evd, j + 2)
                pe.wait_ge(dn_ev, j + 1)
                for f in range(NF):
                    mm = pe.matmul(bank[5 + u][:, 0:D], act_t[:, f, :], arena[:, bass.ds(e * (NF * D) + f * D, D)],
                                   start=f == 0, stop=f == NF - 1)
                mm.then_inc(dn_ps, 1)

            pe.wait_ge(table, 1)
            pe.wait_ge(ld_w1, 16)
            pe.wait_ge(ld_w2, 16)
            def experts(tiles):
                def tile(i, v, turn_no):
                    rows_in(i, (1 + v) % 2, turn_no)
                    turn_up(i - 1, v)
                    expert_up(i)
                    expert_down(i - 1, v)

                rows_in(0, 0, 0)
                expert_up(0)
                with pe.Fori(0, (tiles - 1) // 2) as r:
                    for v in range(2):
                        tile(1 + 2 * r + v, v, r + v)
                if tiles % 2 == 0:
                    tile(tiles - 1, 0, tiles // 2 - 1)
                turn_up(tiles - 1, (tiles - 1) % 2)
                expert_down(tiles - 1, (tiles - 1) % 2)

            with pe.If(general):
                experts(TILES)
            with pe.Else():
                experts(TILES_L)

            pe.wait_ge(ld_v, 16 * 13)
            pe.wait_ge(cb, 1)
            pe.matmul(bank[7][:, 0:B * E1], ones[0:64, :], cgo[0:64].rearrange("p b e -> p (b e)"),
                      start=True, stop=True).then_inc(cg_ps, 1)

            NQ = NSH + E1

            def up_gate(b, q):
                m = (E1 + q) if q < NSH else q - NSH
                n = NQ * b + q
                pe.wait_ge(md, n + 1)
                bk = bank[2 + q % 2]
                for half, w in enumerate((mg_s, mu_s)):
                    for k in range(KD):
                        mm = pe.matmul(bk[:, half * S:(half + 1) * S], w[:, k, m * M1:(m + 1) * M1], x1_t[:, k, :],
                                       start=k == 0, stop=k == KD - 1)
                mm.then_inc(gu_ps, 1)

            def down_shared(b):
                pe.wait_ge(md, NQ * b + NSH + 2)
                pe.wait_ge(d_acc, (1 + E1) * b + 2)
                for n in range(NB):
                    for q in range(NSH):
                        mm = pe.matmul(bank[4][:, n * D:(n + 1) * D], mid[q][:, n * P:(n + 1) * P], md_s[:, E1 + q, :],
                                       start=q == 0, stop=q == NSH - 1)
                mm.then_inc(d_ps, 1)

            def down(b, q):
                e = q - NSH
                pe.wait_ge(md, NQ * b + q + 1 + 2)
                pe.wait_ge(d_acc, (1 + E1) * b + e + 2)
                for n in range(NB):
                    mm = pe.matmul(bank[4 + (1 + e) % 2][:, n * D:(n + 1) * D], mid[q % 2][:, n * P:(n + 1) * P],
                                   md_s[:, e, :], start=True, stop=True)
                mm.then_inc(d_ps, 1)

            with pe.Fori(0, B) as b:
                pe.wait_ge(x1, NB * (b + 1) + 2)
                pe.wait_ge(x1_ev, b + 1)
                for k in range(KD):
                    for n in range(NB):
                        mm = pe.transpose(bank[0][:, k * S + n * P:k * S + (n + 1) * P], x1_s[:, n, k * P:(k + 1) * P], ident[:, :])
                mm.then_inc(x1_ps, 1)
                pe.wait_ge(x1_ev, b + 2)
                pe.wait_ge(rl_sub, b + 1)
                for n in range(NB):
                    for k in range(KD):
                        mm = pe.matmul(bank[1][:, n * E1:(n + 1) * E1], x1_t[:, k, n * P:(n + 1) * P], wt_s[:, k, :],
                                       start=k == 0, stop=k == KD - 1)
                mm.then_inc(rl_ps, 1)
                up_gate(b, 0)
                up_gate(b, 1)
                down_shared(b)
                up_gate(b, 2)
                for q in range(NSH, NQ):
                    if q + 1 < NQ:
                        up_gate(b, q + 1)
                    down(b, q)
                pe.wait_ge(yfin, b + 1)
                pe.wait_ge(z_ev, b + 1)
                pe.wait_ge(pool_r, b + 1)
                for k in range(KD):
                    for n in range(NB):
                        mm = pe.transpose(bank[6][:, k * S + n * P:k * S + (n + 1) * P], acc[:, n, k * P:(k + 1) * P], ident[:, :])
                mm.then_inc(z_ps, 1)

            pe.wait_ge(pool_r, B + 1)
            for k in range(KD):
                mm = pe.matmul(bank[1][0:B, 0:E2], pooled[:, k, :], gw_s[:, k, :], start=k == 0, stop=k == KD - 1)
            mm.then_inc(fl_ps, 1)
            pe.wait_ge(fdg, 1)
            pe.matmul(bank[7][:, 0:B * E2], ones[0:B, :], fdiag.rearrange("p b e -> p (b e)"), start=True, stop=True).then_inc(fg_ps, 1)
            pe.wait_ge(z_ev, B + 1)
            NE = E2 * KD
            with pe.Fori(0, B // 2) as r:
                for e in range(E2):
                    for oc in range(KD):
                        q = e * KD + oc
                        pe.wait_ge(e_act, NE * r + q + 1)
                        for k in range(KD):
                            mm = pe.matmul(bank[2 + q % 2], ew_s[:, k, e, oc * P:(oc + 1) * P], z_t[:, k, bass.ds(r * 2 * S, 2 * S)],
                                           start=k == 0, stop=k == KD - 1)
                        mm.then_inc(e_ps, 1)
                pe.wait_ge(e_acc, NE * (r + 1) + 2)
                pe.wait_ge(r_ev, r + 1)
                for n in range(2 * NB):
                    for oc in range(KD):
                        mm = pe.transpose(bank[4 + n // 2][:, (n % 2) * D + oc * P:(n % 2) * D + (oc + 1) * P],
                                          accf[:, oc, n * P:(n + 1) * P], ident[:, :])
                mm.then_inc(r_ps, 1)

        @block.scalar
        def _(act):
            act.sem_inc(exped, NSIM)
            act.sem_inc(o_ev, 1)
            act.sem_inc(t_eva, 1)
            act.sem_inc(x1_ev, 1)
            act.sem_inc(z_ev, 1)
            act.sem_inc(h_ev, 2)
            act.sem_inc(e_act, 2)
            b_a, b_b = bank[6], bank[7]
            def copies(b):
                act.wait_ge(x_ps, b + 1)
                act.copy(xn_t[:, :, 1:1 + S], b_a.rearrange("p (k t) -> p k t", k=KD)).then_inc(x_ev, 1)
                act.wait_ge(k_ps, b + 1)
                act.copy(k_t[:, 1:1 + S], b_b[:, 0:S]).then_inc(k_ev, 1)
                for j in range(4):
                    act.wait_ge(q_ps, 4 * b + j + 1)
                    act.copy(q_t[:, 2 * j:2 * j + 2, :], (b_a, b_b)[j % 2].rearrange("p (a t) -> p a t", a=2)).then_inc(q_ev, 1)

            def attend(b, more):
                for s in range(H):
                    g = b * H + s
                    act.wait_ge(normed, g + 1)
                    act.wait_ge(simmed, g + 1 + S_FREE)
                    for n, (c0, c1) in enumerate(((0, W0), (W0, SW))):
                        a = act.activation(pr[:, s % NPR, c0:c1], sim[:, s % NSIM, c0:c1], ACT.Exp,
                                           bias=nmax[:, s % NSIM, n:n + 1], scale=-1.0,
                                           accum_out=psum_row[:, s % NPR, n:n + 1])
                    a.then_inc(exped, 1)
                if more:
                    copies(b + 1)
                hold(act, o_ps, b + 1)
                act.copy(tokens[:, bass.ds(b * NB, NB), :], b_a.rearrange("p (n d) -> p n d", n=NB)).then_inc(o_ev, 1)

            def attend_late(c, first, last):
                if not first:
                    act.wait_ge(l_pv, 2 * c)
                    act.copy(at_l[:, :, QL:P], bank[6].rearrange("p (j q) -> p j q", q=QL)).then_inc(l_ac, 1)
                act.wait_ge(l_kc, c + 1)
                act.copy(v_l[0:QL, :, :], bank[7][0:QL, 3 * P:4 * P].rearrange("p (t d) -> p t d", t=2)).then_inc(l_vc, 1)
                act.wait_ge(l_sub, 2 * c + 1)
                act.activation(ex_l[0], sim_l[0], ACT.Exp).then_inc(l_e, 1)
                if not last:
                    act.wait_ge(l_x, c + 2)
                    act.copy(xt_l, bank[7][:, 0:D].rearrange("p (k t) -> p k t", k=KD)).then_inc(l_xc, 1)
                act.wait_ge(l_sub, 2 * c + 2)
                act.activation(ex_l[1], sim_l[1], ACT.Exp).then_inc(l_e, 1)
                if not first:
                    act.wait_ge(l_o, c)
                    act.copy(o_l[:, bass.ds(c - 1, 1), :].rearrange("p a d -> p (a d)"), bank[0][:, 0:D]).then_inc(l_oc, 1)
                act.wait_ge(l_t, 2 * c + 1)
                act.copy(pt_l[0][0:LW, :].rearrange("p (a t) -> p a t", a=2), psum[0:LW, 4:6, :]).then_inc(l_tc, 1)
                act.wait_ge(l_pv, 2 * c + 1)
                act.copy(at_l[:, :, 0:QL], bank[6].rearrange("p (j q) -> p j q", q=QL)).then_inc(l_ac, 1)
                if not last:
                    late_queries(c + 1)
                act.wait_ge(l_t, 2 * c + 2)
                act.copy(pt_l[1][0:LW, :].rearrange("p (a t) -> p a t", a=2), psum[0:LW, 4:6, :]).then_inc(l_tc, 1)

            def late_queries(c):
                for a in range(2):
                    act.wait_ge(l_q, 2 * c + a + 1)
                    act.copy(q_l[:, 4 * a:4 * a + 4, :], bank[a].rearrange("p (j t) -> p j t", j=4)).then_inc(l_qc, 1)

            act.wait_ge(const, NCONST)
            general = branch(act)
            with act.If(general):
                act.wait_ge(xvar, 1)
                act.activation(rstd[:, :], xmv[:, :, 1], ACT.Sqrt, bias=eps_col[:, 0:1]).then_inc(xsd, 1)
                act.wait_ge(setup, NSETUP)
                copies(0)
                with act.Fori(0, B - 1) as b:
                    attend(b, True)
                attend(B - 1, False)

                act.wait_ge(ovar, 1)
                act.activation(r_rstd, omv[:, :, 1], ACT.Sqrt, bias=eps_col[:, 0:1]).then_inc(osd, 1)
                with act.Fori(0, NC // 4) as r:
                    for u in range(4):
                        c = 4 * r + u
                        act.wait_ge(lg_ps, c + 1)
                        act.wait_ge(h_ps, c + 1 + 4)
                        act.copy(h_t[u % 2], bank[u % 2][:, 0:D].rearrange("p (k t) -> p k t", k=KD)).then_inc(h_ev, 1)
            with act.Else():
                act.wait_ge(lvar, 1)
                act.activation(rstd_l[:, 0:NTW], mv_l[:, 0:NTW, 1], ACT.Sqrt, bias=eps_col[:, 0:1]).then_inc(lsd, 1)
                act.wait_ge(l_x, 1)
                act.copy(xt_l, bank[7][:, 0:D].rearrange("p (k t) -> p k t", k=KD)).then_inc(l_xc, 1)
                late_queries(0)
                attend_late(0, True, False)
                with act.Fori(1, NTW - 1) as c:
                    attend_late(c, False, False)
                attend_late(NTW - 1, False, True)
                act.wait_ge(l_pv, 2 * NTW)
                act.copy(at_l[:, :, QL:P], bank[6].rearrange("p (j q) -> p j q", q=QL)).then_inc(l_ac, 1)
                act.wait_ge(l_o, NTW)
                act.copy(o_l[:, NTW, :], bank[1][:, 0:D]).then_inc(l_oc, 1)
                act.wait_ge(l_o, NTW + 1)
                act.copy(o_l[:, NTW - 1, :], bank[0][:, 0:D]).then_inc(l_oc, 1)
                act.wait_ge(lovar, 1)
                act.activation(rstd_l, mv_l[:, :, 1], ACT.Sqrt, bias=eps_col[:, 0:1]).then_inc(losd, 1)
                for m in range((NTW + 2) // 2):
                    n = min(2, NTW + 1 - 2 * m)
                    act.wait_ge(l_ht, m + 1)
                    act.copy(ht_l[:, 2 * m:2 * m + n, :], bank[m][:, 0:n * D].rearrange("p (c d) -> p c d", c=n)).then_inc(l_htc, 1)
            act.wait_ge(lsub, 1)
            act.activation(ex, ex, ACT.Exp).then_inc(lexp, 1)

            act.wait_ge(ld_b, 32)
            act.wait_ge(table, 1)

            def up_copy(i, u):
                act.wait_ge(up_ps, i + 1)
                act.copy(act1[u].rearrange("p (a f) -> p a f", a=2), psum[:, 1:3, :]).then_inc(up_ev, 1)

            def relu_half(j):
                e = act.value_load(tile_e[0:1, bass.ds(j, 1)], min_val=0, max_val=E0 - 1)
                hold(act, t_ps, j + 1)
                for f in range(NF // 2):
                    a = act.activation(act_t[:, f, :], bank[3][:, f * P:(f + 1) * P], ACT.Relu,
                                       bias=b1_s[:, bass.ds(e * NF + f, 1)])
                a.then_inc(t_eva, 1)

            def experts(tiles):
                up_copy(0, 0)
                with act.Fori(0, (tiles - 1) // 2) as r:
                    for v in range(2):
                        relu_half(2 * r + v)
                        up_copy(1 + 2 * r + v, (1 + v) % 2)
                if tiles % 2 == 0:
                    relu_half(tiles - 2)
                    up_copy(tiles - 1, 1)
                relu_half(tiles - 1)

            with act.If(general):
                experts(TILES)
            with act.Else():
                experts(TILES_L)

            NQ = NSH + E1
            with act.Fori(0, B) as b:
                act.wait_ge(x1_ps, b + 2)
                act.copy(x1_t, bank[0].rearrange("p (k t) -> p k t", k=KD)).then_inc(x1_ev, 1)

                def leaky(q):
                    act.wait_ge(gu_ps, NQ * b + q + 1)
                    act.wait_ge(md, NQ * b + q + 1)
                    act.copy(leak[q % 2], bank[2 + q % 2][:, 0:S]).then_inc(lk, 1)

                act.wait_ge(rl_sub, b + 2)
                act.activation(gex, gex, ACT.Exp, scale=0.5).then_inc(rl_exp, 1)
                for q in range(NQ):
                    leaky(q)
                hold(act, z_ps, b + 2)
                act.copy(z_t[:, :, bass.ds(b * S, S)], bank[6].rearrange("p (k t) -> p k t", k=KD)).then_inc(z_ev, 1)
            act.wait_ge(fl_sub, 1)
            act.activation(fex, flog, ACT.Exp, bias=fnm[:, 0:1]).then_inc(fl_exp, 1)
            NE = E2 * KD
            with act.Fori(0, B // 2) as r:
                for e in range(E2):
                    for oc in range(KD):
                        q = e * KD + oc
                        act.wait_ge(e_ps, NE * r + q + 1)
                        act.wait_ge(e_acc, NE * r + q + 1)
                        act.activation(ge[q % 2], bank[2 + q % 2], ACT.Gelu, bias=eb_s[:, oc, e:e + 1]).then_inc(e_act, 1)

        @block.vector
        def _(dve):
            dve.sem_inc(simmed, S_FREE)
            dve.sem_inc(pt_ev, T_FREE)
            dve.sem_inc(at_ev, PV_FREE)
            dve.sem_inc(dn_ev, 2)
            dve.sem_inc(t_evd, 1)
            dve.sem_inc(rl_sub, 1)
            dve.sem_inc(pool_r, 1)
            dve.sem_inc(r_ev, 1)
            dve.sem_inc(x1, 2)
            dve.sem_inc(md, 2)
            dve.sem_inc(d_acc, 2)
            dve.sem_inc(e_acc, 2)
            b_s, b_t, b_pv, b_a, b_b = bank[0:2], bank[2:4], bank[4:6], bank[6], bank[7]

            dve.wait_ge(ld_mask, 16)
            mv = mask_u8.rearrange("p (b s) -> p b s", b=B)
            dve.tensor_reduce(early_f[:, :], mv[:, :, 0:KEY0], mybir.AxisListType.XY, ALU.max).then_inc(lflag, 1)
            dve.wait_ge(lflag, 1)
            dve.tensor_copy(early_i[:, :], early_f[:, :]).then_inc(early, 1)
            dve.wait_ge(const, NCONST)
            dve.tensor_copy(iota_f[:, :], iota_i[:, :]).then_inc(setup, 1)
            dve.tensor_scalar(rev8[:, :], iota_i[:, 0:8], -1.0, 8.0, ALU.mult, ALU.add).then_inc(setup, 1)
            dve.wait_ge(ld_w, 16 * NLD)
            for k in range(KD):
                dve.tensor_scalar(wq_s[:, k, :], wq_s[:, k, :], gin[:, k:k + 1], DH ** -0.5, ALU.mult, ALU.mult).then_inc(setup, 1)
                for half in range(2):
                    dve.tensor_scalar(wk_s[:, k, half * DH:(half + 1) * DH], wkv_r[:, k, 0:DH], gin[:, k:k + 1], None,
                                      ALU.mult)
                dve.tensor_scalar(wv_s[:, k, :], wkv_r[:, k, DH:], gin[:, k:k + 1], None, ALU.mult).then_inc(setup, 1)
                dve.tensor_scalar(router[:, k, :], router[:, k, :], gout[:, k:k + 1], None, ALU.mult).then_inc(setup, 1)

            def general_setup():
                for k in range(4):
                    dve.wait_ge(ld_x[k], 48 if k == 0 else 16)
                    for c in range(k * NC // 4, (k + 1) * NC // 4):
                        st = dve.bn_stats(xstat[:, c, :], tokens[:, c, :])
                st.then_inc(sch, 1)
                dve.wait_ge(sch, 1)
                for c in range(NC):
                    st = dve.bn_aggr(xmv[:, c, :], xstat[:, c, :])
                st.then_inc(xvar, 1)
                dve.wait_ge(ld_bias, 48)
                dve.tensor_copy(k_t[:, 0:1], nk_col[:, :]).then_inc(gsetup, 1)
                for c0 in (0, W0):
                    dve.tensor_copy(bias[:, :, c0], nb_bc[:, :]).then_inc(gsetup, 1)
                dve.tensor_scalar(penalty[:, :, 1:W0], mv[:, :, 0:P], BIG, -BIG, ALU.mult, ALU.add).then_inc(gsetup, 1)
                dve.tensor_scalar(penalty[:, :, W0 + 1:SW], mv, BIG, -BIG, ALU.mult, ALU.add).then_inc(gsetup, 1)
                dve.wait_ge(xsd, 1)
                dve.reciprocal(rstd[:, :], rstd[:, :]).then_inc(gsetup, 1)
                dve.wait_ge(gsetup, NGSETUP)
                dve.scalar_tensor_tensor(shift[:, :], xmv[:, :, 0], -1.0, rstd[:, :], ALU.mult, ALU.mult).then_inc(sch, 1)
                dve.wait_ge(sch, 2)

            def normalise_x(b, first):
                if not first:
                    dve.wait_ge(x_ps, b)
                for n in range(NB):
                    c = b * NB + n
                    i = dve.tensor_scalar(xn[:, n, :], tokens[:, bass.ds(c, 1), :].rearrange("p a d -> p (a d)"),
                                          rstd[:, bass.ds(c, 1)], shift[:, bass.ds(c, 1)], ALU.mult, ALU.add)
                i.then_inc(xnorm, 1)

            def copy_v(b):
                dve.wait_ge(v_ps, b + 1)
                dve.tensor_copy(v_last[96:P, :, :], b_b[96:P, S + P:2 * S].rearrange("p (n d) -> p n d", n=NB))
                dve.tensor_copy(v_s[:, :, :], b_b[:, S:S + P].rearrange("p (n d) -> p n d", n=NB)).then_inc(v_ev, 1)

            def biased(b, s):
                g = b * H + s
                dve.wait_ge(exped, g + 1)
                hold(dve, scores, g + 1)
                for n, (c0, c1) in enumerate(((0, W0), (W0, SW))):
                    i = dve.tensor_tensor_reduce(sim[:, s % NSIM, c0:c1], b_s[s % 2][:, c0:c1], bias[:, s, c0:c1], -1.0, 3e38,
                                                 ALU.add, ALU.min, nmax[:, s % NSIM, n:n + 1])
                i.then_inc(simmed, 1)

            def invert(b, s):
                g = b * H + s
                dve.wait_ge(normed, g + 1)
                dve.wait_ge(exped, g + 1 + NSIM)
                dve.reciprocal(rinv[:, s % NPR, :], psum_row[:, s % NPR, :]).then_inc(recip, 1)

            def copy_pt(b, s):
                g = b * H + s
                dve.wait_ge(turned, g + 1 + NPN)
                dve.wait_ge(pv, g + 1)
                dve.tensor_copy(p_t[:, s % NPT, :], b_t[s % 2][:, 0:3 * P]).then_inc(pt_ev, 1)

            def copy_at(b, k):
                dve.wait_ge(pv, b * H + 4 * k + 4 + NPT)
                dve.tensor_copy(at_t[:, 2 * k:2 * k + 2, :], b_pv[k % 2].rearrange("p (a t) -> p a t", a=2)).then_inc(at_ev, 1)

            def attend(b, more):
                for s in range(H):
                    biased(b, s)
                    if s >= 1:
                        invert(b, s - 1)
                    if s >= 2:
                        copy_pt(b, s - 2)
                    if s >= 7 and s % 4 == 3:
                        copy_at(b, (s - 7) // 4)
                    if s == 8 and more:
                        normalise_x(b + 1, False)
                invert(b, H - 1)
                copy_pt(b, H - 2)
                copy_pt(b, H - 1)
                copy_at(b, 3)
                dve.wait_ge(last_ps, b + 2)
                dve.wait_ge(at_ev, 4 * b + 4 + PV_FREE)
                dve.tensor_tensor(at_t[:, :, P - 1:S:P], at_t[:, :, P - 1:S:P],
                                  b_t[0][:, 0:NB * NPAIR].rearrange("p (n j) -> p j n", n=NB), ALU.add).then_inc(at_done, 1)
                if more:
                    copy_v(b + 1)
            def normalise_late(c):
                row = x_l[:, bass.ds(c, 1), :].rearrange("p a d -> p (a d)")
                dve.tensor_scalar(xn_l, row, mv_l[:, bass.ds(c, 1), 0], rstd_l[:, bass.ds(c, 1)], ALU.subtract, ALU.mult).then_inc(l_xn, 1)

            def late_keys(c):
                dve.wait_ge(l_kv, c + 1)
                dve.tensor_copy(k_l[:, :, 0:QL], bank[7][:, 2 * P:3 * P].rearrange("p (t s) -> p t s", t=2)).then_inc(l_kc, 1)

            def attend_late(c, first, last):
                at = [0]

                def llink(ins):
                    at[0] += 1
                    ins.then_inc(l_dv, 1)
                    hold(dve, l_dv, LDV0 + LDV * c + at[0])

                def scores(t):
                    hold(dve, l_s, 2 * c + t + 1)
                    llink(dve.tensor_tensor(sim_l[t].rearrange("p (a j) w -> p a j w", a=2),
                                            psum[:, 2 * t:2 * t + 2, 0:4 * LW].rearrange("p a (j w) -> p a j w", w=LW),
                                            bias_l.rearrange("p (a j) w -> p a j w", a=2), ALU.add))
                    llink(dve.tensor_reduce(nm_l[t], sim_l[t], AXX, ALU.max))
                    dve.tensor_tensor(sim_l[t], sim_l[t], nm_l[t].unsqueeze(2).broadcast_to([P, NPAIR, LW]),
                                      ALU.subtract).then_inc(l_sub, 1)

                def probs(t):
                    hold(dve, l_e, 2 * c + t + 1)
                    llink(dve.tensor_reduce(rs_l[t], ex_l[t], AXX, ALU.add))
                    llink(dve.reciprocal(rs_l[t], rs_l[t]))
                    dve.tensor_tensor(ex_l[t], ex_l[t], rs_l[t].unsqueeze(2).broadcast_to([P, NPAIR, LW]),
                                      ALU.mult).then_inc(l_p, 1)

                if not last:
                    hold(dve, l_x, c + 1)
                    normalise_late(c + 1)
                scores(0)
                scores(1)
                probs(0)
                if not first:
                    hold(dve, l_oc, c)
                    dve.bn_stats(st_l[:, bass.ds(c - 1, 1), :].rearrange("p a s -> p (a s)"),
                                 o_l[:, bass.ds(c - 1, 1), :].rearrange("p a d -> p (a d)"))
                probs(1)
                if not last:
                    late_keys(c + 1)
                assert at[0] == LDV

            LDV = 8
            LDV0 = 2

            def late_attention():
                dve.wait_ge(ld_x[0], 32)
                for c in range(NTW):
                    st = dve.bn_stats(st_l[:, c, :], x_l[:, c, :])
                st.then_inc(l_dv, 1)
                dve.wait_ge(l_dv, 1)
                for c in range(NTW):
                    st = dve.bn_aggr(mv_l[:, c, :], st_l[:, c, :])
                st.then_inc(lvar, 1)
                for t in range(2):
                    dve.tensor_copy(bias_l[t * DH:(t + 1) * DH, :, QL], nb_bc[t * DH:(t + 1) * DH, t:H:2]).then_inc(lsetup, 1)
                dve.tensor_copy(k_l[:, :, QL], nk_col[:, 0:1].broadcast_to([P, 2])).then_inc(lsetup, 1)
                dve.tensor_scalar(at_null, ones[:, :], nv_col[:, 0:1], None, ALU.mult).then_inc(lsetup, 1)
                dve.tensor_scalar(pen_l[:, :, 0:QL], mv[:, :, KEY0:S], BIG, -BIG, ALU.mult, ALU.add).then_inc(lsetup, 1)
                dve.wait_ge(lsd, 1)
                dve.reciprocal(rstd_l[:, 0:NTW], rstd_l[:, 0:NTW]).then_inc(l_dv, 1)
                dve.wait_ge(l_dv, 2)
                normalise_late(0)
                late_keys(0)
                dve.wait_ge(lconst, 2)
                dve.wait_ge(lsetup, 5)
                attend_late(0, True, False)
                with dve.Fori(1, NTW - 1) as c:
                    attend_late(c, False, False)
                attend_late(NTW - 1, False, True)
                end = LDV0 + LDV * NTW
                for k, c in enumerate((NTW, NTW - 1)):
                    dve.wait_ge(l_oc, NTW + k)
                    st = dve.bn_stats(st_l[:, c, :], o_l[:, c, :])
                st.then_inc(l_dv, 1)
                dve.wait_ge(l_dv, end + 1)
                for c in range(NTW + 1):
                    st = dve.bn_aggr(mv_l[:, c, :], st_l[:, c, :])
                st.then_inc(lovar, 1)
                dve.wait_ge(losd, 1)
                dve.reciprocal(rstd_l, rstd_l).then_inc(l_dv, 1)
                dve.wait_ge(l_dv, end + 2)
                for c in range(NTW + 1):
                    dve.tensor_scalar(h_l[:, c, :], o_l[:, c, :], mv_l[:, c, 0:1], rstd_l[:, c:c + 1], ALU.subtract, ALU.mult).then_inc(l_h, 1)
                dve.wait_ge(l_lg, 1)
                dve.tensor_copy(lg, bank[7][:, 0:E0].unsqueeze(1).broadcast_to([P, NC, E0])).then_inc(l_dv, 1)
                dve.wait_ge(l_dv, end + 3)
                dve.tensor_copy(lg[P - QL:P, 1:NC:NB, :], bank[6][P - QL:P, 0:B * E0].rearrange("p (b e) -> p b e", b=B)).then_inc(l_dv, 1)
                dve.wait_ge(l_dv, end + 4)

            general = branch(dve)
            with dve.If(general):
                general_setup()
                normalise_x(0, True)
                copy_v(0)
                with dve.Fori(0, B - 1) as b:
                    attend(b, True)
                attend(B - 1, False)

                dve.wait_ge(o_ev, B + 1)
                for c in range(NC):
                    i = dve.bn_stats(ostat[:, c, :], tokens[:, c, :])
                i.then_inc(gch0, 1)
                dve.wait_ge(gch0, 1)
                for c in range(NC):
                    i = dve.bn_aggr(omv[:, c, :], ostat[:, c, :])
                i.then_inc(ovar, 1)
                dve.wait_ge(osd, 1)
                dve.reciprocal(r_rstd, r_rstd).then_inc(gch0, 1)
                dve.wait_ge(gch0, 2)
                dve.wait_ge(o_ev, B + 1)
                with dve.Fori(0, NC // 4) as r:
                    for u in range(4):
                        c = 4 * r + u
                        dve.wait_ge(h_ps, c + 1)
                        dve.wait_ge(h_st[u], 16 * r + 16)
                        dve.tensor_scalar(h_n[u], tokens[:, bass.ds(c, 1), :].rearrange("p a d -> p (a d)"),
                                          omv[:, bass.ds(c, 1), 0], r_rstd[:, bass.ds(c, 1)], ALU.subtract, ALU.mult).then_inc(hnorm, 1)
                dve.wait_ge(lg_ps, NC + 2)
                dve.tensor_copy(lg, bank[7][:, 0:NC * E0].rearrange("p (c e) -> p c e", e=E0)).then_inc(gch0, 1)
                dve.wait_ge(gch0, 3)
            with dve.Else():
                late_attention()

            steps = [0]

            def link(ins):
                steps[0] += 1
                ins.then_inc(dch, 1)
                dve.wait_ge(dch, steps[0])

            link(dve.tensor_reduce(lmax, lg, AXX, ALU.max))
            bc = [P, NC, E0]
            bt = [P, E0, NC]
            dve.tensor_tensor(ex, lg, lmax.unsqueeze(2).broadcast_to(bc), ALU.subtract).then_inc(lsub, 1)
            link(dve.tensor_tensor(hit, lg, lmax.unsqueeze(2).broadcast_to(bc), ALU.is_equal))
            link(dve.tensor_tensor(hit, hit, rev8[:, :].unsqueeze(1).broadcast_to(bc), ALU.mult))
            link(dve.tensor_reduce(top, hit, AXX, ALU.max))
            link(dve.tensor_tensor(oh, top.unsqueeze(1).broadcast_to(bt), rev8[:, :].unsqueeze(2).broadcast_to(bt), ALU.is_equal))
            dve.wait_ge(lexp, 1)
            link(dve.tensor_reduce(esum, ex, AXX, ALU.add))
            link(dve.reciprocal(prob, esum))
            link(dve.tensor_tensor(pe_key, oh, prob.unsqueeze(1).broadcast_to(bt), ALU.mult))
            link(dve.memset(thr[:, :], THR0))
            link(dve.memset(bit[:, :], 1 << (NSTEP - 1)))
            base, per = steps[0], 6
            with dve.Fori(0, NSTEP) as r:
                at = [0]

                def chain(ins):
                    at[0] += 1
                    ins.then_inc(dch, 1)
                    hold(dve, dch, base + per * r + at[0])

                chain(dve.tensor_tensor(cand[:, :], thr[:, :], bit[:, :], ALU.bitwise_or))
                chain(dve.tensor_tensor(cmp_s, pe_key, cand[:, :].bitcast(F32).unsqueeze(2).broadcast_to(bt), ALU.is_ge))
                dve.tensor_reduce(part, cmp_s, AXX, ALU.add).then_inc(cpart, 1)
                hold(dve, csum, r + 1)
                chain(dve.tensor_scalar(part, bank[6][:, 0:E0], float(CAPACITY), None, ALU.is_ge))
                chain(dve.tensor_tensor(step_bit[:, :], part, bit[:, :], ALU.mult))
                chain(dve.tensor_tensor(thr[:, :], thr[:, :], step_bit[:, :], ALU.bitwise_or))
                chain(dve.tensor_scalar(bit[:, :], bit[:, :], 1, None, ALU.logical_shift_right))
                assert at[0] == per
            steps[0] = base + per * NSTEP
            thr_bc = thr[:, :].bitcast(F32).unsqueeze(2).broadcast_to(bt)
            link(dve.tensor_tensor(above, pe_key, thr_bc, ALU.is_gt))
            dve.tensor_tensor(tie, pe_key, thr_bc, ALU.is_equal).then_inc(tie_in, 1)
            dve.tensor_reduce(part, above, AXX, ALU.add).then_inc(cpart, 1)
            link(dve.memset(seg, 1.0))
            link(dve.memset(seg[:, :, 0:1], 0.0))

            def flat(ap):
                return ap.rearrange("p e c -> p (e c)")

            def ranks(n):
                dve.wait_ge(tie_ps, n)
                w = E0 * NC
                link(dve.tensor_copy(flat(tot), bank[5][:, 0:w]))
                link(dve.tensor_tensor_scan(flat(run), flat(seg), flat(tot), 0.0, ALU.mult, ALU.add))
                link(dve.tensor_tensor(flat(rank), flat(run), flat(tot), ALU.subtract))
                link(dve.tensor_tensor(flat(rank), flat(rank), bank[4][:, 0:w], ALU.add))

            dve.wait_ge(csum, NSTEP + 1)
            link(dve.tensor_scalar(budget, bank[6][:, 0:E0], -1.0, float(CAPACITY), ALU.mult, ALU.add))
            ranks(1)
            link(dve.tensor_tensor(rank, rank, budget.unsqueeze(2).broadcast_to(bt), ALU.is_lt))
            link(dve.tensor_tensor(rank, rank, tie, ALU.mult))
            link(dve.tensor_tensor(fin, above, rank, ALU.add))
            link(dve.tensor_reduce(kept, fin[:, 1:E0, :].rearrange("p e c -> p c e"), AXX, ALU.add))
            link(dve.tensor_scalar(fin[:, 0, :], kept, -1.0, 1.0, ALU.mult, ALU.add))
            dve.wait_ge(slots, 4)
            link(dve.tensor_tensor(above, fin, slot[:, :].unsqueeze(1).broadcast_to(bt), ALU.mult))
            dve.sem_inc(tie_in, 1)
            link(dve.tensor_tensor(token_s[:, :], token_i[:, :], slot[:, :], ALU.mult))
            ranks(2)
            link(dve.tensor_scalar(cnt_i[:, :], run[:, :, NC - 1], reserved[:, 0:1], float(P - 1), ALU.add, ALU.add))
            link(dve.tensor_scalar(cnt_i[:, :], cnt_i[:, :], 7, None, ALU.logical_shift_right))
            link(dve.tensor_copy(ntile, cnt_i[:, :]))
            link(dve.tensor_tensor_scan(tcum, ones[:, 0:E0], ntile, 0.0, ALU.mult, ALU.add))
            link(dve.tensor_tensor(tstart, tcum, ntile, ALU.subtract))
            link(dve.tensor_scalar(tcum, tstart, float(P), None, ALU.mult))
            link(dve.scalar_tensor_tensor(rank, rank, reserved[:, 0:1], slot[:, :].unsqueeze(1).broadcast_to(bt), ALU.add, ALU.mult))
            link(dve.tensor_tensor(rank, rank, tcum.unsqueeze(2).broadcast_to(bt), ALU.add))
            link(dve.tensor_tensor(rank, rank, fin, ALU.mult))
            link(dve.tensor_reduce(pos, rank.rearrange("p e c -> p c e"), AXX, ALU.add))
            link(dve.tensor_copy(pos_i[:, :], pos))
            link(dve.tensor_scalar(hi_i[:, :], pos_i[:, :], 7, None, ALU.logical_shift_right))
            link(dve.tensor_copy(hi, hi_i[:, :]))
            link(dve.scalar_tensor_tensor(lo, hi, -float(P), pos, ALU.mult, ALU.add))
            bx = [P, TILES, E0 - 1]
            link(dve.tensor_tensor(tcmp, iota_f[:, 0:TILES].unsqueeze(2).broadcast_to(bx),
                                   tstart[:, 1:E0].unsqueeze(1).broadcast_to(bx), ALU.is_ge))
            link(dve.tensor_reduce(tile_f, tcmp, AXX, ALU.add))
            link(dve.tensor_copy(tile_e[:, :], tile_f))

            for m in range(NC // NTC):
                if m:
                    dve.wait_ge(tab_ps, m)
                cols = slice(m * NTC, (m + 1) * NTC)
                bl, bh = [P, NTC, P], [P, NTC, TILES]
                dve.tensor_tensor(oh_lo, iota_f[:, :].unsqueeze(1).broadcast_to(bl), lo[:, cols].unsqueeze(2).broadcast_to(bl), ALU.is_equal)
                link(dve.tensor_tensor(oh_hi, iota_f[:, 0:TILES].unsqueeze(1).broadcast_to(bh), hi[:, cols].unsqueeze(2).broadcast_to(bh),
                                       ALU.is_equal))
                dve.tensor_tensor(oh_hi, oh_hi, token_s[:, cols].unsqueeze(2).broadcast_to(bh), ALU.mult).then_inc(onehot, 1)
            dve.wait_ge(tab_ps, NC // NTC)
            dve.tensor_copy(row_tok[:, :], bank[3][:, 0:TILES]).then_inc(table, 1)

            dve.wait_ge(ld_b, 32)

            def scale_rows(i):
                dve.wait_ge(g_ps, i + 1 + 2)
                for k in range(KD):
                    m = dve.tensor_scalar(g_t[:, k, :], bank[0][:, k * P:(k + 1) * P], gout[:, k:k + 1], None, ALU.mult)
                m.then_inc(g_ev, 1)

            def relu_half(j):
                e = dve.value_load(tile_e[0:1, bass.ds(j, 1)], min_val=0, max_val=E0 - 1)
                dve.wait_ge(t_ps, j + 1)
                for f in range(NF // 2, NF):
                    m = dve.tensor_scalar(act_t[:, f, :], bank[4][:, (f - 4) * P:(f - 3) * P], b1_s[:, bass.ds(e * NF + f, 1)], 0.0,
                                          ALU.add, ALU.max)
                m.then_inc(t_evd, 1)
                return e

            def add_bias(i, u, e, turn_no):
                dve.wait_ge(dn_ps, i + 1)
                dve.wait_ge(y_st[u], 16 * turn_no + 16)
                dve.tensor_tensor(y_s[u], bank[5 + u][:, 0:D], b2_s[:, bass.ds(e, 1), :].rearrange("p a d -> p (a d)"),
                                  ALU.add).then_inc(dn_ev, 1)

            def experts(tiles):
                scale_rows(0)
                with dve.Fori(0, (tiles - 1) // 2) as r:
                    for v in range(2):
                        i = 1 + 2 * r + v
                        scale_rows(i)
                        add_bias(i - 1, v, relu_half(i - 1), r)
                if tiles % 2 == 0:
                    scale_rows(tiles - 1)
                    add_bias(tiles - 2, 0, relu_half(tiles - 2), tiles // 2 - 1)
                add_bias(tiles - 1, (tiles - 1) % 2, relu_half(tiles - 1), (tiles - 1) // 2)
                dve.wait_ge(y_st[0], 16 * ((tiles + 1) // 2) + 16)

            with dve.If(general):
                experts(TILES)
            with dve.Else():
                experts(TILES_L)

            dve.wait_ge(ld_v, 16 * 13)
            bo = [64, B, E1]
            dve.tensor_tensor(cgo[0:64], cond_s.unsqueeze(2).broadcast_to(bo), wg_s.unsqueeze(1).broadcast_to(bo), ALU.mult).then_inc(cb, 1)
            dve.wait_ge(cg_ps, 1)
            dve.tensor_copy(cg.rearrange("p b e -> p (b e)"), bank[7][:, 0:B * E1]).then_inc(cg_ev, 1)
            dve.wait_ge(cg_ev, 1)
            dve.wait_ge(ld_again, 16)
            NQ = NSH + E1
            PERB = 18
            with dve.Fori(0, B) as b:
                at2 = [0]

                def clink(ins):
                    at2[0] += 1
                    ins.then_inc(gch, 1)
                    hold(dve, gch, PERB * b + at2[0])

                hold(dve, x1_ps, b + 1)
                for n in range(NB):
                    row = tokens[:, bass.ds(b * NB + n, 1), :].rearrange("p a d -> p (a d)")
                    hold(dve, got2[n], 16 * b + 16)
                    dve.tensor_tensor(x1_s[:, n, :], row, yg[n], ALU.add).then_inc(zch, 1)
                    hold(dve, zch, NB * b + n + 1)
                    dve.tensor_copy(row, x1_s[:, n, :]).then_inc(x1, 1)
                bg = [P, NB, E1]
                dve.wait_ge(rl_ps, b + 1)
                clink(dve.tensor_tensor(glog, bank[1][:, 0:NB * E1].rearrange("p (n e) -> p n e", n=NB),
                                        cg[:, bass.ds(b, 1), :].broadcast_to(bg), ALU.add))
                clink(dve.tensor_reduce(gnm, glog, AXX, ALU.max))
                dve.tensor_tensor(gex, glog, gnm.unsqueeze(2).broadcast_to(bg), ALU.subtract).then_inc(rl_sub, 1)
                hold(dve, rl_exp, b + 1)
                clink(dve.tensor_reduce(gsum, gex, AXX, ALU.add))
                clink(dve.reciprocal(grec, gsum))
                clink(dve.tensor_tensor(gsc, gex, grec.unsqueeze(2).broadcast_to(bg), ALU.mult))
                for n in range(NB):
                    clink(dve.max(gtop[:, n, :], gsc[:, n, :]))
                for n in range(NB):
                    clink(dve.max_index(top_i[:, n, :], gtop[:, n, :], gsc[:, n, :]))
                clink(dve.tensor_copy(gidx_f, top_i[:, :, :]))
                clink(dve.scalar_tensor_tensor(gwsum, gtop[:, :, 0], 1e-20, gtop[:, :, 1], ALU.add, ALU.add))
                clink(dve.reciprocal(grec, gwsum))
                clink(dve.tensor_tensor(gw2, gtop[:, :, 0:2], grec.unsqueeze(2).broadcast_to([P, NB, 2]), ALU.mult))
                io = iota_f[:, 0:E1].unsqueeze(1).broadcast_to(bg)
                for k, dst in enumerate((gone, gtwo)):
                    clink(dve.tensor_tensor(dst, io, gidx_f[:, :, k:k + 1].broadcast_to(bg), ALU.is_equal))
                    clink(dve.tensor_tensor(dst, dst, gw2[:, :, k:k + 1].broadcast_to(bg), ALU.mult))
                clink(dve.tensor_tensor(gate, gone, gtwo, ALU.add))

                def product(q):
                    dve.wait_ge(lk, NQ * b + q + 1)
                    if q >= NSH:
                        hold(dve, d_ps, (1 + E1) * b + (1 if q < 2 * NSH else q - NSH))
                    dve.scalar_tensor_tensor(mid[q % 2], leak[q % 2], 0.01, leak[q % 2], ALU.mult, ALU.max).then_inc(leaked, 1)
                    dve.wait_ge(leaked, NQ * b + q + 1)
                    dve.tensor_tensor(mid[q % 2], mid[q % 2], bank[2 + q % 2][:, S:2 * S], ALU.mult).then_inc(md, 1)

                def add_expert(q):
                    e = q - NSH
                    dve.wait_ge(d_ps, (1 + E1) * b + 2 + e)
                    dve.wait_ge(d_acc, (1 + E1) * b + 1 + e + 2)
                    for n in range(NB):
                        m = dve.scalar_tensor_tensor(acc[:, n, :], bank[4 + (1 + e) % 2][:, n * D:(n + 1) * D], gate[:, n, e:e + 1],
                                                     acc[:, n, :], ALU.mult, ALU.add)
                    m.then_inc(d_acc, 1)

                product(0)
                product(1)
                dve.wait_ge(d_ps, (1 + E1) * b + 1)
                dve.wait_ge(z_ps, b + 1)
                dve.tensor_copy(acc.rearrange("p n d -> p (n d)"), bank[4]).then_inc(d_acc, 1)
                product(2)
                for q in range(NSH, NQ):
                    if q + 1 < NQ:
                        product(q + 1)
                    add_expert(q)
                dve.wait_ge(d_acc, (1 + E1) * (b + 1) + 2)
                dve.sem_inc(yfin, 1)
                hold(dve, z_ev, b + 2)
                dve.tensor_reduce(pooled[:, :, bass.ds(b, 1)].rearrange("p k a -> p (k a)"),
                                  bank[6].rearrange("p (k t) -> p k t", k=KD), AXX, ALU.add).then_inc(pool_r, 1)
                PERB_seen = at2[0]
            assert PERB_seen == PERB, PERB_seen

            fs = [0]

            def flink(ins):
                fs[0] += 1
                ins.then_inc(fch, 1)
                dve.wait_ge(fch, fs[0])

            dve.wait_ge(fl_ps, 1)
            flink(dve.scalar_tensor_tensor(flog, bank[1][0:B, 0:E2], 1.0 / S, gb_s, ALU.mult, ALU.add))
            flink(dve.max(ftop, flog))
            dve.tensor_scalar(fnm, ftop[:, 0:1], -1.0, None, ALU.mult).then_inc(fl_sub, 1)
            flink(dve.tensor_scalar(fkeep, flog, ftop[:, 1:2], None, ALU.is_ge))
            dve.wait_ge(fl_exp, 1)
            flink(dve.tensor_tensor(fex, fex, fkeep, ALU.mult))
            flink(dve.tensor_reduce(fsum, fex, AXX, ALU.add))
            flink(dve.reciprocal(fsum, fsum))
            flink(dve.tensor_scalar(fgate, fex, fsum[:, 0:1], None, ALU.mult))
            bd = [B, B, E2]
            dve.tensor_tensor(fdiag, fgate.unsqueeze(1).broadcast_to(bd), ident[0:B, 0:B].unsqueeze(2).broadcast_to(bd),
                              ALU.mult).then_inc(fdg, 1)
            dve.wait_ge(fg_ps, 1)
            flink(dve.tensor_copy(fg_bc.rearrange("p b e -> p (b e)"), bank[7][:, 0:B * E2]))
            NE = E2 * KD
            with dve.Fori(0, B // 2) as r:
                hold(dve, r_ps, r + 1)
                for e in range(E2):
                    for oc in range(KD):
                        q = e * KD + oc
                        hold(dve, e_act, NE * r + q + 1 + 2)
                        if e:
                            hold(dve, e_acc, NE * r + q - KD + 1 + 2)
                        for half in range(2):
                            o = accf[:, oc, half * S:(half + 1) * S]
                            src = ge[q % 2][:, half * S:(half + 1) * S]
                            w = fg_bc[:, bass.ds(2 * r + half, 1), e]
                            m = (dve.scalar_tensor_tensor(o, src, w, o, ALU.mult, ALU.add) if e else
                                 dve.tensor_scalar(o, src, w, None, ALU.mult))
                        m.then_inc(e_acc, 1)
                dve.wait_ge(r_ps, r + 2)
                dve.wait_ge(stored, 16 * r + 16)
                for n in range(2):
                    m = dve.tensor_tensor(res[:, 2 * n:2 * n + 2, :], bank[4 + n].rearrange("p (a d) -> p a d", a=2),
                                          tokens[:, bass.ds(r * 2 * NB + 2 * n, 2), :], ALU.add)
                m.then_inc(r_ev, 1)


def kernel(**inputs):
    import concourse.bacc as bacc
    from concourse import mybir
    from concourse.bass_utils import run_bass_kernel_spmd

    def chunks(a, p=128):
        return a.reshape(a.shape[0] // p, p, -1).transpose(1, 0, 2)

    i = {k: np.asarray(v) for k, v in inputs.items()}
    laid = {
        "x": i["x"].reshape(4096, 256),
        "side": i["fside_16xSxS_0"],
        "cond_t": i["cond_64"].T,
        "null_kv": i["cond_64"][0:2],
        "mask": i["mask_BxS_bk0"].reshape(1, 4096),
        "g_in": i["L0_cond_g_in"].reshape(2, 128).T,
        "null_bias": i["L0_cond_null_attn_bias"],
        "wq": i["L0_cond_Wq"], "wkv": i["L0_cond_Wkv"], "wo": i["L0_cond_Wo"],
        "router_t": i["L0_ffn_router_w"].T,
        "w1": i["L0_ffn_W1"].reshape(8, 2, 128, 1024).transpose(2, 0, 1, 3).reshape(128, -1),
        "b1": i["L0_ffn_b1"].reshape(64, 128).T,
        "w2": i["L0_ffn_W2"].reshape(8, 8, 128, 256).transpose(2, 0, 1, 3).reshape(128, -1),
        "b2": i["L0_ffn_b2"],
        "wt_t": i["L1_cond_wt"].T, "wg_t": i["L1_cond_wg"].T,
        "moe_gate": chunks(i["L1_cond_w_gate"].transpose(1, 0, 2).reshape(256, 1024)),
        "moe_up": chunks(i["L1_cond_w_up"].transpose(1, 0, 2).reshape(256, 1024)),
        "moe_down": i["L1_cond_w_down"],
        "sw_gate": i["L1_cond_sw_gate"], "sw_up": i["L1_cond_sw_up"], "sw_down": i["L1_cond_sw_down"],
        "gate_w_t": i["L1_ffn_gate_w"].T, "gate_b": i["L1_ffn_gate_b"],
        "expert_w_t": i["L1_ffn_expert_w"].transpose(2, 0, 1).reshape(2, 128, 8, 256).transpose(1, 0, 2, 3),
        "expert_b_t": i["L1_ffn_expert_b"].reshape(8, 2, 128).transpose(2, 1, 0),
        "g_out": i["L0_cond_g_out"].reshape(2, 128).T,
    }
    nc = bacc.Bacc("TRN2", target_bir_lowering=False, num_devices=1)
    arrays, aps = {}, {}
    for name, a in laid.items():
        arrays[name] = np.ascontiguousarray(a)
        aps[name] = nc.dram_tensor(name, arrays[name].shape, mybir.dt.from_np(arrays[name].dtype), kind="ExternalInput").ap()
    aps["out"] = nc.dram_tensor("out", (4096, 256), mybir.dt.float32, kind="ExternalOutput").ap()
    bass_adaln_ffn_kernel(nc, **aps)
    r = run_bass_kernel_spmd(nc, [arrays], core_ids=[0])
    return r.results[0]["out"].reshape(16, 256, 256)
```

```python
import numpy as np


def bass_adaln_ffn_kernel(
    nc, x, side, cond_t, null_kv, mask, g_in, null_bias, wq, wkv, wo, router_t,
    w1, b1, w2, b2, wt_t, wg_t, moe_gate, moe_up, moe_down, sw_gate, sw_up, sw_down,
    gate_w_t, gate_b, expert_w_t, expert_b, g_out, out,
):
    from contextlib import ExitStack
    import concourse.bass as bass
    from concourse import mybir

    F32 = mybir.dt.float32
    BF16 = mybir.dt.bfloat16
    I32 = mybir.dt.int32
    U8 = mybir.dt.uint8
    ALU = mybir.AluOpType
    ACT = mybir.ActivationFunctionType
    AXX = mybir.AxisListType.X

    P = 128
    B, S, D = 16, 256, 256
    KD = D // P
    NB = S // P
    T = B * S
    NC = T // P
    H, DH = 16, 64
    INNER = H * DH
    NPAIR = H // 2
    W0, W1C = 1 + P, 1 + S
    SW = W0 + W1C
    EPS = 1e-5
    BIG = float(2.0 ** 100)
    QL = S // 4
    KEY0 = S - QL
    LW = QL + 1
    NTW = B // 2
    E0, FF = 8, 1024
    NF = FF // P
    CAPACITY = int(np.ceil(T / E0 * 1.25))
    TILES = (T + E0 * (P - 1)) // P
    TILES_L = (B * QL + E0 + E0 * (P - 1)) // P
    BITS = 3
    NSTEP = 27 // BITS
    THR0 = 0x38000000
    NCAND = 2 ** BITS - 1
    E1, M1 = 8, 128
    NSH = 2
    E2 = 8
    RT = 3
    TILES2 = -(-((2 * T + E1 * (P - 1)) // P) // RT) * RT

    ctx = ExitStack()
    with ctx:
        def sb(name, shape, dt=F32):
            return ctx.enter_context(nc.sbuf_tensor(name, shape, dt))

        def sem(name):
            return ctx.enter_context(nc.semaphore(name))

        psum = ctx.enter_context(nc.psum_tensor("psum", [P, 8, 512], F32))
        bank = [psum[:, k, :] for k in range(8)]
        tokens = sb("tokens", [P, NC, D])
        big_w = sb("big_w", [P, E0 * KD * FF])
        arena = sb("arena", [P, 23216])

        class Arena:
            def __init__(self, base):
                self.base, self.at = base, 0

            def take(self, *shape, rows=P):
                n = int(np.prod(shape))
                ap = self.base[0:rows, self.at:self.at + n]
                self.at += n
                assert self.at <= self.base.shape[1], self.at
                if len(shape) == 2:
                    ap = ap.rearrange("p (a b) -> p a b", b=shape[1])
                if len(shape) == 3:
                    ap = ap.rearrange("p (a b c) -> p a b c", b=shape[1], c=shape[2])
                return ap

        ident = sb("ident", [P, P])
        ones = sb("ones", [P, P])
        before = sb("before", [P, P])
        iota_i = sb("iota_i", [P, P], I32)
        iota_f = sb("iota_f", [P, P])
        token_i = sb("token_i", [P, NC], I32)
        rev8 = sb("rev8", [P, 8])
        ones_bf = sb("ones_bf", [1, P], BF16)
        penalty = sb("penalty", [1, B, SW], BF16)
        eps_col = sb("eps_col", [P, 1])
        gin = sb("gin", [P, KD])
        gout = sb("gout", [P, KD])
        nb_bc = sb("nb_bc", [P, H])
        xstat = sb("xstat", [P, NC, 6])
        xmv = sb("xmv", [P, NC, 2])
        rstd = sb("rstd", [P, NC])
        shift = sb("shift", [P, NC])
        router = sb("router", [P, KD, E0])

        A = Arena(arena)
        wq_s = A.take(KD, INNER)
        wkv_r = A.take(KD, 2 * DH)
        wk_s = A.take(KD, P)
        wv_s = A.take(KD, DH)
        wo_s = A.take(NPAIR, D)
        nk_col = sb("nk_col", [P, 1])
        nv_col = sb("nv_col", [P, 1])
        early_f = sb("early_f", [1, 1])
        early_i = sb("early_i", [1, 1], I32)
        L = Arena(arena)
        L.at = A.at
        bias = A.take(H, SW)
        xn = A.take(NB, D)
        xn_t = A.take(KD, 1 + S)
        q_t = A.take(NPAIR, S)
        k_t = A.take(1 + S)
        v_s = A.take(NB, DH)
        v_last = A.take(NB, DH)
        null_v = A.take(DH)
        e_first = A.take(P)
        NSIM, NPR, NPN, NPT = 4, 2, 4, 4
        sim = A.take(NSIM, SW)
        pr = A.take(NPR, SW)
        pn = A.take(NPN, SW)
        p_t = A.take(NPT, 3 * P)
        p_last = A.take(NB, 2, NPAIR)
        nmax = A.take(NSIM, 2)
        psum_row = A.take(NPR, 2)
        rinv = A.take(NPR, 2)
        at_t = A.take(NPAIR, S)
        mask_u8 = A.take(B * S // 4, rows=1).bitcast(U8)

        bias_l = L.take(NPAIR, LW)
        x_l = L.take(NTW, D)
        o_l = L.take(NTW + 1, D)
        h_l = L.take(NTW + 1, D)
        xn_l = L.take(D)
        xt_l = L.take(KD, P)
        q_l = L.take(NPAIR, P)
        k_l = L.take(2, LW)
        v_l = L.take(2, DH)
        sim_l = [L.take(NPAIR, LW) for _ in range(2)]
        ex_l = [L.take(NPAIR, LW) for _ in range(2)]
        pt_l = [L.take(NPAIR * P) for _ in range(2)]
        at_l = L.take(NPAIR, P)
        at_null = L.take(P)
        nm_l = [L.take(NPAIR) for _ in range(2)]
        rs_l = [L.take(NPAIR) for _ in range(2)]
        st_l = L.take(NTW + 1, 6)
        mv_l = L.take(NTW + 1, 2)
        rstd_l = L.take(NTW + 1)
        ht_l = tokens[:, 0:NTW + 1, :]
        pen_l = penalty[:, :, :].rearrange("p b c -> p (b c)")[:, 0:B * LW].rearrange("p (b c) -> p b c", c=LW)

        R = Arena(arena[:, E0 * NF * D:])
        omv = R.take(NC, 2)
        r_rstd = R.take(NC)
        h_n = [R.take(D) for _ in range(4)]
        h_t = [R.take(KD, P) for _ in range(2)]
        lg = R.take(NC, E0)
        lmax = R.take(NC)
        ex = R.take(NC, E0)
        esum = R.take(NC)
        prob = R.take(NC)
        hit = R.take(NC, E0)
        top = R.take(NC)
        oh = R.take(E0, NC)
        pe_key = R.take(E0, NC)
        thr = R.take(E0).bitcast(I32)
        cand = R.take(NCAND * E0).bitcast(I32).rearrange("p (k e) -> p k e", k=NCAND)
        units = sb("units", [P, NSTEP + 1, NCAND * E0], I32)
        raised = R.take(NCAND * E0).bitcast(I32).rearrange("p (k e) -> p k e", k=NCAND)
        added = R.take(E0).bitcast(I32)
        ahead = R.take(NCAND * E0).bitcast(I32).rearrange("p (k e) -> p k e", k=NCAND)
        part = R.take(E0)
        part_0 = R.take(NCAND * E0 // 2).bitcast(BF16).rearrange("p (k e) -> p k e", k=NCAND)
        one_b = R.take(P // 2).bitcast(BF16)
        even_b = R.take(P // 2).bitcast(BF16)
        cmp_s = R.base[:, R.at:R.at + NCAND * E0 * NC // 2].bitcast(BF16)
        above = R.take(E0, NC)
        tie = R.take(E0, NC)
        budget = R.take(E0)
        seg = R.take(E0, NC)
        run = R.take(E0, NC)
        rank = R.take(E0, NC)
        fin = R.take(E0, NC)
        kept = R.take(NC)
        cnt_i = sb("cnt_i", [P, E0], I32)
        ntile = R.take(E0)
        tcum = R.take(E0)
        tstart = R.take(E0)
        pos = R.take(NC)
        slot = sb("slot", [P, NC])
        reserved = sb("reserved", [P, 1])
        token_s = R.take(NC).bitcast(I32)
        tok_part = R.take(2 * NC).bitcast(I32).rearrange("p (a c) -> p a c", a=2)
        pos_i = sb("pos_i", [P, NC], I32)
        hi_i = R.take(NC).bitcast(I32)
        hi = R.take(NC)
        lo = R.take(NC)
        NTC = 8
        oh_lo = R.take(NTC * P // 2).bitcast(BF16).rearrange("p (c l) -> p c l", c=NTC)
        oh_eq = R.take(NTC * TILES // 2).bitcast(BF16).rearrange("p (c l) -> p c l", c=NTC)
        oh_hi = R.take(NTC * TILES).bitcast(BF16).rearrange("p (c a l) -> p c a l", c=NTC, a=2)
        tok_ab = R.take(2, NC)
        tab_b = R.take(TILES)
        tcmp = R.take(TILES, E0 - 1)
        tile_f = R.take(TILES)
        tile_e = sb("tile_e", [P, TILES2], I32)
        row_tok = sb("row_tok", [P, TILES2], I32)

        G = Arena(arena)
        w2_s = G.take(E0, NF, D)
        b1_s = G.take(E0 * NF)
        b2_s = G.take(E0, D)
        gath = [G.take(D) for _ in range(2)]
        g_t = G.take(KD, P)
        act1 = [G.take(FF) for _ in range(2)]
        act_t = G.take(NF, P)
        y_s = [G.take(D) for _ in range(2)]
        w1_s = big_w[:, :].rearrange("p (e k f) -> p e k f", e=E0, k=KD)
        gidx = [sb(f"gidx{k}", [P, 1], I32) for k in range(2)]

        V = Arena(tokens[:, :, :].rearrange("p c d -> p (c d)"))
        mgu_s = V.take(KD, E1, 2 * M1)
        sg_s = V.take(KD, NSH * M1)
        su_s = V.take(KD, NSH * M1)
        md_s = V.take(E1 + NSH, D)
        wt_s = V.take(KD, E1)
        wg_s = V.take(E1, rows=64)
        cond_s = V.take(B, rows=64)
        cgo = V.take(B, E1)
        cg = V.take(B, E1)
        X = Arena(big_w)
        x2 = X.take(NC, D)
        ew_s = X.take(KD, E2, D)
        eb_row = X.take(E2 * D, rows=1)
        gw_s = X.take(KD, E2)
        gb_bc = X.take(E2)
        N = Arena(arena)
        p_s = N.take(NC, D)
        yg = [N.take(NB, D) for _ in range(4)]
        x1_s = [N.take(NB, D) for _ in range(2)]
        x1_t = [N.take(KD, S) for _ in range(2)]
        oh_lo2 = [N.take(NTC * P // 2).bitcast(BF16).rearrange("p (c l) -> p c l", c=NTC) for _ in range(2)]
        oh_eq2 = N.take(NTC * TILES2 // 2).bitcast(BF16).rearrange("p (c l) -> p c l", c=NTC)
        oh_hi2 = [N.take(NTC * TILES2).bitcast(BF16).rearrange("p (c a l) -> p c a l", c=NTC, a=2) for _ in range(2)]
        tab_b2 = N.take(TILES2)
        assert N.at <= E0 * NF * D
        N.at = NC * D
        c_gath = [N.take(D) for _ in range(RT)]
        c_gt = [N.take(KD, P) for _ in range(RT)]
        c_leak = [N.take(M1) for _ in range(RT)]
        c_mid = [N.take(M1) for _ in range(RT)]
        c_midt = [N.take(M1) for _ in range(RT)]
        c_y = [N.take(D) for _ in range(RT)]
        N.at = NC * D
        yk = [N.take(2 * NB, D) for _ in range(RT)]
        z_s = [N.take(NB, D) for _ in range(RT)]
        z_t = [N.take(KD, S) for _ in range(RT)]
        ge = [N.take(NB, D) for _ in range(2)]
        res = [N.take(NB, D) for _ in range(RT)]
        pooled = N.take(KD)
        flog = N.take(E2)
        ftop = N.take(8)
        fnm = N.take(1)
        fkeep = N.take(E2)
        fex = N.take(E2)
        fsum = N.take(1)
        fgate = N.take(E2)
        gate = N.take(B, E2)
        gsort = [N.take(8) for _ in range(RT)]
        fcnt = N.take(1)
        feq = N.take(1)
        fmany = N.take(1)
        Q = Arena(arena[:, E0 * NF * D:])
        glog = Q.take(NC, E1)
        gnm = Q.take(NC)
        gex = Q.take(NC, E1)
        gsum = Q.take(NC)
        ghit = Q.take(NC, E1)
        gtop = Q.take(NC)
        m1 = Q.take(NC)
        m2 = Q.take(NC)
        oh1 = Q.take(E1, NC)
        oh2 = Q.take(E1, NC)
        both = Q.take(E1, NC)
        seg2 = Q.take(E1, NC)
        run2 = Q.take(E1, NC)
        rank2 = Q.take(E1, NC)
        prod2 = Q.take(E1, NC)
        w_k = sb("w_k", [P, 2, NC])
        pos_k = Q.take(NC, 2)
        hi_k = Q.take(NC, 2)
        lo_k = Q.take(NC, 2)
        ntile2 = Q.take(E1)
        tcum2 = Q.take(E1)
        tstart2 = Q.take(E1)
        tcmp2 = Q.take(TILES2, E1 - 1)
        tile_f2 = Q.take(TILES2)
        tok_ab2 = Q.take(2, NC)
        leak = [Q.take(S) for _ in range(NSH)]
        gu = [Q.take(2 * S) for _ in range(NSH)]
        mid = [[Q.take(S) for _ in range(NSH)] for _ in range(2)]
        token2_i = sb("token2_i", [P, NC], I32)
        pos_k_i = sb("pos_k_i", [P, NC, 2], I32)
        hi_k_i = Q.take(2 * NC).bitcast(I32).rearrange("p (c k) -> p c k", k=2)
        tok_part2 = Q.take(2 * NC).bitcast(I32).rearrange("p (a c) -> p a c", a=2)
        tile_e2, row_tok2 = tile_e, row_tok
        c_idx_s = [sb(f"c_idx{k}", [P, 1], I32) for k in range(RT)]
        a_idx_s = [sb(f"a_idx{k}", [P, NB], I32) for k in range(4)]
        d_idx_s = [sb(f"d_idx{k}", [P, 2 * NB], I32) for k in range(RT)]
        d_top = sb("d_top", [P, 8], mybir.dt.uint32)
        d_ids = [sb(f"d_ids{k}", [P, 8], I32) for k in range(RT)]
        many_i = sb("many_i", [P, 1], I32)

        h_dram = nc.dram_tensor("h_sorted_from", [T, D], F32, kind="Internal").ap()
        h_late = nc.dram_tensor("h_late", [1 + B * QL, D], F32, kind="Internal").ap()
        y_late = nc.dram_tensor("y_late", [TILES_L * P, D], F32, kind="Internal").ap()
        x1_dram = nc.dram_tensor("x1", [T, D], F32, kind="Internal").ap()
        y2_dram = nc.dram_tensor("y2_sorted", [TILES2 * P, D], F32, kind="Internal").ap()
        y_dram = nc.dram_tensor("y_sorted", [TILES * P, D], F32, kind="Internal").ap()

        ld_x = [sem(f"ld_x{k}") for k in range(4)]
        ld_w = sem("ld_w")
        ld_bias = sem("ld_bias")
        ld_wo = sem("ld_wo")
        ld_mask = sem("ld_mask")
        ld_w1 = sem("ld_w1")
        ld_w2 = sem("ld_w2")
        ld_b = sem("ld_b")
        ld_v = sem("ld_v")
        const = sem("const")
        gconst = sem("gconst")
        early = sem("early")
        gsetup = sem("gsetup")
        gch0 = sem("gch0")
        slots = sem("slots")
        l_sub = sem("l_sub")
        l_e = sem("l_e")
        l_p = sem("l_p")
        l_t = sem("l_t")
        l_tc = sem("l_tc")
        l_pv = sem("l_pv")
        l_ac = sem("l_ac")
        l_oc = sem("l_oc")
        l_ht = sem("l_ht")
        l_htc = sem("l_htc")
        l_lg = sem("l_lg")
        l_hs = sem("l_hs")
        setup = sem("setup")
        xvar = sem("xvar")
        xsd = sem("xsd")
        xnorm = sem("xnorm")
        x_ps = sem("x_ps")
        x_ev = sem("x_ev")
        k_ps = sem("k_ps")
        k_ev = sem("k_ev")
        q_ps = sem("q_ps")
        q_ev = sem("q_ev")
        v_ps = sem("v_ps")
        v_ev = sem("v_ev")
        scores = sem("scores")
        simmed = sem("simmed")
        exped = sem("exped")
        recip = sem("recip")
        normed = sem("normed")
        turned = sem("turned")
        pt_ev = sem("pt_ev")
        pv = sem("pv")
        at_ev = sem("at_ev")
        last_ps = sem("last_ps")
        at_done = sem("at_done")
        o_ps = sem("o_ps")
        o_ev = sem("o_ev")
        dch = sem("dch")
        ovar = sem("ovar")
        osd = sem("osd")
        hnorm = sem("hnorm")
        h_ps = sem("h_ps")
        h_ev = sem("h_ev")
        h_st = [sem(f"h_st{k}") for k in range(4)]
        lg_ps = sem("lg_ps")
        lsub = sem("lsub")
        lexp = sem("lexp")
        cpart = sem("cpart")
        csum = sem("csum")
        tie_in = sem("tie_in")
        tie_ps = sem("tie_ps")
        onehot = sem("onehot")
        tab_ps = sem("tab_ps")
        tab_ps2 = sem("tab_ps2")
        onehot2 = sem("onehot2")
        table = sem("table")
        idx_ok = sem("idx_ok")
        got = [sem(f"got{k}") for k in range(2)]
        g_ps = sem("g_ps")
        g_ev = sem("g_ev")
        up_ps = sem("up_ps")
        up_ev = sem("up_ev")
        t_ps = sem("t_ps")
        t_eva = sem("t_eva")
        t_evd = sem("t_evd")
        dn_ps = sem("dn_ps")
        dn_ev = sem("dn_ev")
        y_st = [sem(f"y_st{k}") for k in range(2)]
        late_qk = sem("late_qk")
        cgc = sem("cgc")
        cg_ps = sem("cg_ps")
        row_idx = sem("row_idx")
        a_add = sem("a_add")
        a_x1 = sem("a_x1")
        a_t = sem("a_t")
        a_tc = sem("a_tc")
        a_gu = sem("a_gu")
        a_lk = sem("a_lk")
        a_lkd = sem("a_lkd")
        a_md = sem("a_md")
        a_lg = sem("a_lg")
        a_d = sem("a_d")
        a_dc = sem("a_dc")
        rl_sub = sem("rl_sub")
        rl_exp = sem("rl_exp")
        c_g = sem("c_g")
        c_gc = sem("c_gc")
        c_up = sem("c_up")
        c_lk = sem("c_lk")
        c_lkd = sem("c_lkd")
        c_md = sem("c_md")
        c_mt = sem("c_mt")
        c_mtc = sem("c_mtc")
        c_dn = sem("c_dn")
        c_yc = sem("c_yc")
        d_z1 = sem("d_z1")
        d_z = sem("d_z")
        d_zt = sem("d_zt")
        d_ztc = sem("d_ztc")
        d_keep = sem("d_keep")
        d_lg = sem("d_lg")
        d_ch = sem("d_ch")
        d_sub = sem("d_sub")
        d_exp = sem("d_exp")
        d_ok = sem("d_ok")
        d_e = sem("d_e")
        d_ge = sem("d_ge")
        d_r1 = sem("d_r1")
        d_res = sem("d_res")
        d_all = sem("d_all")
        f_r = sem("f_r")
        ld_x2 = [sem(f"ld_x2{k}") for k in range(4)]
        a_got = [sem(f"a_got{k}") for k in range(4)]
        a_st = [sem(f"a_st{k}") for k in range(2)]
        c_got = [sem(f"c_got{k}") for k in range(3)]
        c_st = [sem(f"c_st{k}") for k in range(3)]
        d_got = [sem(f"d_got{k}") for k in range(3)]
        d_st = [sem(f"d_st{k}") for k in range(3)]
        held = sem("held")

        def hold(eng, s, value):
            eng.wait_ge(s, value)
            eng.sem_inc(held)


        NSETUP = 8
        NGSETUP = 6
        NCONST = 9
        NGCONST = 7
        NLD = 10

        def branch(eng):
            eng.wait_ge(early, 2)
            return eng.value_load(early_i[0:1, 0:1], min_val=0, max_val=1) == 1
        S_FREE, T_FREE, PV_FREE = 2, 2, 2

        def more_gates(eng):
            eng.wait_ge(d_all, 1)
            return eng.value_load(many_i[0:1, 0:1], min_val=0, max_val=1) == 1

        NLD2 = 11
        NLD3 = 4
        NCH = 10

        block = ctx.enter_context(nc.Block())

        SH_X, SH_T, SH_G = 2, 10, 12
        X_STOP = [1, B // 4, 3 * B // 8, B // 2]

        def up_bank(b):
            return 4 if isinstance(b, int) and b >= SH_G else 1

        def late_shared(s):
            return range(SH_G, SH_G + 2) if s == 0 else range(SH_G + 1 + s, min(SH_G + 2 + s, B))

        def shared_products(eng, b, u):
            for q in range(NSH):
                hold(eng, a_lk, 3 * (2 * b + q + 1))
                eng.tensor_tensor(leak[q], gu[q][:, 0:S], leak[q], ALU.subtract).then_inc(a_lkd, 1)
                hold(eng, a_lkd, 2 * b + q + 1)
                eng.tensor_tensor(mid[u][q], leak[q], gu[q][:, S:], ALU.mult).then_inc(a_md, 1)

        @block.sync
        def _(sp):
            for s in h_st + y_st + ld_x2:
                sp.sem_inc(s, 16)
            xr = x.rearrange("(c p) d -> p c d", p=P)
            late_x = x.rearrange("(c t s) d -> t s c d", t=2, s=S)
            late_side = side.rearrange("(j t) q k -> t q j k", t=2)

            def load_second():
                for dst, src in (
                    (wt_s, wt_t.rearrange("(k p) e -> p k e", p=P)), (wg_s, wg_t), (cond_s, cond_t),
                    (sg_s, sw_gate.rearrange("(k p) m -> p k m", p=P)), (su_s, sw_up.rearrange("(k p) m -> p k m", p=P)),
                    (md_s[:, E1:, :], sw_down.rearrange("(k p) d -> p k d", p=P)),
                    (md_s[:, 0:E1, :], moe_down.rearrange("e m d -> m e d")),
                ):
                    sp.dma_start(dst, src).then_inc(ld_v, 16)
                for k in range(KD):
                    for half, src in enumerate((moe_gate, moe_up)):
                        sp.dma_start(mgu_s[:, k, :, half * M1:(half + 1) * M1], src[:, k, :].rearrange("p (e m) -> p e m", e=E1)
                                     ).then_inc(ld_v, 16)

            sp.dma_start(mask_u8, mask).then_inc(ld_mask, 16)
            for t in range(2):
                sp.dma_start(x_l[t * QL:(t + 1) * QL, :, :], late_x[t, KEY0:S, :, :]).then_inc(ld_x[0], 16)
            for dst, src in (
                (gin[:, :], g_in), (wkv_r, wkv.rearrange("(k p) n -> p k n", p=P)),
                (wq_s, wq.rearrange("(k p) n -> p k n", p=P)), (nb_bc[:, :], null_bias.partition_broadcast(P)),
                (nk_col[0:DH, :], null_kv[0:1, :].rearrange("a d -> d a")),
                (nk_col[DH:P, :], null_kv[0:1, :].rearrange("a d -> d a")),
                (nv_col[0:DH, :], null_kv[1:2, :].rearrange("a d -> d a")),
                (nv_col[DH:P, :], null_kv[1:2, :].rearrange("a d -> d a")),
                (gout[:, :], g_out), (router[:, :, :], router_t.rearrange("(k p) e -> p k e", p=P)),
            ):
                sp.dma_start(dst, src).then_inc(ld_w, 16)
            general = branch(sp)

            with sp.If(general):
                sp.wait_ge(ld_x[0], 32)
                for k in range(4):
                    n = NC // 4
                    sp.dma_start(tokens[:, k * n:(k + 1) * n, :], xr[:, k * n:(k + 1) * n, :]).then_inc(ld_x[k], 16)
                sp.dma_start(null_v[0:1, :], null_kv[1:2, :]).then_inc(ld_bias, 16)
                sp.dma_start(bias[:, :, 1:W0], side[:, 0:P, 0:P].rearrange("h q k -> q h k")).then_inc(ld_bias, 16)
                sp.dma_start(bias[:, :, W0 + 1:SW], side[:, P:S, :].rearrange("h q k -> q h k")).then_inc(ld_bias, 16)
                sp.dma_start(wo_s, wo.rearrange("(j p) n -> p j n", p=P)).then_inc(ld_wo, 16)
                sp.dma_start(big_w[:, :], w1).then_inc(ld_w1, 16)
                sp.wait_ge(o_ps, B)
                sp.dma_start(w2_s, w2.rearrange("p (e k d) -> p e k d", e=E0, k=NF)).then_inc(ld_w2, 16)
                with sp.Fori(0, NC // 4) as r:
                    for u in range(4):
                        sp.wait_ge(hnorm, 4 * r + u + 1)
                        sp.dma_start(h_dram[bass.ds((4 * r + u) * P, P), :], h_n[u]).then_inc(h_st[u], 16)
                load_second()
            with sp.Else():
                for t in range(2):
                    rows = slice(t * QL, (t + 1) * QL)
                    sp.dma_start(bias_l[rows, :, 0:QL], late_side[t, KEY0:S, :, KEY0:S]).then_inc(ld_bias, 16)
                    sp.dma_start(v_l[QL:LW, t, :], null_kv[1:2, :]).then_inc(ld_bias, 16)
                sp.dma_start(wo_s, wo.rearrange("(j p) n -> p j n", p=P)).then_inc(ld_wo, 16)
                sp.dma_start(big_w[:, :], w1).then_inc(ld_w1, 16)
                sp.wait_ge(hnorm, NTW + 1)
                sp.dma_start(h_late[0:1, :], h_l[0:1, NTW, :]).then_inc(l_hs, 16)
                sp.dma_start(h_late[1:, :].rearrange("(c p) d -> p c d", p=P), h_l[:, 0:NTW, :]).then_inc(l_hs, 16)
                sp.wait_ge(l_lg, 1)
                sp.wait_ge(l_hs, 32)
                sp.dma_start(w2_s, w2.rearrange("p (e k d) -> p e k d", e=E0, k=NF)).then_inc(ld_w2, 16)
                load_second()
            sp.wait_ge(table, 1)
            sp.wait_ge(got[0], 16)
            sp.dma_start(b1_s, b1).then_inc(ld_b, 16)
            sp.dma_start(b2_s, b2.rearrange("e d -> (e d)").partition_broadcast(P)
                         .rearrange("p (e d) -> p e d", e=E0)).then_inc(ld_b, 16)

            def store_tiles(tiles, rows):
                def store_tile(i, u):
                    sp.wait_ge(dn_ev, i + 1 + 2)
                    sp.dma_start(rows[bass.ds(i * P, P), :], y_s[u]).then_inc(y_st[u], 16)

                store_tile(0, 0)
                with sp.Fori(0, (tiles - 1) // 2) as r:
                    for v in range(2):
                        store_tile(1 + 2 * r + v, (1 + v) % 2)
                if tiles % 2 == 0:
                    store_tile(tiles - 1, 1)
                sp.wait_ge(up_ps, tiles)

            with sp.If(general):
                store_tiles(TILES, y_dram)
            with sp.Else():
                store_tiles(TILES_L, y_late)
            def load_x(r):
                for u in range(4):
                    sp.wait_ge(ld_x2[u], 16 * r + 16)
                    c = (4 * r + u) * NB
                    sp.dma_start(x2[:, bass.ds(c, NB), :], xr[:, bass.ds(c, NB), :]).then_inc(ld_x2[u], 16)


            x1r = x1_dram.rearrange("(c p) d -> p c d", p=P)
            outr = out.rearrange("(c p) d -> p c d", p=P)

            def store_x1(r):
                for u in range(4):
                    sp.wait_ge(a_x1, 4 * r + u + 1)
                    sp.dma_start(x1r[:, bass.ds((4 * r + u) * NB, NB), :], x1_s[u % 2]).then_inc(a_st[u % 2], 16)

            load_x(0)
            with sp.Fori(1, B // 4) as r:
                load_x(r)
                store_x1(r - 1)
            store_x1(B // 4 - 1)
            for dst, src in (
                (ew_s, expert_w_t), (eb_row[0:1, :], expert_b), (gw_s, gate_w_t.rearrange("(k p) e -> p k e", p=P)),
                (gb_bc, gate_b.partition_broadcast(P)),
            ):
                sp.dma_start(dst, src).then_inc(ld_v, 16)
            with sp.Fori(0, TILES2 // RT) as r:
                for u in range(RT):
                    sp.wait_ge(c_yc, RT * r + u + 1)
                    sp.dma_start(y2_dram[bass.ds((RT * r + u) * P, P), :], c_y[u]).then_inc(c_st[u], 16)

            def store_sequence(b, u):
                sp.wait_ge(d_res, b + 1)
                sp.dma_start(outr[:, bass.ds(b * NB, NB), :], res[u]).then_inc(d_st[u], 16)

            with sp.Fori(0, B // RT) as r:
                for u in range(RT):
                    store_sequence(RT * r + u, u)
            for b in range(B - B % RT, B):
                store_sequence(b, b % RT)
            for u in range(RT):
                sp.wait_ge(d_st[u], 16 * len(range(u, B, RT)))
            with sp.If(more_gates(sp)):
                with sp.Fori(0, B) as b:
                    sp.wait_ge(d_res, B + b + 1)
                    sp.dma_start(outr[:, bass.ds(b * NB, NB), :], res[0]).then_inc(d_st[0], 16)
                sp.wait_ge(d_st[0], 16 * (len(range(0, B, RT)) + B))

        @block.gpsimd
        def _(pool):
            pool.sem_inc(normed, NPR)
            pool.memset(ident[:, :], 0.0).then_inc(const, 1)
            pool.memset(ones[:, :], 1.0).then_inc(const, 1)
            pool.memset(ones_bf[:, :], 1.0).then_inc(const, 1)
            pool.memset(eps_col[:, :], EPS).then_inc(const, 1)
            pool.memset(penalty[:, :, :], 0.0).then_inc(const, 1)
            pool.iota(iota_i[:, :], [[1, P]], base=0, channel_multiplier=0).then_inc(const, 1)
            pool.iota(token2_i[:, :], [[P, NC]], base=0, channel_multiplier=1).then_inc(const, 1)
            pool.wait_ge(const, 7)
            pool.affine_select(out=ident[:, :], in_=ident[:, :], compare_op=ALU.not_equal, fill=1.0, base=0,
                               pattern=[[-1, P]], channel_multiplier=1).then_inc(const, 1)
            pool.affine_select(out=before[:, :], in_=ones[:, :], compare_op=ALU.is_gt, fill=0.0, base=0,
                               pattern=[[1, P]], channel_multiplier=-1).then_inc(const, 1)
            for s in range(NSTEP + 1):
                for k in range(NCAND):
                    pool.memset(units[:, s, k * E0:(k + 1) * E0], (k + 1) << BITS * (NSTEP - 1 - s) if s < NSTEP else 0)
            general = branch(pool)

            def norm_head(b, s):
                g = b * H + s
                pool.wait_ge(recip, g + 1)
                hold(pool, turned, g + 1)
                if s == 0:
                    hold(pool, last_ps, b + 1)
                src, dst, ri = pr[:, s % NPR, :], pn[:, s % NPN, :], rinv[:, s % NPR, :]
                pool.tensor_tensor(p_last[:, :, s % 2, s // 2], src[:, P:SW:S + 1], ri, ALU.mult)
                pool.tensor_scalar(dst[:, 0:W0], src[:, 0:W0], ri[:, 0:1], None, ALU.mult)
                pool.tensor_scalar(dst[:, W0:SW], src[:, W0:SW], ri[:, 1:2], None, ALU.mult).then_inc(normed, 1)

            with pool.If(general):
                pool.memset(e_first[0:1, :], 0.0).then_inc(gconst, 1)
                pool.memset(xn_t[:, :, 0:1], 0.0).then_inc(gconst, 1)
                pool.memset(v_last, 0.0).then_inc(gconst, 1)
                pool.wait_ge(gconst, 3)
                pool.memset(e_first[0:1, 0:1], 1.0).then_inc(gconst, 1)
                pool.memset(slot[:, :], 1.0).then_inc(slots, 1)
                pool.iota(token_i[:, :], [[P, NC]], base=0, channel_multiplier=1).then_inc(slots, 1)
                pool.memset(reserved[:, :], 0.0).then_inc(slots, 2)
                pool.wait_ge(ld_bias, 48)
                for c0 in (1, W0 + 1 + P):
                    pool.affine_select(out=bias[:, :, c0:c0 + P], in_=bias[:, :, c0:c0 + P], compare_op=ALU.is_ge, fill=-BIG,
                                       base=0, pattern=[[0, H], [-1, P]], channel_multiplier=1).then_inc(gconst, 1)
                pool.wait_ge(gsetup, NGSETUP)
                pool.sem_inc(gconst, 1)
                with pool.Fori(0, B) as b:
                    for s in range(H):
                        norm_head(b, s)
            with pool.Else():
                pool.wait_ge(ld_bias, 64)
                pool.wait_ge(const, NCONST)
                for t in range(2):
                    if t:
                        pool.wait_ge(gconst, 1)
                    rows = bias_l[t * QL:(t + 1) * QL, :, 0:QL]
                    pool.affine_select(out=rows, in_=rows, compare_op=ALU.is_ge, fill=-BIG, base=0,
                                       pattern=[[0, NPAIR], [-1, QL]], channel_multiplier=1).then_inc(gconst, 1)
                pool.wait_ge(gconst, 2)
                pool.memset(slot[:, :], 0.0).then_inc(slots, 1)
                pool.memset(reserved[:, :], 1.0).then_inc(slots, 1)
                pool.iota(token_i[:, :], [[QL // NB, NC]], base=1 - QL // NB - (P - QL), channel_multiplier=1).then_inc(slots, 1)
                pool.wait_ge(slots, 3)
                pool.memset(slot[P - QL:P, 1:NC:NB], 1.0).then_inc(slots, 1)

            def gathers(tiles, rows):
                def gather(i, u):
                    hold(pool, g_ps, i + 1)
                    pool.tensor_copy(gidx[u][:, :], row_tok[:, bass.ds(i, 1)]).then_inc(idx_ok, 1)
                    hold(pool, idx_ok, i + 1)
                    pool.indirect_dma_start(gath[u], None, rows, bass.IndirectOffsetOnAxis(ap=gidx[u][:, 0:1], axis=0)
                                            ).then_inc(got[u], 16)

                gather(0, 0)
                with pool.Fori(0, (tiles - 1) // 2) as r:
                    for v in range(2):
                        gather(1 + 2 * r + v, (1 + v) % 2)
                if tiles % 2 == 0:
                    gather(tiles - 1, 1)
                pool.wait_ge(y_st[0], 16 * ((tiles + 1) // 2) + 16)
                pool.wait_ge(y_st[1], 16 * (tiles // 2) + 16)

            pool.wait_ge(table, 1)
            with pool.If(general):
                for u in range(4):
                    pool.wait_ge(h_st[u], 16 * (NC // 4) + 16)
                gathers(TILES, h_dram)
            with pool.Else():
                pool.wait_ge(l_hs, 32)
                gathers(TILES_L, h_late)

            def gather_rows(dst, rows, idx, done):
                pool.indirect_dma_start(dst, None, rows, bass.IndirectOffsetOnAxis(ap=idx, axis=0)).then_inc(done, 16)

            def expert_rows(rows):
                def sequence(b, u, first):
                    if not first:
                        hold(pool, a_x1, b - 3)
                    pool.tensor_copy(a_idx_s[u][:, :], pos_i[:, bass.ds(b * NB, NB)]).then_inc(row_idx, 1)
                    hold(pool, row_idx, b + 1)
                    for n in range(NB):
                        gather_rows(yg[u][:, n, :], rows, a_idx_s[u][:, n:n + 1], a_got[u])

                for b in range(4):
                    sequence(b, b, True)
                with pool.Fori(1, B // 4) as r:
                    for u in range(4):
                        sequence(4 * r + u, u, False)

            with pool.If(general):
                expert_rows(y_dram)
            with pool.Else():
                expert_rows(y_late)

            pool.wait_ge(a_md, NSH * SH_X)
            with pool.Fori(SH_X // 2, SH_T // 2) as r:
                for u in range(2):
                    shared_products(pool, 2 * r + u, u)

            pool.wait_ge(table, 2)
            for u in range(2):
                pool.wait_ge(a_st[u], 16 * (B // 2))

            def choice_rows(i, u, first):
                if not first:
                    hold(pool, c_g, i - RT + 1)
                pool.tensor_copy(c_idx_s[u][:, :], row_tok2[:, bass.ds(i, 1)]).then_inc(row_idx, 1)
                hold(pool, row_idx, B + i + 1)
                gather_rows(c_gath[u], x1_dram, c_idx_s[u][:, 0:1], c_got[u])

            for i in range(RT):
                choice_rows(i, i, True)
            for b in range(SH_T, SH_G):
                shared_products(pool, b, b % 2)
            with pool.Fori(1, TILES2 // RT) as r:
                for u in range(RT):
                    choice_rows(RT * r + u, u, False)
            for u in range(RT):
                pool.wait_ge(c_st[u], 16 * (TILES2 // RT))

            def chosen(b, u, first):
                if not first:
                    hold(pool, d_z, b - RT + 1)
                pool.tensor_copy(d_idx_s[u][:, :], pos_k_i[:, bass.ds(b * NB, NB), :].rearrange("p n k -> p (n k)")).then_inc(row_idx, 1)
                hold(pool, row_idx, B + TILES2 + b + 1)
                for m in range(2 * NB):
                    gather_rows(yk[u][:, m, :], y2_dram, d_idx_s[u][:, m:m + 1], d_got[u])

            for b in range(RT):
                chosen(b, b, True)
            with pool.Fori(1, B // RT) as r:
                for u in range(RT):
                    chosen(RT * r + u, u, False)
            for b in range(B - B % RT, B):
                chosen(b, b % RT, False)

        @block.tensor
        def _(pe):
            pe.sem_inc(turned, NPN)
            pe.sem_inc(pv, NPT)
            pe.sem_inc(last_ps, 1)
            pe.sem_inc(h_ps, 4)
            pe.sem_inc(lg_ps, 2)
            pe.sem_inc(g_ps, 2)
            b_s, b_t, b_pv, b_a, b_b = bank[0:2], bank[2:4], bank[4:6], bank[6], bank[7]

            def project_x(b, first):
                pe.wait_ge(xnorm, b + 1)
                if not first:
                    pe.wait_ge(o_ev, b)
                for k in range(KD):
                    for n in range(NB):
                        mm = pe.transpose(b_a[:, k * S + n * P:k * S + (n + 1) * P], xn[:, n, k * P:(k + 1) * P], ident[:, :])
                mm.then_inc(x_ps, 1)
                pe.wait_ge(x_ev, b + 1)
                if not first:
                    pe.wait_ge(v_ev, b)
                for k in range(KD):
                    mm = pe.matmul(b_b[:, 0:S], wk_s[:, k, :], xn_t[:, k, 1:1 + S], start=k == 0, stop=k == KD - 1)
                mm.then_inc(k_ps, 1)
                for j in range(4):
                    bk = (b_a, b_b)[j % 2]
                    if j == 1:
                        pe.wait_ge(k_ev, b + 1)
                    if j >= 2:
                        pe.wait_ge(q_ev, 4 * b + j - 1)
                    for i in range(2):
                        for k in range(KD):
                            c = (2 * j + i) * P
                            mm = pe.matmul(bk[:, i * S:(i + 1) * S], wq_s[:, k, c:c + P], xn_t[:, k, 1:1 + S],
                                           start=k == 0, stop=k == KD - 1)
                    mm.then_inc(q_ps, 1)

            def project_v(b):
                pe.wait_ge(q_ev, 4 * b + 4)
                for n in range(NB):
                    o = b_b[:, S + n * DH:S + (n + 1) * DH]
                    for k in range(KD):
                        pe.matmul(o, xn_t[:, k, n * P:(n + 1) * P], wv_s[:, k, :], start=k == 0, stop=n == 1 and k == KD - 1)
                    if n == 0:
                        pe.matmul(o, e_first[0:1, :], null_v[0:1, :], start=False, stop=True)
                for n in range(NB):
                    o = b_b[96:P, S + P + n * DH:S + P + (n + 1) * DH]
                    for k in range(KD):
                        mm = pe.matmul(o, xn_t[:, k, 97 + n * P:129 + n * P], wv_s[:, k, :], start=k == 0, stop=k == KD - 1)
                mm.then_inc(v_ps, 1)

            def qk(b, s):
                g, bk = b * H + s, b_s[s % 2]
                half = slice(DH * (s % 2), DH * (s % 2) + DH)
                if s == 0:
                    pe.wait_ge(q_ev, 4 * b + 4)
                    pe.wait_ge(k_ev, b + 1)
                hold(pe, simmed, g + 1)
                pe.matmul(bk[:, 0:SW], ones_bf[0:1, :], penalty[0:1, bass.ds(b, 1), :].rearrange("p a c -> p (a c)"),
                          start=True, stop=False)
                for c0, w, n in ((0, W0, 0), (W0, W1C, 1)):
                    mm = pe.matmul(bk[:, c0:c0 + w], q_t[half, s // 2, n * P:(n + 1) * P], k_t[half, 0:w],
                                   start=False, stop=n == NB - 1)
                mm.then_inc(scores, 1)

            def turn(b, s):
                g, bk = b * H + s, b_t[s % 2]
                pe.wait_ge(normed, g + 1 + NPR)
                pe.wait_ge(pt_ev, g + 1)
                for n, c0 in enumerate((0, W0, W0 + P)):
                    mm = pe.transpose(bk[:, n * P:(n + 1) * P], pn[:, s % NPN, c0:c0 + P], ident[:, :])
                mm.then_inc(turned, 1)

            def weigh(b, s):
                g, j = b * H + s, s // 2
                pe.wait_ge(pt_ev, g + 1 + T_FREE)
                if s == 0:
                    pe.wait_ge(v_ev, b + 1)
                if s % 4 == 0:
                    pe.wait_ge(at_ev, 4 * b + s // 4 + 1)
                o = b_pv[(s // 4) % 2][DH * (s % 2):DH * (s % 2) + DH, (j % 2) * S:(j % 2) * S + S]
                pe.matmul(o, v_s[:, 0, :], p_t[:, s % NPT, 0:S], start=True, stop=False)
                pe.matmul(o[:, P:S], v_s[:, 1, :], p_t[:, s % NPT, S:S + P], start=False, stop=True).then_inc(pv, 1)

            def last_keys(b):
                pe.wait_ge(normed, (b + 1) * H + NPR)
                pe.wait_ge(pt_ev, (b + 1) * H - 1 + T_FREE)
                for n in range(NB):
                    for hf in range(2):
                        mm = pe.matmul(b_t[0][DH * hf:DH * hf + DH, n * NPAIR:(n + 1) * NPAIR], v_last[96:P, n, :],
                                       p_last[96:P, n, hf, :], start=True, stop=True)
                mm.then_inc(last_ps, 1)

            def project_o(b):
                pe.wait_ge(at_done, b + 1)
                for n in range(NB):
                    for j in range(NPAIR):
                        mm = pe.matmul(b_a[:, n * D:(n + 1) * D], at_t[:, j, n * P:(n + 1) * P], wo_s[:, j, :],
                                       start=j == 0, stop=j == NPAIR - 1)
                mm.then_inc(o_ps, 1)

            def attend(b, more):
                for s in range(H):
                    qk(b, s)
                    if s >= 2:
                        turn(b, s - 2)
                    if s >= 3:
                        weigh(b, s - 3)
                if more:
                    project_x(b + 1, False)
                turn(b, H - 2)
                weigh(b, H - 3)
                turn(b, H - 1)
                weigh(b, H - 2)
                weigh(b, H - 1)
                last_keys(b)
                if more:
                    project_v(b + 1)
                project_o(b)

            def turn_late_x(c):
                pe.wait_ge(xnorm, c + 1)
                for k in range(KD):
                    mm = pe.transpose(bank[7][:, k * P:(k + 1) * P], xn_l[:, k * P:(k + 1) * P], ident[:, :])
                mm.then_inc(x_ps, 1)

            def project_late_kv(c):
                pe.wait_ge(x_ev, c + 1)
                for k in range(KD):
                    pe.matmul(bank[7][:, 2 * P:3 * P], wk_s[:, k, :], xt_l[:, k, :], start=k == 0, stop=k == KD - 1)
                for t in range(2):
                    for k in range(KD):
                        mm = pe.matmul(bank[7][0:QL, 3 * P + t * DH:3 * P + (t + 1) * DH], xt_l[:, k, t * QL:(t + 1) * QL],
                                       wv_s[:, k, :], start=k == 0, stop=k == KD - 1)
                mm.then_inc(k_ps, 1)

            def project_late_q(c):
                for j in range(NPAIR):
                    for k in range(KD):
                        mm = pe.matmul(bank[j // 4][:, (j % 4) * P:(j % 4 + 1) * P], wq_s[:, k, j * P:(j + 1) * P], xt_l[:, k, :],
                                       start=k == 0, stop=k == KD - 1)
                    if j % 4 == 3:
                        mm.then_inc(q_ps, 1)

            def late_scores(c, t):
                for a in range(2):
                    bk = bank[2 * t + a]
                    pe.matmul(bk[:, 0:4 * LW].rearrange("p (j w) -> p j w", w=LW), ones_bf[0:1, :],
                              pen_l[0:1, bass.ds(2 * c + t, 1), :].broadcast_to([1, 4, LW]), start=True, stop=False)
                    for j in range(4):
                        for u in range(2):
                            half = slice(u * DH, (u + 1) * DH)
                            mm = pe.matmul(bk[half, j * LW:(j + 1) * LW], q_l[half, 4 * a + j, t * QL:(t + 1) * QL],
                                           k_l[half, t, :], start=False, stop=j == 3)
                mm.then_inc(late_qk, 1)

            def turn_late(t):
                for j in range(NPAIR):
                    mm = pe.transpose(bank[4 + j // 4][0:LW, (j % 4) * P:(j % 4 + 1) * P], ex_l[t][:, j, :], ident[:, :])
                mm.then_inc(l_t, 1)

            def weigh_late(t):
                for u in range(2):
                    mm = pe.matmul(bank[6][u * DH:(u + 1) * DH, :].rearrange("p (j q) -> p j q", q=QL), v_l[0:LW, t, :],
                                   pt_l[t][0:LW, :].rearrange("p (j u q) -> p j u q", u=2, q=QL)[:, :, u, :], start=True, stop=True)
                mm.then_inc(l_pv, 1)

            def project_late_o(bk, lhs):
                for j in range(NPAIR):
                    mm = pe.matmul(bk[:, 0:D], lhs(j), wo_s[:, j, :], start=j == 0, stop=j == NPAIR - 1)
                mm.then_inc(o_ps, 1)

            def attend_late(c, first, last):
                pe.wait_ge(q_ev, 2 * c + 2)
                pe.wait_ge(k_ev, c + 1)
                late_scores(c, 0)
                if not first:
                    pe.wait_ge(l_tc, 2 * c)
                    pe.wait_ge(l_ac, 2 * c - 1)
                    weigh_late(1)
                late_scores(c, 1)
                if not last:
                    pe.wait_ge(v_ev, c + 1)
                    turn_late_x(c + 1)
                pe.wait_ge(l_sub, 2 * c + 1)
                if not first:
                    pe.wait_ge(l_ac, 2 * c)
                    project_late_o(bank[0], lambda j: at_l[:, j, :])
                pe.wait_ge(l_p, 2 * c + 1)
                turn_late(0)
                if not last:
                    project_late_kv(c + 1)
                pe.wait_ge(l_tc, 2 * c + 1)
                pe.wait_ge(v_ev, c + 1)
                weigh_late(0)
                if not last:
                    if not first:
                        pe.wait_ge(l_oc, c)
                    project_late_q(c + 1)
                pe.wait_ge(l_p, 2 * c + 2)
                turn_late(1)

            pe.wait_ge(const, NCONST)
            general = branch(pe)
            with pe.If(general):
                pe.wait_ge(gconst, NGCONST)
                pe.wait_ge(setup, NSETUP)
                project_x(0, True)
                project_v(0)
                pe.wait_ge(ld_wo, 16)
                with pe.Fori(0, B - 1) as b:
                    attend(b, True)
                attend(B - 1, False)

                pe.wait_ge(o_ev, B + 1)
                with pe.Fori(0, NC // 4) as r:
                    for half in range(2):
                        for u in (2 * half, 2 * half + 1):
                            c = 4 * r + u
                            pe.wait_ge(hnorm, c + 1)
                            pe.wait_ge(h_ev, c + 1)
                            for k in range(KD):
                                mm = pe.transpose(bank[u % 2][:, k * P:(k + 1) * P], h_n[u][:, k * P:(k + 1) * P], ident[:, :])
                            mm.then_inc(h_ps, 1)
                        for u in (2 * half, 2 * half + 1):
                            c = 4 * r + u
                            pe.wait_ge(h_ev, c + 1 + 2)
                            for k in range(KD):
                                mm = pe.matmul(bank[7][:, bass.ds(c * E0, E0)], h_t[u % 2][:, k, :], router[:, k, :],
                                               start=k == 0, stop=k == KD - 1)
                            mm.then_inc(lg_ps, 1)
            with pe.Else():
                pe.wait_ge(setup, NSETUP)
                pe.wait_ge(gsetup, 5)
                turn_late_x(0)
                project_late_kv(0)
                project_late_q(0)
                attend_late(0, True, False)
                pe.wait_ge(ld_wo, 16)
                with pe.Fori(1, NTW - 1) as c:
                    attend_late(c, False, False)
                attend_late(NTW - 1, False, True)
                pe.wait_ge(l_tc, 2 * NTW)
                pe.wait_ge(l_ac, 2 * NTW - 1)
                weigh_late(1)
                project_late_o(bank[1], lambda j: at_null)
                pe.wait_ge(l_ac, 2 * NTW)
                project_late_o(bank[0], lambda j: at_l[:, j, :])
                for c in range(NTW + 1):
                    pe.wait_ge(hnorm, c + 1)
                    if c == 0:
                        pe.wait_ge(l_oc, NTW + 1)
                    for k in range(KD):
                        mm = pe.transpose(bank[c // 2][:, (c % 2 * KD + k) * P:(c % 2 * KD + k + 1) * P], h_l[:, c, k * P:(k + 1) * P],
                                          ident[:, :])
                    if c % 2 or c == NTW:
                        mm.then_inc(l_ht, 1)
                for c in range(NTW + 1):
                    pe.wait_ge(l_htc, c // 2 + 1)
                    for t in range(2):
                        o = (bank[6][P - QL:P, (2 * c + t) * E0:(2 * c + t + 1) * E0] if c < NTW else
                             bank[7][t * QL:(t + 1) * QL, 0:E0])
                        for k in range(KD):
                            mm = pe.matmul(o, ht_l[:, c, k * P + t * QL:k * P + (t + 1) * QL], router[:, k, :],
                                           start=k == 0, stop=k == KD - 1)
                mm.then_inc(l_lg, 1)
            cols = E0 * NC
            def count(r, late):
                n = NC // NB if late else NC
                w = NCAND * E0
                for c in range(n):
                    if c % (n // 2) == 0:
                        pe.wait_ge(cpart, 2 * r + 1 + c // (n // 2))
                    if late and c == 0:
                        pe.matmul(bank[6][:, 0:w], even_b, part_0.rearrange("p k e -> p (k e)"), start=True, stop=False)
                    mm = pe.matmul(bank[6][:, 0:w], one_b, cmp_s[:, c * w:(c + 1) * w], start=c == 0 and not late, stop=c == n - 1)
                mm.then_inc(csum, 1)

            with pe.If(general):
                with pe.Fori(0, NSTEP // 3) as r:
                    for u in range(3):
                        count(3 * r + u, False)
            with pe.Else():
                with pe.Fori(0, NSTEP // 3) as r:
                    for u in range(3):
                        count(3 * r + u, True)
            pe.wait_ge(cpart, 2 * NSTEP + 1)
            pe.matmul(bank[6][:, 0:E0], ones[:, :], part, start=True, stop=True).then_inc(csum, 1)
            for n, what in enumerate((tie, above)):
                flat = what.rearrange("p e c -> p (e c)")
                pe.wait_ge(tie_in, n + 1)
                pe.matmul(bank[4][:, 0:cols], before[:, :], flat, start=True, stop=True)
                pe.matmul(bank[5][:, 0:cols], ones[:, :], flat, start=True, stop=True).then_inc(tie_ps, 1)

            def fill_table(cols):
                for m in range(cols // NTC):
                    pe.wait_ge(onehot, 2 * m + 2)
                    for c in range(NTC):
                        mm = pe.matmul(bank[3][:, 0:2 * TILES], oh_lo[:, c, :], oh_hi[:, c, :, :].rearrange("p a l -> p (a l)"), start=m + c == 0,
                                       stop=m == cols // NTC - 1 and c == NTC - 1)
                    mm.then_inc(tab_ps, 1)

            with pe.If(general):
                fill_table(NC)
            with pe.Else():
                fill_table(NC // NB)

            def numbers(cells, n):
                assert E0 == E1 == E2
                return nc.values_load_multi_w_load_instructions(
                    cells, engines=[mybir.EngineType.PE], min_val=0, max_val=E0 - 1,
                    skip_runtime_bounds_check_because="a place among 8, or how many of 7 comparisons hold")[1]

            def rows_in(i, u, turn_no):
                hold(pe, got[u], 16 * turn_no + 16)
                pe.wait_ge(g_ev, i)
                for k in range(KD):
                    mm = pe.transpose(bank[0][:, k * P:(k + 1) * P], gath[u][:, k * P:(k + 1) * P], ident[:, :])
                mm.then_inc(g_ps, 1)

            def expert_up(i, e):
                pe.wait_ge(g_ev, i + 1)
                pe.wait_ge(up_ev, i)
                for k in range(KD):
                    for f in range(2):
                        mm = pe.matmul(bank[1 + f], g_t[:, k, :],
                                       big_w[:, bass.ds(e * (KD * FF) + (k * FF + f * 512), 512)],
                                       start=k == 0, stop=k == KD - 1)
                mm.then_inc(up_ps, 1)

            def turn_up(j, u):
                pe.wait_ge(up_ev, j + 1)
                pe.wait_ge(t_eva, j + 1)
                pe.wait_ge(t_evd, j + 1)
                for f in range(NF):
                    mm = pe.transpose(bank[3 + f // 4][:, (f % 4) * P:(f % 4 + 1) * P], act1[u][:, f * P:(f + 1) * P], ident[:, :])
                mm.then_inc(t_ps, 1)

            def expert_down(j, u, e):
                pe.wait_ge(t_eva, j + 2)
                pe.wait_ge(t_evd, j + 2)
                pe.wait_ge(dn_ev, j + 1)
                for f in range(NF):
                    mm = pe.matmul(bank[5 + u][:, 0:D], act_t[:, f, :], arena[:, bass.ds(e * (NF * D) + f * D, D)],
                                   start=f == 0, stop=f == NF - 1)
                mm.then_inc(dn_ps, 1)

            pe.wait_ge(table, 1)
            pe.wait_ge(ld_w1, 16)
            pe.wait_ge(ld_w2, 16)
            def experts(tiles):
                def tile(i, v, turn_no, e_down, e_up):
                    rows_in(i, (1 + v) % 2, turn_no)
                    turn_up(i - 1, v)
                    expert_up(i, e_up)
                    expert_down(i - 1, v, e_down)

                rows_in(0, 0, 0)
                expert_up(0, numbers(tile_e[0:1, 0:1], 1)[0])
                with pe.Fori(0, (tiles - 1) // 2) as r:
                    e = numbers(tile_e[0:1, bass.ds(2 * r, 3)], 3)
                    for v in range(2):
                        tile(1 + 2 * r + v, v, r + v, e[v], e[v + 1])
                if tiles % 2 == 0:
                    e = numbers(tile_e[0:1, tiles - 2:tiles], 2)
                    tile(tiles - 1, 0, tiles // 2 - 1, e[0], e[1])
                turn_up(tiles - 1, (tiles - 1) % 2)
                expert_down(tiles - 1, (tiles - 1) % 2, numbers(tile_e[0:1, tiles - 1:tiles], 1)[0])

            with pe.If(general):
                experts(TILES)
            with pe.Else():
                experts(TILES_L)

            pe.wait_ge(ld_v, 16 * NLD2)
            pe.wait_ge(cgc, 1)
            pe.matmul(bank[6][:, 0:B * E1], ones[0:64, :], cgo[0:64].rearrange("p b e -> p (b e)"),
                      start=True, stop=True).then_inc(cg_ps, 1)

            def turn_x1(b, u):
                pe.wait_ge(a_x1, b + 1)
                if not isinstance(b, int) or b >= 2:
                    pe.wait_ge(a_tc, 2 * b - 2)
                for k in range(KD):
                    for n in range(NB):
                        mm = pe.transpose(bank[3 * u][:, k * S + n * P:k * S + (n + 1) * P], x1_s[u][:, n, k * P:(k + 1) * P], ident[:, :])
                mm.then_inc(a_t, 1)

            def choice_logits(b, u):
                pe.wait_ge(a_tc, 2 * b + 1)
                for n in range(NB):
                    for k in range(KD):
                        mm = pe.matmul(bank[7][:, bass.ds((b * NB + n) * E1, E1)], x1_t[u][:, k, n * P:(n + 1) * P], wt_s[:, k, :],
                                       start=k == 0, stop=k == KD - 1)
                mm.then_inc(a_lg, 1)

            def shared_up(b, q, first):
                if not first:
                    pe.wait_ge(a_lk, 3 * (2 * b - 1 + q))
                for half, w in enumerate((sg_s, su_s)):
                    for k in range(KD):
                        mm = pe.matmul(bank[up_bank(b) + q][:, half * S:(half + 1) * S], w[:, k, q * M1:(q + 1) * M1],
                                       p_s[:, bass.ds(b * NB + k, 1), :].rearrange("p a t -> p (a t)"), start=k == 0, stop=k == KD - 1)
                mm.then_inc(a_gu, 1)

            def shared_down(b, u):
                pe.wait_ge(a_md, 2 * b + 2)
                if not isinstance(b, int) or b > 0:
                    pe.wait_ge(a_dc, b)
                for n in range(NB):
                    for q in range(NSH):
                        mm = pe.matmul(bank[6][:, n * D:(n + 1) * D], mid[u][q][:, n * P:(n + 1) * P], md_s[:, E1 + q, :],
                                       start=q == 0, stop=q == NSH - 1)
                mm.then_inc(a_d, 1)

            def shared(b, alone=False):
                for q in range(NSH):
                    shared_up(b, q, b == 0)
                if not alone:
                    shared_down(b - 1, (b - 1) % 2)

            NT2 = 2 * NC // NTC

            def fill_table2(m, u):
                pe.wait_ge(onehot2, m + 1)
                for c in range(NTC):
                    mm = pe.matmul(bank[3][:, 0:2 * TILES2], oh_lo2[u][:, c, :], oh_hi2[u][:, c, :, :].rearrange("p a l -> p (a l)"),
                                   start=isinstance(m, int) and m + c == 0, stop=isinstance(m, int) and m == NT2 - 1 and c == NTC - 1)
                mm.then_inc(tab_ps2, 1)

            turn_x1(0, 0)
            turn_x1(1, 1)
            choice_logits(0, 0)
            for b in range(SH_X + 1):
                with pe.Fori(X_STOP[b], X_STOP[b + 1]) as r:
                    for u in range(2):
                        turn_x1(2 * r + u, u)
                        choice_logits(2 * r + u - 1, 1 - u)
                if b < SH_X:
                    shared(b, alone=b == 0)
            choice_logits(B - 1, 1)
            for b in range(SH_X, SH_X + 2):
                shared(b)
            pe.wait_ge(tie_in, 3)
            flat = both.rearrange("p e c -> p (e c)")
            pe.matmul(bank[4][:, 0:cols], before[:, :], flat, start=True, stop=True)
            pe.matmul(bank[5][:, 0:cols], ones[:, :], flat, start=True, stop=True).then_inc(tie_ps, 1)
            for b in range(SH_X + 2, SH_X + 4):
                shared(b)
            for m in range(NT2):
                fill_table2(m, m % 2)
                if m % 2 == 0:
                    shared(SH_X + 4 + m // 2)
            for b in range(SH_T, SH_G):
                shared(b)
            shared_down(SH_G - 1, (SH_G - 1) % 2)

            def choice_in(i, u, turn_no):
                hold(pe, c_got[u], 16 * turn_no + 16)
                if not isinstance(i, int) or i > 0:
                    pe.wait_ge(c_gc, i)
                for k in range(KD):
                    mm = pe.transpose(bank[0][:, k * P:(k + 1) * P], c_gath[u][:, k * P:(k + 1) * P], ident[:, :])
                mm.then_inc(c_g, 1)

            def choice_up(i, u, e):
                pe.wait_ge(c_gc, i + 1)
                if not isinstance(i, int) or i >= RT:
                    pe.wait_ge(c_md, i - RT + 1)
                for k in range(KD):
                    mm = pe.matmul(bank[2 + u][:, 0:2 * M1], c_gt[u][:, k, :],
                                   mgu_s[:, k, bass.ds(e, 1), :].rearrange("p a m -> p (a m)"), start=k == 0, stop=k == KD - 1)
                mm.then_inc(c_up, 1)

            def choice_turn(i, u):
                pe.wait_ge(c_md, i + 1)
                if not isinstance(i, int) or i > 0:
                    pe.wait_ge(c_mtc, i)
                pe.transpose(bank[1][:, 0:M1], c_mid[u], ident[:, :]).then_inc(c_mt, 1)

            def choice_down(i, u, e):
                pe.wait_ge(c_mtc, i + 1)
                if not isinstance(i, int) or i > 0:
                    pe.wait_ge(c_yc, i)
                pe.matmul(bank[5][:, 0:D], c_midt[u], md_s[:, bass.ds(e, 1), :].rearrange("p a d -> p (a d)"),
                          start=True, stop=True).then_inc(c_dn, 1)

            def choice_step(i, u, turn_no, e_down, e_up):
                static = isinstance(i, int)
                down, up = not static or 4 <= i, not static or 1 <= i < TILES2 + 1
                if not static or i < TILES2:
                    choice_in(i, u, turn_no)
                if not static or 3 <= i < TILES2 + 3:
                    choice_turn(i - 3, u)
                if down:
                    choice_down(i - 4, (u - 4) % RT, e_down)
                if up:
                    choice_up(i - 1, (u - 1) % RT, e_up)

            pe.wait_ge(table, 2)
            e = numbers(tile_e2[0:1, 0:2 * RT - 1], 2 * RT - 1)
            for i in range(2 * RT):
                choice_step(i, i % RT, i // RT, e[i - 4] if i >= 4 else None, e[i - 1] if i else None)
            with pe.Fori(2, TILES2 // RT) as r:
                e = numbers(tile_e2[0:1, bass.ds(RT * r - 4, RT + 3)], RT + 3)
                for u in range(RT):
                    choice_step(RT * r + u, u, r, e[u], e[u + 3])
            e = numbers(tile_e2[0:1, TILES2 - 4:TILES2], 4)
            for i in range(4):
                choice_step(TILES2 + i, i % RT, TILES2 // RT + i // RT, e[i], e[3])

            def turn_z(b, u):
                pe.wait_ge(d_z, b + 1)
                if not isinstance(b, int) or b > 0:
                    pe.wait_ge(d_ztc, 2 * b)
                for k in range(KD):
                    for n in range(NB):
                        mm = pe.transpose(bank[0][:, k * S + n * P:k * S + (n + 1) * P], z_s[u][:, n, k * P:(k + 1) * P], ident[:, :])
                mm.then_inc(d_zt, 1)

            def gate_logits(b):
                pe.wait_ge(d_ztc, 2 * b + 2)
                if not isinstance(b, int) or b > 0:
                    pe.wait_ge(d_ok, b)
                for k in range(KD):
                    mm = pe.matmul(bank[1][:, 0:E2], pooled[:, k:k + 1].broadcast_to([P, P]), gw_s[:, k, :],
                                   start=k == 0, stop=k == KD - 1)
                mm.then_inc(d_lg, 1)

            def gated(b, u, choice, n, e):
                if n == 0 and (not isinstance(b, int) or b > 0):
                    pe.wait_ge(d_ge, 2 * b - 1 + choice)
                o = bank[2 + choice][:, n * D:(n + 1) * D]
                for k in range(KD):
                    pe.matmul(o, z_t[u][:, k, n * P:(n + 1) * P], ew_s[:, k, bass.ds(e, 1), :].rearrange("p a d -> p (a d)"),
                              start=k == 0, stop=False)
                mm = pe.matmul(o, ones[0:1, :], eb_row[0:1, bass.ds(e * D, D)], start=False, stop=True)
                if n == NB - 1:
                    mm.then_inc(d_e, 1)

            def experts_of(b, u):
                hold(pe, d_ok, b + 1)
                return numbers(d_ids[u][0:1, 0:2], 2)

            def gated_step(b, u):
                static = isinstance(b, int)
                front, back, v = not static or b < B, not static or b >= 2, (u - 2) % RT
                if back:
                    ids = experts_of(b - 2, v)
                    gated(b - 2, v, 0, 0, ids[0])
                if front:
                    turn_z(b, u)
                if back:
                    gated(b - 2, v, 0, 1, ids[0])
                if front:
                    gate_logits(b)
                if back:
                    for n in range(NB):
                        gated(b - 2, v, 1, n, ids[1])

            pe.wait_ge(c_yc, TILES2)
            pe.wait_ge(ld_v, 16 * (NLD2 + NLD3))
            for b in range(RT):
                for s in late_shared(b):
                    shared(s, alone=s == SH_G)
                gated_step(b, b)
            shared_down(B - 1, (B - 1) % 2)
            with pe.Fori(1, B // RT) as r:
                for u in range(RT):
                    gated_step(RT * r + u, u)
            for b in range(B - B % RT, B + 2):
                gated_step(b, b % RT)

            def every_expert(b, first):
                pe.wait_ge(d_keep, B + b + 1)
                for e in range(E2):
                    if not first or e >= 2:
                        pe.wait_ge(d_ge, 2 * B + E2 * b + e - 1)
                    for n in range(NB):
                        o = bank[2 + e % 2][:, n * D:(n + 1) * D]
                        for k in range(KD):
                            pe.matmul(o, z_t[0][:, k, n * P:(n + 1) * P], ew_s[:, k, e, :], start=k == 0, stop=False)
                        mm = pe.matmul(o, ones[0:1, :], eb_row[0:1, e * D:(e + 1) * D], start=False, stop=True)
                    mm.then_inc(d_e, 1)

            with pe.If(more_gates(pe)):
                every_expert(0, True)
                with pe.Fori(1, B) as b:
                    every_expert(b, False)

        @block.scalar
        def _(act):
            act.sem_inc(exped, NSIM)
            act.sem_inc(o_ev, 1)
            act.sem_inc(t_eva, 1)
            act.sem_inc(h_ev, 2)
            b_a, b_b = bank[6], bank[7]
            def copies(b):
                act.wait_ge(x_ps, b + 1)
                act.copy(xn_t[:, :, 1:1 + S], b_a.rearrange("p (k t) -> p k t", k=KD)).then_inc(x_ev, 1)
                act.wait_ge(k_ps, b + 1)
                act.copy(k_t[:, 1:1 + S], b_b[:, 0:S]).then_inc(k_ev, 1)
                for j in range(4):
                    act.wait_ge(q_ps, 4 * b + j + 1)
                    act.copy(q_t[:, 2 * j:2 * j + 2, :], (b_a, b_b)[j % 2].rearrange("p (a t) -> p a t", a=2)).then_inc(q_ev, 1)

            def attend(b, more):
                for s in range(H):
                    g = b * H + s
                    act.wait_ge(normed, g + 1)
                    act.wait_ge(simmed, g + 1 + S_FREE)
                    for n, (c0, c1) in enumerate(((0, W0), (W0, SW))):
                        a = act.activation(pr[:, s % NPR, c0:c1], sim[:, s % NSIM, c0:c1], ACT.Exp,
                                           bias=nmax[:, s % NSIM, n:n + 1], scale=-1.0,
                                           accum_out=psum_row[:, s % NPR, n:n + 1])
                    a.then_inc(exped, 1)
                if more:
                    copies(b + 1)
                hold(act, o_ps, b + 1)
                act.copy(tokens[:, bass.ds(b * NB, NB), :], b_a.rearrange("p (n d) -> p n d", n=NB)).then_inc(o_ev, 1)

            def attend_late(c, first, last):
                if not first:
                    act.wait_ge(l_pv, 2 * c)
                    act.copy(at_l[:, :, QL:P], bank[6].rearrange("p (j q) -> p j q", q=QL)).then_inc(l_ac, 1)
                act.wait_ge(k_ev, c + 1)
                act.copy(v_l[0:QL, :, :], bank[7][0:QL, 3 * P:4 * P].rearrange("p (t d) -> p t d", t=2)).then_inc(v_ev, 1)
                act.wait_ge(l_sub, 2 * c + 1)
                act.activation(ex_l[0], sim_l[0], ACT.Exp).then_inc(l_e, 1)
                if not last:
                    act.wait_ge(x_ps, c + 2)
                    act.copy(xt_l, bank[7][:, 0:D].rearrange("p (k t) -> p k t", k=KD)).then_inc(x_ev, 1)
                act.wait_ge(l_sub, 2 * c + 2)
                act.activation(ex_l[1], sim_l[1], ACT.Exp).then_inc(l_e, 1)
                if not first:
                    act.wait_ge(o_ps, c)
                    act.copy(o_l[:, bass.ds(c - 1, 1), :].rearrange("p a d -> p (a d)"), bank[0][:, 0:D]).then_inc(l_oc, 1)
                act.wait_ge(l_t, 2 * c + 1)
                act.copy(pt_l[0][0:LW, :].rearrange("p (a t) -> p a t", a=2), psum[0:LW, 4:6, :]).then_inc(l_tc, 1)
                act.wait_ge(l_pv, 2 * c + 1)
                act.copy(at_l[:, :, 0:QL], bank[6].rearrange("p (j q) -> p j q", q=QL)).then_inc(l_ac, 1)
                if not last:
                    late_queries(c + 1)
                act.wait_ge(l_t, 2 * c + 2)
                act.copy(pt_l[1][0:LW, :].rearrange("p (a t) -> p a t", a=2), psum[0:LW, 4:6, :]).then_inc(l_tc, 1)

            def late_queries(c):
                for a in range(2):
                    act.wait_ge(q_ps, 2 * c + a + 1)
                    act.copy(q_l[:, 4 * a:4 * a + 4, :], bank[a].rearrange("p (j t) -> p j t", j=4)).then_inc(q_ev, 1)

            act.wait_ge(const, NCONST)
            general = branch(act)
            with act.If(general):
                act.wait_ge(xvar, 1)
                act.activation(rstd[:, :], xmv[:, :, 1], ACT.Sqrt, bias=eps_col[:, 0:1]).then_inc(xsd, 1)
                act.wait_ge(setup, NSETUP)
                copies(0)
                with act.Fori(0, B - 1) as b:
                    attend(b, True)
                attend(B - 1, False)

                act.wait_ge(ovar, 1)
                act.activation(r_rstd, omv[:, :, 1], ACT.Sqrt, bias=eps_col[:, 0:1]).then_inc(osd, 1)
                with act.Fori(0, NC // 4) as r:
                    for u in range(4):
                        c = 4 * r + u
                        act.wait_ge(lg_ps, c + 1)
                        act.wait_ge(h_ps, c + 1 + 4)
                        act.copy(h_t[u % 2], bank[u % 2][:, 0:D].rearrange("p (k t) -> p k t", k=KD)).then_inc(h_ev, 1)
            with act.Else():
                act.wait_ge(xvar, 1)
                act.activation(rstd_l[:, 0:NTW], mv_l[:, 0:NTW, 1], ACT.Sqrt, bias=eps_col[:, 0:1]).then_inc(xsd, 1)
                act.wait_ge(x_ps, 1)
                act.copy(xt_l, bank[7][:, 0:D].rearrange("p (k t) -> p k t", k=KD)).then_inc(x_ev, 1)
                late_queries(0)
                attend_late(0, True, False)
                with act.Fori(1, NTW - 1) as c:
                    attend_late(c, False, False)
                attend_late(NTW - 1, False, True)
                act.wait_ge(l_pv, 2 * NTW)
                act.copy(at_l[:, :, QL:P], bank[6].rearrange("p (j q) -> p j q", q=QL)).then_inc(l_ac, 1)
                act.wait_ge(o_ps, NTW)
                act.copy(o_l[:, NTW, :], bank[1][:, 0:D]).then_inc(l_oc, 1)
                act.wait_ge(o_ps, NTW + 1)
                act.copy(o_l[:, NTW - 1, :], bank[0][:, 0:D]).then_inc(l_oc, 1)
                act.wait_ge(ovar, 1)
                act.activation(rstd_l, mv_l[:, :, 1], ACT.Sqrt, bias=eps_col[:, 0:1]).then_inc(osd, 1)
                for m in range((NTW + 2) // 2):
                    n = min(2, NTW + 1 - 2 * m)
                    act.wait_ge(l_ht, m + 1)
                    act.copy(ht_l[:, 2 * m:2 * m + n, :], bank[m][:, 0:n * D].rearrange("p (c d) -> p c d", c=n)).then_inc(l_htc, 1)
            act.wait_ge(lsub, 1)
            act.activation(ex, ex, ACT.Exp).then_inc(lexp, 1)

            act.wait_ge(ld_b, 32)
            act.wait_ge(table, 1)

            def up_copy(i, u):
                act.wait_ge(up_ps, i + 1)
                act.copy(act1[u].rearrange("p (a f) -> p a f", a=2), psum[:, 1:3, :]).then_inc(up_ev, 1)

            def relu_half(j):
                e = act.value_load(tile_e[0:1, bass.ds(j, 1)], min_val=0, max_val=E0 - 1)
                hold(act, t_ps, j + 1)
                for f in range(NF // 2):
                    a = act.activation(act_t[:, f, :], bank[3][:, f * P:(f + 1) * P], ACT.Relu,
                                       bias=b1_s[:, bass.ds(e * NF + f, 1)])
                a.then_inc(t_eva, 1)

            def experts(tiles):
                up_copy(0, 0)
                with act.Fori(0, (tiles - 1) // 2) as r:
                    for v in range(2):
                        relu_half(2 * r + v)
                        up_copy(1 + 2 * r + v, (1 + v) % 2)
                if tiles % 2 == 0:
                    relu_half(tiles - 2)
                    up_copy(tiles - 1, 1)
                relu_half(tiles - 1)

            with act.If(general):
                experts(TILES)
            with act.Else():
                experts(TILES_L)

            def copy_x1(b, u):
                act.wait_ge(a_t, b + 1)
                src = bank[3 * u].rearrange("p (k t) -> p k t", k=KD)
                act.copy(x1_t[u], src).then_inc(a_tc, 1)
                act.copy(p_s[:, bass.ds(b * NB, NB), :], src).then_inc(a_tc, 1)

            def copy_shared(b):
                act.wait_ge(a_d, b + 1)
                act.copy(p_s[:, bass.ds(b * NB, NB), :], bank[6].rearrange("p (n d) -> p n d", n=NB)).then_inc(a_dc, 1)

            def shared(b, alone=False):
                first = isinstance(b, int) and b == 0
                for q in range(NSH):
                    if not first:
                        act.wait_ge(a_md, 2 * b - 1 + q)
                    hold(act, a_gu, 2 * b + q + 1)
                    up = bank[up_bank(b) + q]
                    act.activation(leak[q], up[:, 0:S], ACT.Relu, scale=-0.01).then_inc(a_lk, 1)
                    act.activation(gu[q][:, 0:S], up[:, 0:S], ACT.Relu).then_inc(a_lk, 1)
                    act.copy(gu[q][:, S:], up[:, S:]).then_inc(a_lk, 1)
                if not alone:
                    copy_shared(b - 1)

            for b in range(SH_X + 1):
                with act.Fori(X_STOP[b] if b else 0, X_STOP[b + 1]) as r:
                    for u in range(2):
                        copy_x1(2 * r + u, u)
                if b < SH_X:
                    shared(b, alone=b == 0)
            act.wait_ge(rl_sub, 1)
            act.activation(gex, gex, ACT.Exp, scale=0.5).then_inc(rl_exp, 1)
            with act.Fori(SH_X, SH_G) as b:
                shared(b)
            copy_shared(SH_G - 1)

            def choice_step(i, u, turn_no):
                static = isinstance(i, int)
                if not static or i < TILES2:
                    act.wait_ge(c_g, i + 1)
                    act.copy(c_gt[u], bank[0][:, 0:D].rearrange("p (k t) -> p k t", k=KD)).then_inc(c_gc, 1)
                if not static or 4 <= i:
                    w = (u - 4) % RT
                    if not static or i - 4 >= RT:
                        hold(act, c_st[w], 16 * (turn_no - (2 if u == 0 else 1)))
                    hold(act, c_dn, i - 3)
                    act.copy(c_y[w], bank[5][:, 0:D]).then_inc(c_yc, 1)
                if not static or 1 <= i < TILES2 + 1:
                    v = (u - 1) % RT
                    act.wait_ge(c_up, i)
                    act.copy(c_leak[v], bank[2 + v][:, 0:M1]).then_inc(c_lk, 1)

            for i in range(3 * RT):
                choice_step(i, i % RT, i // RT)
            with act.Fori(3, TILES2 // RT) as r:
                for u in range(RT):
                    choice_step(RT * r + u, u, r)
            for i in range(TILES2, TILES2 + 4):
                choice_step(i, i % RT, i // RT)

            def copy_z(b, u):
                act.wait_ge(d_zt, b + 1)
                for k in range(KD):
                    act.activation(z_t[u][:, k, :], bank[0][:, k * S:(k + 1) * S], ACT.Copy,
                                   accum_out=pooled[:, k:k + 1]).then_inc(d_ztc, 1)

            def gates(b):
                act.wait_ge(d_sub, b + 1)
                act.activation(fex, flog, ACT.Exp, bias=fnm[:, 0:1]).then_inc(d_exp, 1)

            def gelu(b, c):
                act.wait_ge(d_e, 2 * b + c + 1)
                if not isinstance(b, int) or b > 0:
                    act.wait_ge(d_r1 if c == 0 else d_res, b)
                act.activation(ge[c].rearrange("p n d -> p (n d)"), bank[2 + c], ACT.Gelu).then_inc(d_ge, 1)

            def keep_z(b, u):
                act.wait_ge(d_ztc, 2 * b + 2)
                act.copy(p_s[:, bass.ds(b * NB, NB), :], z_t[u]).then_inc(d_keep, 1)

            def gated_step(b, u):
                static = isinstance(b, int)
                front, back = not static or b < B, not static or b >= 2
                if front:
                    copy_z(b, u)
                if back:
                    gelu(b - 2, 0)
                if front:
                    gates(b)
                if back:
                    gelu(b - 2, 1)
                if front:
                    keep_z(b, u)

            for b in range(RT):
                for s in late_shared(b):
                    shared(s, alone=s == SH_G)
                gated_step(b, b)
            copy_shared(B - 1)
            with act.Fori(1, B // RT) as r:
                for u in range(RT):
                    gated_step(RT * r + u, u)
            for b in range(B - B % RT, B + 2):
                gated_step(b, b % RT)

            def every_expert(b, first):
                if not first:
                    act.wait_ge(d_e, 2 * B + E2 * b)
                act.copy(z_t[0], p_s[:, bass.ds(b * NB, NB), :]).then_inc(d_keep, 1)
                for e in range(E2):
                    act.wait_ge(d_e, 2 * B + E2 * b + e + 1)
                    if not first or e >= 2:
                        act.wait_ge(f_r, E2 * b + e - 1)
                    act.activation(ge[e % 2].rearrange("p n d -> p (n d)"), bank[2 + e % 2], ACT.Gelu).then_inc(d_ge, 1)

            with act.If(more_gates(act)):
                act.wait_ge(d_keep, B)
                every_expert(0, True)
                with act.Fori(1, B) as b:
                    every_expert(b, False)

        @block.vector
        def _(dve):
            dve.sem_inc(simmed, S_FREE)
            dve.sem_inc(pt_ev, T_FREE)
            dve.sem_inc(at_ev, PV_FREE)
            dve.sem_inc(dn_ev, 2)
            dve.sem_inc(t_evd, 1)
            b_s, b_t, b_pv, b_a, b_b = bank[0:2], bank[2:4], bank[4:6], bank[6], bank[7]

            dve.wait_ge(ld_mask, 16)
            mv = mask_u8.rearrange("p (b s) -> p b s", b=B)
            dve.tensor_reduce(early_f[:, :], mv[:, :, 0:KEY0], mybir.AxisListType.XY, ALU.max).then_inc(early, 1)
            dve.wait_ge(early, 1)
            dve.tensor_copy(early_i[:, :], early_f[:, :]).then_inc(early, 1)
            def scale_weights():
                dve.wait_ge(const, NCONST)
                dve.tensor_copy(iota_f[:, :], iota_i[:, :]).then_inc(setup, 1)
                dve.tensor_scalar(rev8[:, :], iota_i[:, 0:8], -1.0, 8.0, ALU.mult, ALU.add).then_inc(setup, 1)
                dve.wait_ge(ld_w, 16 * NLD)
                for k in range(KD):
                    dve.tensor_scalar(wq_s[:, k, :], wq_s[:, k, :], gin[:, k:k + 1], DH ** -0.5, ALU.mult, ALU.mult).then_inc(setup, 1)
                    for half in range(2):
                        dve.tensor_scalar(wk_s[:, k, half * DH:(half + 1) * DH], wkv_r[:, k, 0:DH], gin[:, k:k + 1], None,
                                          ALU.mult)
                    dve.tensor_scalar(wv_s[:, k, :], wkv_r[:, k, DH:], gin[:, k:k + 1], None, ALU.mult).then_inc(setup, 1)
                    dve.tensor_scalar(router[:, k, :], router[:, k, :], gout[:, k:k + 1], None, ALU.mult).then_inc(setup, 1)

            def general_setup():
                scale_weights()
                for k in range(4):
                    dve.wait_ge(ld_x[k], 48 if k == 0 else 16)
                    for c in range(k * NC // 4, (k + 1) * NC // 4):
                        st = dve.bn_stats(xstat[:, c, :], tokens[:, c, :])
                st.then_inc(gch0, 1)
                dve.wait_ge(gch0, 1)
                for c in range(NC):
                    st = dve.bn_aggr(xmv[:, c, :], xstat[:, c, :])
                st.then_inc(xvar, 1)
                dve.wait_ge(ld_bias, 48)
                dve.tensor_copy(k_t[:, 0:1], nk_col[:, :]).then_inc(gsetup, 1)
                for c0 in (0, W0):
                    dve.tensor_copy(bias[:, :, c0], nb_bc[:, :]).then_inc(gsetup, 1)
                dve.tensor_scalar(penalty[:, :, 1:W0], mv[:, :, 0:P], BIG, -BIG, ALU.mult, ALU.add).then_inc(gsetup, 1)
                dve.tensor_scalar(penalty[:, :, W0 + 1:SW], mv, BIG, -BIG, ALU.mult, ALU.add).then_inc(gsetup, 1)
                dve.wait_ge(xsd, 1)
                dve.reciprocal(rstd[:, :], rstd[:, :]).then_inc(gsetup, 1)
                dve.wait_ge(gsetup, NGSETUP)
                dve.scalar_tensor_tensor(shift[:, :], xmv[:, :, 0], -1.0, rstd[:, :], ALU.mult, ALU.mult).then_inc(gch0, 1)
                dve.wait_ge(gch0, 2)

            def normalise_x(b, first):
                if not first:
                    dve.wait_ge(x_ps, b)
                for n in range(NB):
                    c = b * NB + n
                    i = dve.tensor_scalar(xn[:, n, :], tokens[:, bass.ds(c, 1), :].rearrange("p a d -> p (a d)"),
                                          rstd[:, bass.ds(c, 1)], shift[:, bass.ds(c, 1)], ALU.mult, ALU.add)
                i.then_inc(xnorm, 1)

            def copy_v(b):
                dve.wait_ge(v_ps, b + 1)
                dve.tensor_copy(v_last[96:P, :, :], b_b[96:P, S + P:2 * S].rearrange("p (n d) -> p n d", n=NB))
                dve.tensor_copy(v_s[:, :, :], b_b[:, S:S + P].rearrange("p (n d) -> p n d", n=NB)).then_inc(v_ev, 1)

            def biased(b, s):
                g = b * H + s
                dve.wait_ge(exped, g + 1)
                hold(dve, scores, g + 1)
                for n, (c0, c1) in enumerate(((0, W0), (W0, SW))):
                    i = dve.tensor_tensor_reduce(sim[:, s % NSIM, c0:c1], b_s[s % 2][:, c0:c1], bias[:, s, c0:c1], -1.0, 3e38,
                                                 ALU.add, ALU.min, nmax[:, s % NSIM, n:n + 1])
                i.then_inc(simmed, 1)

            def invert(b, s):
                g = b * H + s
                dve.wait_ge(normed, g + 1)
                dve.wait_ge(exped, g + 1 + NSIM)
                dve.reciprocal(rinv[:, s % NPR, :], psum_row[:, s % NPR, :]).then_inc(recip, 1)

            def copy_pt(b, s):
                g = b * H + s
                dve.wait_ge(turned, g + 1 + NPN)
                dve.wait_ge(pv, g + 1)
                dve.tensor_copy(p_t[:, s % NPT, :], b_t[s % 2][:, 0:3 * P]).then_inc(pt_ev, 1)

            def copy_at(b, k):
                dve.wait_ge(pv, b * H + 4 * k + 4 + NPT)
                dve.tensor_copy(at_t[:, 2 * k:2 * k + 2, :], b_pv[k % 2].rearrange("p (a t) -> p a t", a=2)).then_inc(at_ev, 1)

            def attend(b, more):
                for s in range(H):
                    biased(b, s)
                    if s >= 1:
                        invert(b, s - 1)
                    if s >= 2:
                        copy_pt(b, s - 2)
                    if s >= 7 and s % 4 == 3:
                        copy_at(b, (s - 7) // 4)
                    if s == 8 and more:
                        normalise_x(b + 1, False)
                invert(b, H - 1)
                copy_pt(b, H - 2)
                copy_pt(b, H - 1)
                copy_at(b, 3)
                dve.wait_ge(last_ps, b + 2)
                dve.wait_ge(at_ev, 4 * b + 4 + PV_FREE)
                dve.tensor_tensor(at_t[:, :, P - 1:S:P], at_t[:, :, P - 1:S:P],
                                  b_t[0][:, 0:NB * NPAIR].rearrange("p (n j) -> p j n", n=NB), ALU.add).then_inc(at_done, 1)
                if more:
                    copy_v(b + 1)
            def normalise_late(c):
                row = x_l[:, bass.ds(c, 1), :].rearrange("p a d -> p (a d)")
                dve.tensor_scalar(xn_l, row, mv_l[:, bass.ds(c, 1), 0], rstd_l[:, bass.ds(c, 1)], ALU.subtract, ALU.mult).then_inc(xnorm, 1)

            def late_keys(c):
                dve.wait_ge(k_ps, c + 1)
                dve.tensor_copy(k_l[:, :, 0:QL], bank[7][:, 2 * P:3 * P].rearrange("p (t s) -> p t s", t=2)).then_inc(k_ev, 1)

            def attend_late(c, first, last):
                at = [0]

                def llink(ins):
                    at[0] += 1
                    ins.then_inc(gch0, 1)
                    hold(dve, gch0, LDV0 + LDV * c + at[0])

                def biased_late(t):
                    hold(dve, late_qk, 2 * c + t + 1)
                    llink(dve.tensor_tensor(sim_l[t].rearrange("p (a j) w -> p a j w", a=2),
                                            psum[:, 2 * t:2 * t + 2, 0:4 * LW].rearrange("p a (j w) -> p a j w", w=LW),
                                            bias_l.rearrange("p (a j) w -> p a j w", a=2), ALU.add))
                    llink(dve.tensor_reduce(nm_l[t], sim_l[t], AXX, ALU.max))
                    dve.tensor_tensor(sim_l[t], sim_l[t], nm_l[t].unsqueeze(2).broadcast_to([P, NPAIR, LW]),
                                      ALU.subtract).then_inc(l_sub, 1)

                def probs(t):
                    hold(dve, l_e, 2 * c + t + 1)
                    llink(dve.tensor_reduce(rs_l[t], ex_l[t], AXX, ALU.add))
                    llink(dve.reciprocal(rs_l[t], rs_l[t]))
                    dve.tensor_tensor(ex_l[t], ex_l[t], rs_l[t].unsqueeze(2).broadcast_to([P, NPAIR, LW]),
                                      ALU.mult).then_inc(l_p, 1)

                if not last:
                    hold(dve, x_ps, c + 1)
                    normalise_late(c + 1)
                biased_late(0)
                biased_late(1)
                probs(0)
                if not first:
                    hold(dve, l_oc, c)
                    dve.bn_stats(st_l[:, bass.ds(c - 1, 1), :].rearrange("p a s -> p (a s)"),
                                 o_l[:, bass.ds(c - 1, 1), :].rearrange("p a d -> p (a d)"))
                probs(1)
                if not last:
                    late_keys(c + 1)
                assert at[0] == LDV

            LDV = 8
            LDV0 = 2

            def late_attention():
                dve.wait_ge(ld_x[0], 32)
                for c in range(NTW):
                    st = dve.bn_stats(st_l[:, c, :], x_l[:, c, :])
                st.then_inc(gch0, 1)
                dve.wait_ge(gch0, 1)
                for c in range(NTW):
                    st = dve.bn_aggr(mv_l[:, c, :], st_l[:, c, :])
                st.then_inc(xvar, 1)
                scale_weights()
                for t in range(2):
                    dve.tensor_copy(bias_l[t * DH:(t + 1) * DH, :, QL], nb_bc[t * DH:(t + 1) * DH, t:H:2]).then_inc(gsetup, 1)
                dve.tensor_copy(k_l[:, :, QL], nk_col[:, 0:1].broadcast_to([P, 2])).then_inc(gsetup, 1)
                dve.tensor_scalar(at_null, ones[:, :], nv_col[:, 0:1], None, ALU.mult).then_inc(gsetup, 1)
                dve.tensor_scalar(pen_l[:, :, 0:QL], mv[:, :, KEY0:S], BIG, -BIG, ALU.mult, ALU.add).then_inc(gsetup, 1)
                dve.wait_ge(xsd, 1)
                dve.reciprocal(rstd_l[:, 0:NTW], rstd_l[:, 0:NTW]).then_inc(gch0, 1)
                dve.wait_ge(gch0, 2)
                normalise_late(0)
                late_keys(0)
                dve.wait_ge(gconst, 2)
                dve.wait_ge(gsetup, 5)
                attend_late(0, True, False)
                with dve.Fori(1, NTW - 1) as c:
                    attend_late(c, False, False)
                attend_late(NTW - 1, False, True)
                end = LDV0 + LDV * NTW
                for k, c in enumerate((NTW, NTW - 1)):
                    dve.wait_ge(l_oc, NTW + k)
                    st = dve.bn_stats(st_l[:, c, :], o_l[:, c, :])
                st.then_inc(gch0, 1)
                dve.wait_ge(gch0, end + 1)
                for c in range(NTW + 1):
                    st = dve.bn_aggr(mv_l[:, c, :], st_l[:, c, :])
                st.then_inc(ovar, 1)
                dve.wait_ge(osd, 1)
                dve.reciprocal(rstd_l, rstd_l).then_inc(gch0, 1)
                dve.wait_ge(gch0, end + 2)
                for c in range(NTW + 1):
                    dve.tensor_scalar(h_l[:, c, :], o_l[:, c, :], mv_l[:, c, 0:1], rstd_l[:, c:c + 1], ALU.subtract, ALU.mult).then_inc(hnorm, 1)
                dve.wait_ge(l_lg, 1)
                dve.tensor_copy(lg, bank[7][:, 0:E0].unsqueeze(1).broadcast_to([P, NC, E0])).then_inc(gch0, 1)
                dve.wait_ge(gch0, end + 3)
                dve.tensor_copy(lg[P - QL:P, 1:NC:NB, :], bank[6][P - QL:P, 0:B * E0].rearrange("p (b e) -> p b e", b=B)).then_inc(gch0, 1)
                dve.wait_ge(gch0, end + 4)

            general = branch(dve)
            with dve.If(general):
                general_setup()
                normalise_x(0, True)
                copy_v(0)
                with dve.Fori(0, B - 1) as b:
                    attend(b, True)
                attend(B - 1, False)

                dve.wait_ge(o_ev, B + 1)
                for c in range(NC):
                    i = dve.bn_stats(xstat[:, c, :], tokens[:, c, :])
                i.then_inc(gch0, 1)
                dve.wait_ge(gch0, 3)
                for c in range(NC):
                    i = dve.bn_aggr(omv[:, c, :], xstat[:, c, :])
                i.then_inc(ovar, 1)
                dve.wait_ge(osd, 1)
                dve.reciprocal(r_rstd, r_rstd).then_inc(gch0, 1)
                dve.wait_ge(gch0, 4)
                dve.wait_ge(o_ev, B + 1)
                with dve.Fori(0, NC // 4) as r:
                    for u in range(4):
                        c = 4 * r + u
                        dve.wait_ge(h_ps, c + 1)
                        dve.wait_ge(h_st[u], 16 * r + 16)
                        dve.tensor_scalar(h_n[u], tokens[:, bass.ds(c, 1), :].rearrange("p a d -> p (a d)"),
                                          omv[:, bass.ds(c, 1), 0], r_rstd[:, bass.ds(c, 1)], ALU.subtract, ALU.mult).then_inc(hnorm, 1)
                dve.wait_ge(lg_ps, NC + 2)
                dve.tensor_copy(lg, bank[7][:, 0:NC * E0].rearrange("p (c e) -> p c e", e=E0)).then_inc(gch0, 1)
                dve.wait_ge(gch0, 5)
            with dve.Else():
                late_attention()

            steps = [0]

            def link(ins):
                steps[0] += 1
                ins.then_inc(dch, 1)
                dve.wait_ge(dch, steps[0])

            link(dve.tensor_reduce(lmax, lg, AXX, ALU.max))
            bc = [P, NC, E0]
            bt = [P, E0, NC]
            dve.tensor_tensor(ex, lg, lmax.unsqueeze(2).broadcast_to(bc), ALU.subtract).then_inc(lsub, 1)
            link(dve.tensor_tensor(hit, lg, lmax.unsqueeze(2).broadcast_to(bc), ALU.is_equal))
            link(dve.tensor_tensor(hit, hit, rev8[:, :].unsqueeze(1).broadcast_to(bc), ALU.mult))
            link(dve.tensor_reduce(top, hit, AXX, ALU.max))
            link(dve.tensor_tensor(oh, top.unsqueeze(1).broadcast_to(bt), rev8[:, :].unsqueeze(2).broadcast_to(bt), ALU.is_equal))
            dve.wait_ge(lexp, 1)
            link(dve.tensor_reduce(esum, ex, AXX, ALU.add))
            link(dve.reciprocal(prob, esum))
            link(dve.tensor_tensor(pe_key, oh, prob.unsqueeze(1).broadcast_to(bt), ALU.mult))
            dve.memset(one_b, 1.0)
            dve.memset(even_b, float(NC - NC // NB))
            link(dve.memset(thr[:, :], THR0))
            raised_f = raised.rearrange("p k e -> p (k e)")
            b3 = [P, NCAND, E0]
            thr_3 = thr[:, :].unsqueeze(1).broadcast_to(b3)
            link(dve.tensor_tensor(cand[:, :, :], units[:, 0, :].rearrange("p (k e) -> p k e", k=NCAND), thr_3, ALU.bitwise_or))
            base, per = steps[0], 3

            def search(late):
                keys, n = (pe_key[:, :, NB - 1:NC:NB], NC // NB) if late else (pe_key, NC)
                half = n // 2
                b5 = [P, half, NCAND, E0]
                larger = cmp_s[:, 0:NCAND * E0 * n].rearrange("p (c k e) -> p c k e", c=n, k=NCAND)

                def step(r):
                    at = [0]

                    def chain(ins):
                        at[0] += 1
                        ins.then_inc(dch, 1)
                        hold(dve, dch, base + per * r + at[0])

                    unit = units[:, bass.ds(r, 1), :].rearrange("p a e -> p (a e)")
                    unit_next = units[:, bass.ds(r + 1, 1), :].rearrange("p a (k e) -> p (a k) e", k=NCAND)
                    if late:
                        dve.tensor_tensor(part_0, pe_key[:, :, 0].unsqueeze(1).broadcast_to(b3), cand[:, :, :].bitcast(F32), ALU.is_ge)
                    for c in (0, half):
                        dve.tensor_tensor(larger[:, c:c + half], keys[:, :, c:c + half].rearrange("p e c -> p c e").unsqueeze(2).broadcast_to(b5),
                                          cand[:, :, :].bitcast(F32).unsqueeze(1).broadcast_to(b5), ALU.is_ge).then_inc(cpart, 1)
                    dve.tensor_tensor(ahead[:, :, :], unit_next, thr_3, ALU.bitwise_or)
                    hold(dve, csum, r + 1)
                    chain(dve.scalar_tensor_tensor(raised_f, bank[6][:, 0:NCAND * E0], float(CAPACITY), unit, ALU.is_ge, ALU.mult))
                    chain(dve.tensor_reduce(added[:, :], raised[:, :, :].rearrange("p k e -> p e k"), AXX, ALU.max))
                    dve.tensor_tensor(thr[:, :], thr[:, :], added[:, :], ALU.bitwise_or)
                    chain(dve.tensor_tensor(cand[:, :, :], ahead[:, :, :], added[:, :].unsqueeze(1).broadcast_to(b3), ALU.bitwise_or))
                    assert at[0] == per

                with dve.Fori(0, NSTEP // 3) as r:
                    for u in range(3):
                        step(3 * r + u)

            dve.wait_ge(slots, 4)
            with dve.If(general):
                search(False)
            with dve.Else():
                search(True)
            steps[0] = base + per * NSTEP
            thr_bc = thr[:, :].bitcast(F32).unsqueeze(2).broadcast_to(bt)
            link(dve.tensor_tensor(above, pe_key, thr_bc, ALU.is_gt))
            dve.tensor_tensor(tie, pe_key, thr_bc, ALU.is_equal).then_inc(tie_in, 1)
            dve.tensor_reduce(part, above, AXX, ALU.add).then_inc(cpart, 1)
            link(dve.memset(seg, 1.0))
            link(dve.memset(seg[:, :, 0:1], 0.0))

            def flat(ap):
                return ap.rearrange("p e c -> p (e c)")

            def ranks(n):
                dve.wait_ge(tie_ps, n)
                w = E0 * NC
                link(dve.tensor_tensor_scan(flat(run), flat(seg), bank[5][:, 0:w], 0.0, ALU.mult, ALU.add))
                link(dve.tensor_tensor(flat(rank), flat(run), bank[5][:, 0:w], ALU.subtract))
                link(dve.tensor_tensor(flat(rank), flat(rank), bank[4][:, 0:w], ALU.add))

            dve.wait_ge(csum, NSTEP + 1)
            link(dve.tensor_scalar(budget, bank[6][:, 0:E0], -1.0, float(CAPACITY), ALU.mult, ALU.add))
            ranks(1)
            link(dve.tensor_tensor(rank, rank, budget.unsqueeze(2).broadcast_to(bt), ALU.is_lt))
            link(dve.tensor_tensor(rank, rank, tie, ALU.mult))
            link(dve.tensor_tensor(fin, above, rank, ALU.add))
            link(dve.tensor_reduce(kept, fin[:, 1:E0, :].rearrange("p e c -> p c e"), AXX, ALU.add))
            link(dve.tensor_scalar(fin[:, 0, :], kept, -1.0, 1.0, ALU.mult, ALU.add))
            dve.wait_ge(slots, 4)
            link(dve.tensor_tensor(above, fin, slot[:, :].unsqueeze(1).broadcast_to(bt), ALU.mult))
            dve.sem_inc(tie_in, 1)
            link(dve.tensor_tensor(token_s[:, :], token_i[:, :], slot[:, :], ALU.mult))
            dve.tensor_scalar(tok_part[:, 0, :], token_s[:, :], 8, None, ALU.logical_shift_right)
            link(dve.tensor_scalar(tok_part[:, 1, :], token_s[:, :], 255, None, ALU.bitwise_and))
            link(dve.tensor_copy(tok_ab, tok_part[:, :, :]))
            ranks(2)
            link(dve.tensor_scalar(cnt_i[:, :], run[:, :, NC - 1], reserved[:, 0:1], float(P - 1), ALU.add, ALU.add))
            link(dve.tensor_scalar(cnt_i[:, :], cnt_i[:, :], 7, None, ALU.logical_shift_right))
            link(dve.tensor_copy(ntile, cnt_i[:, :]))
            link(dve.tensor_tensor_scan(tcum, ones[:, 0:E0], ntile, 0.0, ALU.mult, ALU.add))
            link(dve.tensor_tensor(tstart, tcum, ntile, ALU.subtract))
            link(dve.tensor_scalar(tcum, tstart, float(P), None, ALU.mult))
            link(dve.scalar_tensor_tensor(rank, rank, reserved[:, 0:1], slot[:, :].unsqueeze(1).broadcast_to(bt), ALU.add, ALU.mult))
            link(dve.tensor_tensor(rank, rank, tcum.unsqueeze(2).broadcast_to(bt), ALU.add))
            link(dve.tensor_tensor(rank, rank, fin, ALU.mult))
            link(dve.tensor_reduce(pos, rank.rearrange("p e c -> p c e"), AXX, ALU.add))
            link(dve.tensor_copy(pos_i[:, :], pos))
            link(dve.tensor_scalar(hi_i[:, :], pos_i[:, :], 7, None, ALU.logical_shift_right))
            link(dve.tensor_copy(hi, hi_i[:, :]))
            link(dve.scalar_tensor_tensor(lo, hi, -float(P), pos, ALU.mult, ALU.add))
            bx = [P, TILES, E0 - 1]
            link(dve.tensor_tensor(tcmp, iota_f[:, 0:TILES].unsqueeze(2).broadcast_to(bx),
                                   tstart[:, 1:E0].unsqueeze(1).broadcast_to(bx), ALU.is_ge))
            link(dve.tensor_reduce(tile_f, tcmp, AXX, ALU.add))
            link(dve.tensor_copy(tile_e[:, 0:TILES], tile_f))

            def fill_table(blocks):
                for m, cols in enumerate(blocks):
                    if m:
                        dve.wait_ge(tab_ps, m)
                    bl, bh = [P, NTC, P], [P, NTC, TILES]
                    dve.tensor_tensor(oh_lo, iota_f[:, :].unsqueeze(1).broadcast_to(bl), lo[:, cols].unsqueeze(2).broadcast_to(bl),
                                      ALU.is_equal)
                    dve.tensor_tensor(oh_eq, iota_f[:, 0:TILES].unsqueeze(1).broadcast_to(bh), hi[:, cols].unsqueeze(2).broadcast_to(bh),
                                      ALU.is_equal).then_inc(onehot, 1)
                    dve.wait_ge(onehot, 2 * m + 1)
                    for a in range(2):
                        o = dve.tensor_tensor(oh_hi[:, :, a, :], oh_eq, tok_ab[:, a, cols].unsqueeze(2).broadcast_to(bh), ALU.mult)
                    o.then_inc(onehot, 1)
                dve.wait_ge(tab_ps, len(blocks))

            early_blocks = [slice(n, n + NB * (NTC - 1) + 1, NB) for n in range(0, NC, NB * NTC)]
            late_blocks = [slice(n, n + NB * (NTC - 1) + 1, NB) for n in range(NB - 1, NC, NB * NTC)]
            with dve.If(general):
                fill_table(early_blocks + late_blocks)
            with dve.Else():
                fill_table(late_blocks)
            link(dve.tensor_copy(tab_b, bank[3][:, TILES:2 * TILES]))
            dve.scalar_tensor_tensor(row_tok[:, 0:TILES], bank[3][:, 0:TILES], 256.0, tab_b, ALU.mult, ALU.add).then_inc(table, 1)

            def scale_rows(i):
                dve.wait_ge(g_ps, i + 1 + 2)
                for k in range(KD):
                    m = dve.tensor_scalar(g_t[:, k, :], bank[0][:, k * P:(k + 1) * P], gout[:, k:k + 1], None, ALU.mult)
                m.then_inc(g_ev, 1)

            def relu_half(j):
                e = dve.value_load(tile_e[0:1, bass.ds(j, 1)], min_val=0, max_val=E0 - 1)
                dve.wait_ge(t_ps, j + 1)
                for f in range(NF // 2, NF):
                    m = dve.tensor_scalar(act_t[:, f, :], bank[4][:, (f - 4) * P:(f - 3) * P], b1_s[:, bass.ds(e * NF + f, 1)], 0.0,
                                          ALU.add, ALU.max)
                m.then_inc(t_evd, 1)
                return e

            def add_bias(i, u, e, turn_no):
                dve.wait_ge(dn_ps, i + 1)
                dve.wait_ge(y_st[u], 16 * turn_no + 16)
                dve.tensor_tensor(y_s[u], bank[5 + u][:, 0:D], b2_s[:, bass.ds(e, 1), :].rearrange("p a d -> p (a d)"),
                                  ALU.add).then_inc(dn_ev, 1)

            def experts(tiles):
                scale_rows(0)
                dve.wait_ge(ld_b, 32)
                with dve.Fori(0, (tiles - 1) // 2) as r:
                    for v in range(2):
                        i = 1 + 2 * r + v
                        scale_rows(i)
                        add_bias(i - 1, v, relu_half(i - 1), r)
                if tiles % 2 == 0:
                    scale_rows(tiles - 1)
                    add_bias(tiles - 2, 0, relu_half(tiles - 2), tiles // 2 - 1)
                add_bias(tiles - 1, (tiles - 1) % 2, relu_half(tiles - 1), (tiles - 1) // 2)
                dve.wait_ge(y_st[0], 16 * ((tiles + 1) // 2) + 16)

            with dve.If(general):
                experts(TILES)
            with dve.Else():
                experts(TILES_L)

            dve.wait_ge(ld_v, 16 * NLD2)
            bo = [64, B, E1]
            dve.tensor_tensor(cgo[0:64], cond_s.unsqueeze(2).broadcast_to(bo), wg_s.unsqueeze(1).broadcast_to(bo), ALU.mult).then_inc(cgc, 1)
            dve.wait_ge(cg_ps, 1)
            dve.tensor_copy(cg.rearrange("p b e -> p (b e)"), bank[6][:, 0:B * E1]).then_inc(cgc, 1)

            def add_x(b, u, q, turn_no, first):
                row = x2[:, bass.ds(b * NB, NB), :]
                hold(dve, ld_x2[q], 16 * turn_no + 32)
                if not first:
                    hold(dve, a_t, b - 1)
                    hold(dve, a_st[u], (b // 2) * 16 if isinstance(b, int) else 32 * turn_no + 16 * (q // 2))
                hold(dve, a_got[q], 32 * turn_no + 32)
                dve.tensor_tensor(x1_s[u], row, yg[q], ALU.add).then_inc(a_add, 1)
                hold(dve, a_add, b + 1)
                dve.tensor_copy(row, x1_s[u]).then_inc(a_x1, 1)

            for b in range(4):
                add_x(b, b % 2, b, 0, b < 2)
            with dve.Fori(1, B // 4 - 1) as r:
                for u in range(4):
                    add_x(4 * r + u, u % 2, u, r, False)
            shared_products(dve, 0, 0)
            for u in range(4):
                add_x(B - 4 + u, u % 2, u, B // 4 - 1, False)
            shared_products(dve, 1, 1)

            dve.wait_ge(a_lg, B)
            dve.wait_ge(cgc, 2)
            b4 = [P, B, NB, E1]
            link(dve.tensor_tensor(glog.rearrange("p (b n) e -> p b n e", b=B),
                                   bank[7][:, 0:NC * E1].rearrange("p (b n e) -> p b n e", b=B, n=NB),
                                   cg.unsqueeze(2).broadcast_to(b4), ALU.add))
            link(dve.tensor_reduce(gnm, glog, AXX, ALU.max))
            dve.tensor_tensor(gex, glog, gnm.unsqueeze(2).broadcast_to(bc), ALU.subtract).then_inc(rl_sub, 1)
            dve.tensor_scalar(tok_part2[:, 0, :], token2_i[:, :], 8, None, ALU.logical_shift_right)
            dve.tensor_scalar(tok_part2[:, 1, :], token2_i[:, :], 255, None, ALU.bitwise_and)
            dve.memset(seg2, 1.0)
            dve.wait_ge(rl_exp, 1)
            link(dve.tensor_reduce(gsum, gex, AXX, ALU.add))
            link(dve.memset(seg2[:, :, 0:1], 0.0))
            link(dve.tensor_copy(tok_ab2, tok_part2[:, :, :]))
            link(dve.reciprocal(gsum, gsum))
            link(dve.tensor_tensor(glog, gex, gsum.unsqueeze(2).broadcast_to(bc), ALU.mult))
            rev_c = rev8[:, :].unsqueeze(1).broadcast_to(bc)
            rev_e = rev8[:, :].unsqueeze(2).broadcast_to(bt)
            for m, oh_k in ((m1, oh1), (m2, oh2)):
                link(dve.tensor_reduce(m, glog, AXX, ALU.max))
                link(dve.tensor_tensor(ghit, glog, m.unsqueeze(2).broadcast_to(bc), ALU.is_equal))
                link(dve.tensor_tensor(ghit, ghit, rev_c, ALU.mult))
                link(dve.tensor_reduce(gtop, ghit, AXX, ALU.max))
                link(dve.tensor_tensor(oh_k, gtop.unsqueeze(1).broadcast_to(bt), rev_e, ALU.is_equal))
                if m is m1:
                    link(dve.scalar_tensor_tensor(glog, oh1.rearrange("p e c -> p c e"), -4.0, glog, ALU.mult, ALU.add))
            link(dve.tensor_tensor(both, oh1, oh2, ALU.add))
            dve.sem_inc(tie_in, 1)
            link(dve.scalar_tensor_tensor(gsum, m1, 1e-20, m2, ALU.add, ALU.add))
            link(dve.reciprocal(gsum, gsum))
            for k, m in enumerate((m1, m2)):
                link(dve.tensor_tensor(w_k[:, k, :], m, gsum, ALU.mult))
            dve.wait_ge(tie_ps, 3)
            w = E1 * NC
            link(dve.tensor_tensor_scan(flat(run2), flat(seg2), bank[5][:, 0:w], 0.0, ALU.mult, ALU.add))
            link(dve.tensor_tensor(flat(rank2), flat(run2), bank[5][:, 0:w], ALU.subtract))
            link(dve.tensor_tensor(flat(rank2), flat(rank2), bank[4][:, 0:w], ALU.add))
            link(dve.tensor_scalar(cnt_i[:, :], run2[:, :, NC - 1], float(P - 1), None, ALU.add))
            link(dve.tensor_scalar(cnt_i[:, :], cnt_i[:, :], 7, None, ALU.logical_shift_right))
            link(dve.tensor_copy(ntile2, cnt_i[:, :]))
            link(dve.tensor_tensor_scan(tcum2, ones[:, 0:E1], ntile2, 0.0, ALU.mult, ALU.add))
            link(dve.tensor_tensor(tstart2, tcum2, ntile2, ALU.subtract))
            link(dve.scalar_tensor_tensor(rank2, tstart2.unsqueeze(2).broadcast_to(bt), float(P), rank2, ALU.mult, ALU.add))
            for k, oh_k in enumerate((oh1, oh2)):
                link(dve.tensor_tensor(prod2, rank2, oh_k, ALU.mult))
                link(dve.tensor_reduce(pos_k[:, :, k], prod2.rearrange("p e c -> p c e"), AXX, ALU.add))
            link(dve.tensor_copy(pos_k_i[:, :, :], pos_k))
            link(dve.tensor_scalar(hi_k_i[:, :, :], pos_k_i[:, :, :], 7, None, ALU.logical_shift_right))
            link(dve.tensor_copy(hi_k, hi_k_i[:, :, :]))
            link(dve.scalar_tensor_tensor(lo_k, hi_k, -float(P), pos_k, ALU.mult, ALU.add))
            bx = [P, TILES2, E1 - 1]
            link(dve.tensor_tensor(tcmp2, iota_f[:, 0:TILES2].unsqueeze(2).broadcast_to(bx),
                                   tstart2[:, 1:E1].unsqueeze(1).broadcast_to(bx), ALU.is_ge))
            link(dve.tensor_reduce(tile_f2, tcmp2, AXX, ALU.add))
            link(dve.tensor_copy(tile_e2[:, :], tile_f2))
            NT2 = 2 * NC // NTC
            for m in range(NT2):
                if m >= 2:
                    dve.wait_ge(tab_ps2, m - 1)
                k, c0, lo2, hi2 = m % 2, (m // 2) * NTC, oh_lo2[m % 2], oh_hi2[m % 2]
                cs = slice(c0, c0 + NTC)
                bl, bh = [P, NTC, P], [P, NTC, TILES2]
                dve.tensor_tensor(lo2, iota_f[:, :].unsqueeze(1).broadcast_to(bl), lo_k[:, cs, k].unsqueeze(2).broadcast_to(bl), ALU.is_equal)
                if m:
                    dve.wait_ge(onehot2, m)
                link(dve.tensor_tensor(oh_eq2, iota_f[:, 0:TILES2].unsqueeze(1).broadcast_to(bh), hi_k[:, cs, k].unsqueeze(2).broadcast_to(bh),
                                       ALU.is_equal))
                for a in range(2):
                    o = dve.tensor_tensor(hi2[:, :, a, :], oh_eq2, tok_ab2[:, a, cs].unsqueeze(2).broadcast_to(bh), ALU.mult)
                o.then_inc(onehot2, 1)
            dve.wait_ge(tab_ps2, NT2)
            link(dve.tensor_copy(tab_b2, bank[3][:, TILES2:2 * TILES2]))
            dve.scalar_tensor_tensor(row_tok2[:, :], bank[3][:, 0:TILES2], 256.0, tab_b2, ALU.mult, ALU.add).then_inc(table, 1)

            def choice_step(i, u):
                static = isinstance(i, int)
                if not static or 3 <= i < TILES2 + 3:
                    dve.wait_ge(c_mt, i - 2)
                    dve.tensor_copy(c_midt[u], bank[1][:, 0:M1]).then_inc(c_mtc, 1)
                if not static or 1 <= i < TILES2 + 1:
                    v = (u - 1) % RT
                    hold(dve, c_lk, i)
                    dve.scalar_tensor_tensor(c_mid[v], c_leak[v], 0.01, c_leak[v], ALU.mult, ALU.max).then_inc(c_lkd, 1)
                    hold(dve, c_lkd, i)
                    dve.tensor_tensor(c_mid[v], c_mid[v], bank[2 + v][:, M1:2 * M1], ALU.mult).then_inc(c_md, 1)

            for i in range(2 * RT):
                choice_step(i, i % RT)
            with dve.Fori(2, TILES2 // RT) as r:
                for u in range(RT):
                    choice_step(RT * r + u, u)
            for i in range(TILES2, TILES2 + 3):
                choice_step(i, i % RT)

            def sum_choices(b, u, turn_no):
                if not isinstance(b, int) or b >= RT:
                    hold(dve, d_zt, b - RT + 1)
                hold(dve, d_got[u], 64 * turn_no + 64)
                hold(dve, a_dc, b + 1)
                for k in range(2):
                    if k:
                        hold(dve, d_z1, b + 1)
                    for n in range(NB):
                        base = z_s[u][:, n, :] if k else p_s[:, bass.ds(b * NB + n, 1), :].rearrange("p a d -> p (a d)")
                        m = dve.scalar_tensor_tensor(z_s[u][:, n, :], yk[u][:, 2 * n + k, :], w_k[:, k, bass.ds(b * NB + n, 1)], base,
                                                     ALU.mult, ALU.add)
                        if n == NB - 1:
                            m.then_inc(d_z if k else d_z1, 1)
                        yield

            def gates(b, u):
                at = [0]

                def glink(ins):
                    at[0] += 1
                    ins.then_inc(d_ch, 1)

                def gwait():
                    hold(dve, d_ch, 1 + NCH * b + at[0])

                hold(dve, d_lg, b + 1)
                glink(dve.scalar_tensor_tensor(flog, bank[1][:, 0:E2], 1.0 / S, gb_bc, ALU.mult, ALU.add))
                yield
                gwait()
                glink(dve.max(ftop, flog))
                yield
                gwait()
                dve.tensor_scalar(fnm, ftop[:, 0:1], -1.0, None, ALU.mult).then_inc(d_sub, 1)
                dve.tensor_scalar(fkeep, flog, ftop[:, 1:2], None, ALU.is_ge)
                dve.tensor_tensor(feq, ftop[:, 0:1], ftop[:, 1:2], ALU.is_equal)
                glink(dve.max_index(d_top[:, :], ftop, flog))
                yield
                gwait()
                dve.tensor_copy(d_ids[u][:, :], d_top[:, :])
                glink(dve.tensor_reduce(fcnt, fkeep, AXX, ALU.add))
                yield
                gwait()
                glink(dve.tensor_tensor(fcnt, fcnt, feq, ALU.add))
                hold(dve, d_exp, b + 1)
                glink(dve.tensor_tensor(fex, fex, fkeep, ALU.mult))
                yield
                gwait()
                glink(dve.tensor_tensor(fmany, fmany, fcnt, ALU.max))
                glink(dve.tensor_reduce(fsum, fex, AXX, ALU.add))
                yield
                gwait()
                glink(dve.reciprocal(fsum, fsum))
                yield
                gwait()
                glink(dve.tensor_scalar(fgate, fex, fsum[:, 0:1], None, ALU.mult))
                yield
                gwait()
                dve.tensor_copy(gate[:, bass.ds(b, 1), :].rearrange("p a e -> p (a e)"), fgate)
                dve.max(gsort[u], fgate).then_inc(d_ok, 1)
                assert at[0] == NCH, at[0]

            def weigh(b, u, turn_no):
                row = x2[:, bass.ds(b * NB, NB), :]
                for c in range(2):
                    hold(dve, d_ge, 2 * b + c + 1)
                    if c == 0 and (not isinstance(b, int) or b >= RT):
                        hold(dve, d_st[u], 16 * turn_no)
                    if c:
                        hold(dve, d_r1, b + 1)
                    dve.scalar_tensor_tensor(res[u], ge[c], gsort[u][:, c:c + 1], res[u] if c else row, ALU.mult, ALU.add
                                             ).then_inc(d_res if c else d_r1, 1)
                    yield

            def gated_step(b, u, turn_no):
                static, v = isinstance(b, int), (u - 2) % RT
                sums = sum_choices(b + 1, (u + 1) % RT, turn_no + (u + 1) // RT) if not static or b + 1 < B else iter(())
                chain = gates(b, u) if not static or b < B else iter(())
                outs = weigh(b - 2, v, turn_no - (u < 2)) if not static or b >= 2 else iter(())
                for first, then, times in ((chain, sums, 4), (chain, outs, 1), (chain, chain, 9), (outs, outs, 2), (sums, sums, 4)):
                    for _ in range(times):
                        next(first, None)
                        next(then, None)

            dve.wait_ge(a_md, NSH * SH_G)
            dve.memset(fmany, 0.0).then_inc(d_ch, 1)
            dve.wait_ge(d_ch, 1)
            dve.wait_ge(ld_v, 16 * (NLD2 + NLD3))
            for b in range(RT):
                for s in late_shared(b):
                    shared_products(dve, s, s % 2)
                if b == 0:
                    for _ in sum_choices(0, 0, 0):
                        pass
                gated_step(b, b, 0)
            with dve.Fori(1, B // RT) as r:
                for u in range(RT):
                    gated_step(RT * r + u, u, r)
            for b in range(B - B % RT, B + 2):
                gated_step(b, b % RT, b // RT)
            dve.wait_ge(d_ch, 1 + NCH * B)
            dve.tensor_scalar(many_i[:, :], fmany, 2.0, None, ALU.is_gt).then_inc(d_all, 1)

            def every_expert(b, first):
                for e in range(E2):
                    hold(dve, d_ge, 2 * B + E2 * b + e + 1)
                    if e == 0 and not first:
                        hold(dve, d_st[0], 16 * b + 16 * len(range(0, B, RT)))
                    if e:
                        hold(dve, f_r, E2 * b + e)
                    for n in range(NB):
                        base = res[0][:, n, :] if e else x2[:, bass.ds(b * NB + n, 1), :].rearrange("p a d -> p (a d)")
                        m = dve.scalar_tensor_tensor(res[0][:, n, :], ge[e % 2][:, n, :], gate[:, bass.ds(b, 1), e], base, ALU.mult, ALU.add)
                    m.then_inc(f_r, 1)
                hold(dve, f_r, E2 * b + E2)
                dve.sem_inc(d_res, 1)

            with dve.If(more_gates(dve)):
                for u in range(RT):
                    dve.wait_ge(d_st[u], 16 * len(range(u, B, RT)))
                every_expert(0, True)
                with dve.Fori(1, B) as b:
                    every_expert(b, False)


def kernel(**inputs):
    import concourse.bacc as bacc
    from concourse import mybir
    from concourse.bass_utils import run_bass_kernel_spmd

    def chunks(a, p=128):
        return a.reshape(a.shape[0] // p, p, -1).transpose(1, 0, 2)

    i = {k: np.asarray(v) for k, v in inputs.items()}
    laid = {
        "x": i["x"].reshape(4096, 256),
        "side": i["fside_16xSxS_0"],
        "cond_t": i["cond_64"].T,
        "null_kv": i["cond_64"][0:2],
        "mask": i["mask_BxS_bk0"].reshape(1, 4096),
        "g_in": i["L0_cond_g_in"].reshape(2, 128).T,
        "null_bias": i["L0_cond_null_attn_bias"],
        "wq": i["L0_cond_Wq"], "wkv": i["L0_cond_Wkv"], "wo": i["L0_cond_Wo"],
        "router_t": i["L0_ffn_router_w"].T,
        "w1": i["L0_ffn_W1"].reshape(8, 2, 128, 1024).transpose(2, 0, 1, 3).reshape(128, -1),
        "b1": i["L0_ffn_b1"].reshape(64, 128).T,
        "w2": i["L0_ffn_W2"].reshape(8, 8, 128, 256).transpose(2, 0, 1, 3).reshape(128, -1),
        "b2": i["L0_ffn_b2"],
        "wt_t": i["L1_cond_wt"].T, "wg_t": i["L1_cond_wg"].T,
        "moe_gate": chunks(i["L1_cond_w_gate"].transpose(1, 0, 2).reshape(256, 1024)),
        "moe_up": chunks(i["L1_cond_w_up"].transpose(1, 0, 2).reshape(256, 1024)),
        "moe_down": i["L1_cond_w_down"],
        "sw_gate": i["L1_cond_sw_gate"], "sw_up": i["L1_cond_sw_up"], "sw_down": i["L1_cond_sw_down"],
        "gate_w_t": i["L1_ffn_gate_w"].T, "gate_b": i["L1_ffn_gate_b"],
        "expert_w_t": i["L1_ffn_expert_w"].transpose(2, 0, 1).reshape(2, 128, 8, 256).transpose(1, 0, 2, 3),
        "expert_b": i["L1_ffn_expert_b"].reshape(1, 2048),
        "g_out": i["L0_cond_g_out"].reshape(2, 128).T,
    }
    nc = bacc.Bacc("TRN2", target_bir_lowering=False, num_devices=1)
    arrays, aps = {}, {}
    for name, a in laid.items():
        arrays[name] = np.ascontiguousarray(a)
        aps[name] = nc.dram_tensor(name, arrays[name].shape, mybir.dt.from_np(arrays[name].dtype), kind="ExternalInput").ap()
    aps["out"] = nc.dram_tensor("out", (4096, 256), mybir.dt.float32, kind="ExternalOutput").ap()
    bass_adaln_ffn_kernel(nc, **aps)
    r = run_bass_kernel_spmd(nc, [arrays], core_ids=[0])
    return r.results[0]["out"].reshape(16, 256, 256)
```
